# Optimizing a Trainium2 kernel written in Bass

```python
import numpy as np
import jax
import jax.numpy as jnp

def _softmax(x, axis=-1):
    return jax.nn.softmax(x, axis=axis)

def _gelu(x):
    return jax.nn.gelu(x, approximate=True)

def _silu(x):
    return jax.nn.silu(x)

def _sigmoid(x):
    return jax.nn.sigmoid(x)

def _layernorm(x, axis=-1, eps=1e-05):
    m = jnp.mean(x, axis=axis, keepdims=True)
    v = jnp.var(x, axis=axis, keepdims=True)
    return (x - m) / jnp.sqrt(v + eps)

def _scatter_add(tgt, idx, src, axis=0):
    return tgt.at[idx].add(src)

def _segment_sum(src, seg, n):
    return jax.ops.segment_sum(src, seg, n)
kernel_name = 'mk_hybrid_d1_jaxref_r4_e9aa7d'

def setup_inputs(seed: int=0):
    np.random.seed(seed)
    _w = jnp.asarray

    def _L0_attn_a_setup():
        import jax, jax.numpy as jnp
        import numpy as np
        H = 16
        DH = 64
        M = 64
        ITERS = 6
        K = 13

        def moore_penrose_inverse(a, iters=ITERS):
            a_abs = jnp.abs(a)
            col = a_abs.sum(axis=-1)
            row = a_abs.sum(axis=-2)
            z = jnp.swapaxes(a, -1, -2) / (jnp.max(col) * jnp.max(row))
            I = jnp.eye(a.shape[-1], dtype=a.dtype)
            for _ in range(iters):
                az = a @ z
                z = 0.25 * z @ (13 * I - az @ (15 * I - az @ (7 * I - az)))
            return z
        key = jax.random.key(seed)
        k1, k2, k3, k4 = jax.random.split(key, 4)
        b, n, dim = (4, 1024, 256)
        inner = H * DH
        x = jax.random.normal(k1, (b, n, dim), dtype=jnp.float32)
        w_qkv = jax.random.normal(k2, (dim, 3 * inner), dtype=jnp.float32) * 0.02
        w_conv = jax.random.normal(k3, (H, 1, K, 1), dtype=jnp.float32) * 0.1
        w_fc = jax.random.normal(k4, (inner, dim), dtype=jnp.float32) * 0.02
        b_fc = jnp.zeros((dim,), dtype=jnp.float32)
        return {'x': x, 'w_qkv': w_qkv, 'w_conv': w_conv, 'w_fc': w_fc, 'b_fc': b_fc}
    _L0_attn_a_in = _L0_attn_a_setup()

    def _L0_attn_b_setup():
        import jax, jax.numpy as jnp
        import numpy as np
        D_MODEL = 256
        N_HEADS = 16
        HEAD_DIM = D_MODEL // N_HEADS
        ROPE_BASE = 10000.0

        def _rope_tables(T, dtype=jnp.float32):
            half = HEAD_DIM // 2
            inv_freq = 1.0 / ROPE_BASE ** (jnp.arange(0, HEAD_DIM, 2, dtype=jnp.float32) / HEAD_DIM)
            t = jnp.arange(T, dtype=jnp.float32)
            freqs = jnp.einsum('i,j->ij', t, inv_freq)
            return (jnp.cos(freqs).astype(dtype), jnp.sin(freqs).astype(dtype))

        def _apply_rotary(x, cos, sin):
            B, T, H, D = x.shape
            xr = x.reshape(B, T, H, D // 2, 2)
            x0, x1 = (xr[..., 0], xr[..., 1])
            c = cos[None, :, None, :]
            s = sin[None, :, None, :]
            out = jnp.stack([x0 * c - x1 * s, x0 * s + x1 * c], axis=-1)
            return out.reshape(B, T, H, D)
        key = jax.random.key(seed)
        ks = jax.random.split(key, 5)
        x = jax.random.normal(ks[0], (4, 256, D_MODEL), dtype=jnp.float32)
        init = 1.0 / np.sqrt(D_MODEL)
        Wq = jax.random.uniform(ks[1], (D_MODEL, D_MODEL), jnp.float32, -init, init)
        Wk = jax.random.uniform(ks[2], (D_MODEL, D_MODEL), jnp.float32, -init, init)
        Wv = jax.random.uniform(ks[3], (D_MODEL, D_MODEL), jnp.float32, -init, init)
        Wo = jax.random.uniform(ks[4], (D_MODEL, D_MODEL), jnp.float32, -init, init)
        return {'x': x, 'Wq': Wq, 'Wk': Wk, 'Wv': Wv, 'Wo': Wo}
    _L0_attn_b_in = _L0_attn_b_setup()

    def _L0_ffn_setup():
        import jax, jax.numpy as jnp
        import numpy as np

        def _ln(x, w, b):
            m = jnp.mean(x, axis=-1, keepdims=True)
            v = jnp.var(x, axis=-1, keepdims=True)
            return (x - m) / jnp.sqrt(v + 1e-05) * w + b
        B, T, C = (4, 512, 256)
        E_RWKV, E = (2, 3)
        H = 4 * C
        S = 0.02
        key = jax.random.key(seed)
        ks = jax.random.split(key, 20)
        d = {}
        d['x'] = jax.random.normal(ks[0], (B, T, C), jnp.float32)
        d['v_first'] = jax.random.normal(ks[1], (B, T, C), jnp.float32)
        d['capital_shares'] = jax.random.uniform(ks[2], (E,), jnp.float32)
        d['ln1_w'] = jnp.ones((C,), jnp.float32)
        d['ln1_b'] = jnp.zeros((C,), jnp.float32)
        d['ln2_w'] = jnp.ones((C,), jnp.float32)
        d['ln2_b'] = jnp.zeros((C,), jnp.float32)
        d['Wr'] = S * jax.random.normal(ks[3], (C, C), jnp.float32)
        d['Wv'] = S * jax.random.normal(ks[4], (C, C), jnp.float32)
        d['Wo'] = S * jax.random.normal(ks[5], (C, C), jnp.float32)
        d['Ws'] = S * jax.random.normal(ks[6], (C, C), jnp.float32)
        d['K_rwkv'] = S * jax.random.normal(ks[7], (E_RWKV, C, H), jnp.float32)
        d['V_rwkv'] = S * jax.random.normal(ks[8], (E_RWKV, H, C), jnp.float32)
        d['conf_rwkv'] = S * jax.random.normal(ks[9], (E_RWKV, C), jnp.float32)
        d['W1'] = S * jax.random.normal(ks[10], (C, C), jnp.float32)
        d['W2'] = S * jax.random.normal(ks[11], (C, C), jnp.float32)
        d['W3'] = S * jax.random.normal(ks[12], (C, C), jnp.float32)
        d['conf_trans'] = S * jax.random.normal(ks[13], (C,), jnp.float32)
        d['w_diff'] = S * jax.random.normal(ks[14], (C,), jnp.float32)
        d['W_aff'] = S * jax.random.normal(ks[15], (C, E), jnp.float32)
        d['W_bridge'] = S * jax.random.normal(ks[16], (C, C), jnp.float32)
        return d
    _L0_ffn_in = _L0_ffn_setup()
    _d = {'L0_attn_a_x': _L0_attn_a_in['x'], 'L0_attn_a_w_qkv': _L0_attn_a_in['w_qkv'], 'L0_attn_a_w_conv': _L0_attn_a_in['w_conv'], 'L0_attn_a_w_fc': _L0_attn_a_in['w_fc'], 'L0_attn_a_b_fc': _L0_attn_a_in['b_fc'], 'L0_attn_b_Wq': _L0_attn_b_in['Wq'], 'L0_attn_b_Wk': _L0_attn_b_in['Wk'], 'L0_attn_b_Wv': _L0_attn_b_in['Wv'], 'L0_attn_b_Wo': _L0_attn_b_in['Wo'], 'L0_ffn_v_first': _L0_ffn_in['v_first'], 'L0_ffn_capital_shares': _L0_ffn_in['capital_shares'], 'L0_ffn_ln1_w': _L0_ffn_in['ln1_w'], 'L0_ffn_ln1_b': _L0_ffn_in['ln1_b'], 'L0_ffn_ln2_w': _L0_ffn_in['ln2_w'], 'L0_ffn_ln2_b': _L0_ffn_in['ln2_b'], 'L0_ffn_Wr': _L0_ffn_in['Wr'], 'L0_ffn_Wv': _L0_ffn_in['Wv'], 'L0_ffn_Wo': _L0_ffn_in['Wo'], 'L0_ffn_Ws': _L0_ffn_in['Ws'], 'L0_ffn_K_rwkv': _L0_ffn_in['K_rwkv'], 'L0_ffn_V_rwkv': _L0_ffn_in['V_rwkv'], 'L0_ffn_conf_rwkv': _L0_ffn_in['conf_rwkv'], 'L0_ffn_W1': _L0_ffn_in['W1'], 'L0_ffn_W2': _L0_ffn_in['W2'], 'L0_ffn_W3': _L0_ffn_in['W3'], 'L0_ffn_conf_trans': _L0_ffn_in['conf_trans'], 'L0_ffn_w_diff': _L0_ffn_in['w_diff'], 'L0_ffn_W_aff': _L0_ffn_in['W_aff'], 'L0_ffn_W_bridge': _L0_ffn_in['W_bridge']}
    _x0 = _d['L0_attn_a_x']
    _d['L0_attn_a_x'] = jax.random.normal(jax.random.fold_in(jax.random.key(seed), 1), (8, 512, 256), dtype=_x0.dtype)
    del _x0
    return _d

def reference(L0_attn_a_x, L0_attn_a_w_qkv, L0_attn_a_w_conv, L0_attn_a_w_fc, L0_attn_a_b_fc, L0_attn_b_Wq, L0_attn_b_Wk, L0_attn_b_Wv, L0_attn_b_Wo, L0_ffn_v_first, L0_ffn_capital_shares, L0_ffn_ln1_w, L0_ffn_ln1_b, L0_ffn_ln2_w, L0_ffn_ln2_b, L0_ffn_Wr, L0_ffn_Wv, L0_ffn_Wo, L0_ffn_Ws, L0_ffn_K_rwkv, L0_ffn_V_rwkv, L0_ffn_conf_rwkv, L0_ffn_W1, L0_ffn_W2, L0_ffn_W3, L0_ffn_conf_trans, L0_ffn_w_diff, L0_ffn_W_aff, L0_ffn_W_bridge):

    def _L0_attn_a_ref(x, w_qkv, w_conv, w_fc, b_fc):
        import jax, jax.numpy as jnp
        import numpy as np
        H = 16
        DH = 64
        M = 64
        ITERS = 6
        K = 13

        def moore_penrose_inverse(a, iters=ITERS):
            a_abs = jnp.abs(a)
            col = a_abs.sum(axis=-1)
            row = a_abs.sum(axis=-2)
            z = jnp.swapaxes(a, -1, -2) / (jnp.max(col) * jnp.max(row))
            I = jnp.eye(a.shape[-1], dtype=a.dtype)
            for _ in range(iters):
                az = a @ z
                z = 0.25 * z @ (13 * I - az @ (15 * I - az @ (7 * I - az)))
            return z
        b, n, dim = x.shape
        scale = DH ** (-0.5)
        qkv = x @ w_qkv
        q, k, v = jnp.split(qkv, 3, axis=-1)
        split_heads = lambda t: t.reshape(b, n, H, DH).transpose(0, 2, 1, 3)
        q, k, v = (split_heads(q) * scale, split_heads(k), split_heads(v))
        l = n // M
        q_l = q.reshape(b, H, M, l, DH).sum(axis=3) / l
        k_l = k.reshape(b, H, M, l, DH).sum(axis=3) / l
        sim1 = jnp.einsum('bhid,bhjd->bhij', q, k_l)
        sim2 = jnp.einsum('bhid,bhjd->bhij', q_l, k_l)
        sim3 = jnp.einsum('bhid,bhjd->bhij', q_l, k)
        attn1 = jax.nn.softmax(sim1, axis=-1)
        attn2 = jax.nn.softmax(sim2, axis=-1)
        attn3 = jax.nn.softmax(sim3, axis=-1)
        attn2_inv = moore_penrose_inverse(attn2)
        out = attn1 @ attn2_inv @ (attn3 @ v)
        res = jax.lax.conv_general_dilated(out, w_conv, window_strides=(1, 1), padding=((K // 2, K // 2), (0, 0)), feature_group_count=H, dimension_numbers=('NCHW', 'OIHW', 'NCHW'))
        out = out + res
        out = out.transpose(0, 2, 1, 3).reshape(b, n, H * DH)
        out = out @ w_fc + b_fc
        return out

    def _L0_attn_b_ref(x, Wq, Wk, Wv, Wo):
        import jax, jax.numpy as jnp
        import numpy as np
        D_MODEL = 256
        N_HEADS = 16
        HEAD_DIM = D_MODEL // N_HEADS
        ROPE_BASE = 10000.0

        def _rope_tables(T, dtype=jnp.float32):
            half = HEAD_DIM // 2
            inv_freq = 1.0 / ROPE_BASE ** (jnp.arange(0, HEAD_DIM, 2, dtype=jnp.float32) / HEAD_DIM)
            t = jnp.arange(T, dtype=jnp.float32)
            freqs = jnp.einsum('i,j->ij', t, inv_freq)
            return (jnp.cos(freqs).astype(dtype), jnp.sin(freqs).astype(dtype))

        def _apply_rotary(x, cos, sin):
            B, T, H, D = x.shape
            xr = x.reshape(B, T, H, D // 2, 2)
            x0, x1 = (xr[..., 0], xr[..., 1])
            c = cos[None, :, None, :]
            s = sin[None, :, None, :]
            out = jnp.stack([x0 * c - x1 * s, x0 * s + x1 * c], axis=-1)
            return out.reshape(B, T, H, D)
        B, T, C = x.shape
        H, Dh = (N_HEADS, HEAD_DIM)
        scale = Dh ** (-0.5)
        q = (x @ Wq.T).reshape(B, T, H, Dh)
        k = (x @ Wk.T).reshape(B, T, H, Dh)
        v = (x @ Wv.T).reshape(B, T, H, Dh)
        cos, sin = _rope_tables(T, x.dtype)
        q = _apply_rotary(q, cos, sin)
        k = _apply_rotary(k, cos, sin)
        q = q.transpose(0, 2, 1, 3).astype(jnp.float32)
        k = k.transpose(0, 2, 1, 3).astype(jnp.float32)
        v = v.transpose(0, 2, 1, 3)
        scores = jnp.einsum('bhqd,bhkd->bhqk', q, k) * scale
        causal = jnp.triu(jnp.ones((T, T), dtype=bool), k=1)
        scores = jnp.where(causal[None, None], -jnp.inf, scores)
        attn = jax.nn.softmax(scores, axis=-1).astype(v.dtype)
        out = jnp.einsum('bhqk,bhkd->bhqd', attn, v)
        out = out.transpose(0, 2, 1, 3).reshape(B, T, C)
        return out @ Wo.T

    def _L0_ffn_ref(x, v_first, capital_shares, ln1_w, ln1_b, ln2_w, ln2_b, Wr, Wv, Wo, Ws, K_rwkv, V_rwkv, conf_rwkv, W1, W2, W3, conf_trans, w_diff, W_aff, W_bridge):
        import jax, jax.numpy as jnp
        import numpy as np

        def _ln(x, w, b):
            m = jnp.mean(x, axis=-1, keepdims=True)
            v = jnp.var(x, axis=-1, keepdims=True)
            return (x - m) / jnp.sqrt(v + 1e-05) * w + b
        B, T, C = x.shape
        xln = _ln(x, ln1_w, ln1_b)
        att_out = jax.nn.sigmoid(xln @ Wr) * (xln @ Wv) @ Wo
        rwkv_state = xln @ Ws
        x = x + att_out
        h = _ln(x, ln2_w, ln2_b)
        conf_r = jax.nn.sigmoid(jnp.einsum('btc,ec->bte', h, conf_rwkv))
        conf_t = jax.nn.sigmoid(h @ conf_trans)[..., None]
        confidences = jnp.concatenate([conf_r, conf_t], axis=-1)
        E = confidences.shape[-1]
        difficulty = jax.nn.sigmoid(h @ w_diff)[..., None]
        affinity = h @ W_aff
        bids = confidences * capital_shares * difficulty + affinity
        winners = jnp.argmax(bids, axis=-1)
        flat_h = h.reshape(-1, C)
        flat_state = rwkv_state.reshape(-1, C)
        flat_w = winners.reshape(-1)
        flat_conf = confidences.reshape(-1, E)
        win_conf = jnp.take_along_axis(flat_conf, flat_w[:, None], axis=1)
        scale = win_conf / (jax.lax.stop_gradient(win_conf) + 1e-06)
        hr = jnp.square(jax.nn.relu(jnp.einsum('nc,ech->enh', flat_h, K_rwkv)))
        out_rwkv = jnp.einsum('enh,ehc->enc', hr, V_rwkv)
        out_trans = flat_h @ W1 * jax.nn.sigmoid(flat_state @ W2) @ W3
        all_out = jnp.concatenate([out_rwkv, out_trans[None]], axis=0)
        onehot = jax.nn.one_hot(flat_w, E, dtype=flat_h.dtype)
        final = jnp.einsum('ne,enc->nc', onehot, all_out) * scale
        return x + final.reshape(B, T, C)
    x = L0_attn_a_x
    x = x + _L0_attn_a_ref(_layernorm(x, axis=-1), L0_attn_a_w_qkv, L0_attn_a_w_conv, L0_attn_a_w_fc, L0_attn_a_b_fc)
    x = x + _L0_ffn_ref(_layernorm(x, axis=-1), L0_ffn_v_first, L0_ffn_capital_shares, L0_ffn_ln1_w, L0_ffn_ln1_b, L0_ffn_ln2_w, L0_ffn_ln2_b, L0_ffn_Wr, L0_ffn_Wv, L0_ffn_Wo, L0_ffn_Ws, L0_ffn_K_rwkv, L0_ffn_V_rwkv, L0_ffn_conf_rwkv, L0_ffn_W1, L0_ffn_W2, L0_ffn_W3, L0_ffn_conf_trans, L0_ffn_w_diff, L0_ffn_W_aff, L0_ffn_W_bridge)
    x = x + _L0_attn_b_ref(_layernorm(x, axis=-1), L0_attn_b_Wq, L0_attn_b_Wk, L0_attn_b_Wv, L0_attn_b_Wo)
    x = x + _L0_ffn_ref(_layernorm(x, axis=-1), L0_ffn_v_first, L0_ffn_capital_shares, L0_ffn_ln1_w, L0_ffn_ln1_b, L0_ffn_ln2_w, L0_ffn_ln2_b, L0_ffn_Wr, L0_ffn_Wv, L0_ffn_Wo, L0_ffn_Ws, L0_ffn_K_rwkv, L0_ffn_V_rwkv, L0_ffn_conf_rwkv, L0_ffn_W1, L0_ffn_W2, L0_ffn_W3, L0_ffn_conf_trans, L0_ffn_w_diff, L0_ffn_W_aff, L0_ffn_W_bridge)
    return x

_drawn_inputs = setup_inputs


def setup_inputs(seed=0):
    import zlib

    import numpy as np

    out = dict(_drawn_inputs(seed))
    spreads = {'L0_attn_a_b_fc': (0.0, 0.1),
     'L0_ffn_ln1_w': (1.0, 0.6),
     'L0_ffn_ln1_b': (0.0, 0.8),
     'L0_ffn_ln2_w': (1.0, 0.581),
     'L0_ffn_ln2_b': (0.0, 0.369)}
    factors = {'L0_attn_a_w_qkv': 4.885,
     'L0_attn_a_w_conv': 8.0,
     'L0_attn_a_w_fc': 5.155,
     'L0_attn_b_Wq': 8.0,
     'L0_attn_b_Wk': 8.0,
     'L0_ffn_Wr': 6.66,
     'L0_ffn_Ws': 8.0,
     'L0_ffn_conf_rwkv': 3.769,
     'L0_ffn_W2': 8.0,
     'L0_ffn_conf_trans': 8.0,
     'L0_ffn_w_diff': 7.154}
    for name, (base, spread) in spreads.items():
        noise = np.random.default_rng([zlib.crc32(name.encode()), seed]).standard_normal(out[name].shape)
        drawn = base * np.exp(spread * noise) if base else spread * noise
        out[name] = jnp.asarray(drawn.astype(out[name].dtype))
    for name, factor in factors.items():
        out[name] = (out[name] * factor).astype(out[name].dtype)
    return out
```

```python
from contextlib import ExitStack

import concourse.bass as bass
import numpy as np
from concourse import mybir
from concourse.alu_op_type import AluOpType as ALU

F32 = mybir.dt.float32
F32R = mybir.dt.float32r
BF16 = mybir.dt.bfloat16
ACT = mybir.ActivationFunctionType
AX_X = mybir.AxisListType.X
MAX_ALL = bass.bass_isa.ReduceOp.max

P = 128
B, T, C = 8, 512, 256
TT = T // P
CT = C // P
XB = TT * C
EPS = 1e-5

HA, DA, M = 16, 64, 64
LG = T // M
NP = HA // 2
INNER = HA * DA
ITERS = 6
TAPS = 13
PAD = TAPS // 2
BAND = P + TAPS - 1

HB, DB = 16, 16
QUAD = 4

EXPERTS = 3
HID = 4 * C
HT = HID // P
NH = 2 * HT


def cols(tensor, start, n):
    return tensor[:, bass.ds(start, n)]


class Banks:

    def __init__(self, nc, ctx):
        self.data = [ctx.enter_context(nc.psum_tensor(f"bank{b}", [P, T], F32)) for b in range(8)]
        self.bank_full = [ctx.enter_context(nc.semaphore(f"bank_full{b}")) for b in range(8)]
        self.bank_free = [ctx.enter_context(nc.semaphore(f"bank_free{b}")) for b in range(8)]
        self.used = [0] * 8


class Fills:

    def __init__(self, banks, order, rounds=1):
        self.banks = banks
        self.before = list(banks.used)
        self.each = [0] * 8
        self.place = {}
        for name, b in order:
            self.place[name] = (b, self.each[b])
            self.each[b] += 1
        banks.used = [u + n * rounds for u, n in zip(banks.used, self.each)]

    def data(self, *name):
        return self.banks.data[self.place[name][0]]

    def filled(self, *name):
        return self.banks.bank_full[self.place[name][0]]

    def released(self, *name):
        return self.banks.bank_free[self.place[name][0]]

    def full(self, it, *name):
        b, k = self.place[name]
        return self.banks.bank_full[b], self.before[b] + it * self.each[b] + k + 1

    def read(self, it, *name):
        b, k = self.place[name]
        return self.banks.bank_free[b], self.before[b] + it * self.each[b] + k + 2

    def free(self, it, *name):
        b, k = self.place[name]
        return self.banks.bank_free[b], self.before[b] + it * self.each[b] + k + 1


class Core:

    def __init__(self, nc, ctx):
        self.nc = nc
        self.banks = Banks(nc, ctx)
        self.x = ctx.enter_context(nc.sbuf_tensor("x_tokens", [P, B * XB], F32))
        self.ident = ctx.enter_context(nc.sbuf_tensor("ident", [P, P], F32))
        self.neg_half = ctx.enter_context(nc.sbuf_tensor("neg_half", [P, TT], F32))
        self.setup_done = ctx.enter_context(nc.semaphore("setup_done"))
        self.ident_loaded = ctx.enter_context(nc.semaphore("ident_loaded"))
        self.waits_met = {
            e: ctx.enter_context(nc.semaphore(f"waits_met_{e}")) for e in ("pe", "act", "dve", "pool")
        }

    def met(self, eng, name):
        eng.sem_inc(self.waits_met[name], 1)


def sbuf(nc, ctx, name, shape, dtype=F32):
    return ctx.enter_context(nc.sbuf_tensor(name, shape, dtype))


def landmarks(core, la, dram):
    nc, banks, x = core.nc, core.banks, core.x
    with ExitStack() as ctx:
        sem = lambda name: ctx.enter_context(nc.semaphore(name))
        wqk = sbuf(nc, ctx, "wqk", [P, CT, 2 * INNER])
        stats = sbuf(nc, ctx, "lm_stats", [P, 2, TT, 6])
        mv = sbuf(nc, ctx, "lm_mv", [P, 2, TT, 2])
        rstd = sbuf(nc, ctx, "lm_rstd", [P, 2, TT])
        xn = sbuf(nc, ctx, "lm_xn", [P, 2, TT, C])
        xsum = sbuf(nc, ctx, "lm_xsum", [P, CT, B * M])
        neg_max = sbuf(nc, ctx, "lm_neg_max", [P, B, NP])
        row_sum = sbuf(nc, ctx, "lm_row_sum", [P, B, NP])
        row_rcp = sbuf(nc, ctx, "lm_row_rcp", [P, B, NP])
        sums = sbuf(nc, ctx, "lm_sums", [P, 2, B, NP])
        top = sbuf(nc, ctx, "lm_top", [P, 2])
        top_all = sbuf(nc, ctx, "lm_top_all", [P, 2])
        bound = sbuf(nc, ctx, "lm_bound", [P, 1])

        x_loaded = [sem("x_loaded0"), sem("x_loaded1")]
        w_loaded = sem("wqk_loaded")
        i64_loaded = sem("i64_loaded")
        stats_done, mv_done, var_done, rstd_done, xn_done = map(
            sem, ("lm_stats_done", "lm_mv_done", "lm_var_done", "lm_rstd_done", "lm_xn_done"))
        max_done, exp_done, sum_done, rcp_done, a_done, sums_done = map(
            sem, ("lm_max_done", "lm_exp_done", "lm_sum_done", "lm_rcp_done", "a_done", "sums_done"))
        top_done, top_all_done, bound_done = map(sem, ("top_done", "top_all_done", "bound_done"))

        turn = Fills(banks, [(("xT", par, ct), 2 * par + ct) for par in range(2) for ct in range(CT)], B // 2)
        proj = Fills(banks, [(("ql", n), n % 8) for n in range(2 * NP)])
        soft = Fills(banks, [f for b in range(B) for f in ((("sim", b), b % 4), (("aT", b), 4 + b % 4))])

        with nc.Block() as block:

            @block.sync
            def _(sp):
                for free in banks.bank_free:
                    sp.sem_inc(free, 1)

        with nc.Block() as block:

            @block.sync
            def _(sp):
                sp.dma_start(core.ident[:], dram["ident"]).then_inc(core.ident_loaded, 16)
                sp.dma_start(core.i64[:], dram["i64"]).then_inc(i64_loaded, 16)
                def load(it, par):
                    b = it * 2 + par
                    sp.dma_start(
                        cols(x, b * XB, XB).rearrange("p (t c) -> p t c", c=C),
                        dram["x"][bass.ds(b * T, T), :].rearrange("(t p) c -> p t c", p=P),
                    ).then_inc(x_loaded[par], 16)

                load(0, 0)
                load(0, 1)
                la.load(sp, dram)
                with sp.Fori(1, B // 2) as it:
                    for par in range(2):
                        sp.wait_ge(x_loaded[par], it * 16)
                        load(it, par)

            @block.scalar
            def _(act):
                act.dma_start(wqk[:], dram["w_qkv"][:, 0:2 * INNER].rearrange("(k p) n -> p k n", p=P)).then_inc(w_loaded, 16)
                for n in range(2 * NP):
                    act.wait_ge(*proj.full(0, "ql", n))
                    dst, scale = (core.ql, DA ** -0.5 / LG) if n < NP else (core.kl, 1.0 / LG)
                    nc.scalar.activation(dst[:, n % NP, :], proj.data("ql", n)[:], ACT.Copy, scale=scale).then_inc(
                        proj.released("ql", n), 1)
                for b in range(B + 1):
                    if b < B:
                        act.wait_ge(*soft.read(0, "sim", b))
                        nc.scalar.activation(core.a[:, b], core.a[:, b], ACT.Exp).then_inc(exp_done, 1)
                    if b >= 1:
                        act.wait_ge(*soft.full(0, "aT", b - 1))
                        nc.scalar.activation(
                            core.aT[:, b - 1], soft.data("aT", b - 1)[:].rearrange("p (j m) -> p j m", m=M), ACT.Copy
                        ).then_inc(soft.released("aT", b - 1), 1)

            @block.gpsimd
            def _(pool):
                nc.gpsimd.memset(core.neg_half[:], -0.5).then_inc(core.setup_done, 1)
                pool.wait_ge(core.setup_done, 1)
                with pool.Fori(0, B // 2) as it:
                    for par in range(2):
                        pool.wait_ge(mv_done, it * 2 * TT + (par + 1) * TT)
                        core.met(pool, "pool")
                        nc.gpsimd.tensor_scalar(rstd[:, par, :], mv[:, par, :, 1], EPS, None, ALU.add).then_inc(var_done, 1)
                        pool.wait_ge(var_done, it * 2 + par + 1)
                        nc.gpsimd.tensor_tensor(rstd[:, par, :], rstd[:, par, :], core.neg_half[:], ALU.pow).then_inc(
                            rstd_done, 1)
                pool.wait_ge(top_done, 2)
                nc.gpsimd.partition_all_reduce(top_all[:], top[:], P, MAX_ALL).then_inc(top_all_done, 1)

            @block.vector
            def _(dve):
                with dve.Fori(0, B // 2) as it:
                    for par in range(2):
                        dve.wait_ge(x_loaded[par], it * 16 + 16)
                        core.met(dve, "dve")
                        for t in range(TT):
                            nc.vector.bn_stats(stats[:, par, t, :], cols(x, (it * 2 + par) * XB + t * C, C)).then_inc(stats_done, 1)
                        for t in range(TT):
                            dve.wait_ge(stats_done, it * 2 * TT + par * TT + t + 1)
                            core.met(dve, "dve")
                            nc.vector.bn_aggr(mv[:, par, t, :], stats[:, par, t, :]).then_inc(mv_done, 1)
                    for par in range(2):
                        dve.wait_ge(rstd_done, it * 2 + par + 1)
                        core.met(dve, "dve")
                        for t in range(TT):
                            nc.vector.tensor_scalar(
                                xn[:, par, t, :], cols(x, (it * 2 + par) * XB + t * C, C),
                                mv[:, par, t, 0:1], rstd[:, par, t:t + 1], ALU.subtract, ALU.mult).then_inc(xn_done, 1)
                    for par in range(2):
                        for ct in range(CT):
                            dve.wait_ge(*turn.full(it, "xT", par, ct))
                            core.met(dve, "dve")
                            nc.vector.tensor_reduce(
                                xsum[:, ct, bass.ds((it * 2 + par) * M, M)],
                                turn.data("xT", par, ct)[:].rearrange("p (m l) -> p m l", l=LG),
                                AX_X, ALU.add).then_inc(turn.released("xT", par, ct), 1)
                grid = lambda ap: ap[:].rearrange("p (j m) -> p j m", m=M)
                spread = lambda ap: ap.unsqueeze(2).to_broadcast([P, NP, M])
                for b in range(B + 2):
                    if b < B:
                        dve.wait_ge(*soft.full(0, "sim", b))
                        nc.vector.tensor_reduce(neg_max[:, b], grid(soft.data("sim", b)), AX_X, ALU.max, negate=True).then_inc(max_done, 1)
                        dve.wait_ge(max_done, b + 1)
                        nc.vector.tensor_tensor(core.a[:, b], grid(soft.data("sim", b)), spread(neg_max[:, b]), ALU.add).then_inc(soft.released("sim", b), 1)
                    if 1 <= b <= B:
                        c = b - 1
                        dve.wait_ge(exp_done, c + 1)
                        nc.vector.tensor_reduce(row_sum[:, c], core.a[:, c], AX_X, ALU.add).then_inc(sum_done, 1)
                        dve.wait_ge(sum_done, c + 1)
                        nc.vector.reciprocal(row_rcp[:, c], row_sum[:, c]).then_inc(rcp_done, 1)
                        dve.wait_ge(rcp_done, c + 1)
                        nc.vector.tensor_tensor(core.a[:, c], core.a[:, c], spread(row_rcp[:, c]), ALU.mult).then_inc(a_done, 1)
                        dve.wait_ge(a_done, c + 1)
                        nc.vector.tensor_reduce(sums[:, 0, c], core.a[:, c], AX_X, ALU.add).then_inc(sums_done, 1)
                    if b >= 2:
                        c = b - 2
                        dve.wait_ge(*soft.read(0, "aT", c))
                        nc.vector.tensor_reduce(sums[:, 1, c], core.aT[:, c], AX_X, ALU.add).then_inc(sums_done, 1)
                dve.wait_ge(sums_done, 2 * B)
                for side in range(2):
                    nc.vector.tensor_reduce(top[:, side:side + 1], sums[:, side].rearrange("p b j -> p (b j)"), AX_X, ALU.max).then_inc(top_done, 1)
                dve.wait_ge(top_all_done, 1)
                nc.vector.tensor_tensor(bound[:], top_all[:, 0:1], top_all[:, 1:2], ALU.mult).then_inc(bound_done, 1)
                dve.wait_ge(bound_done, 1)
                nc.vector.reciprocal(core.inv_bound[:], bound[:]).then_inc(bound_done, 1)
                dve.wait_ge(bound_done, 2)

            @block.tensor
            def _(pe):
                pe.wait_ge(core.ident_loaded, 16)
                with pe.Fori(0, B // 2) as it:
                    for par in range(2):
                        pe.wait_ge(xn_done, it * 2 * TT + (par + 1) * TT)
                        for ct in range(CT):
                            pe.wait_ge(*turn.free(it, "xT", par, ct))
                            core.met(pe, "pe")
                            for t in range(TT):
                                last = nc.tensor.transpose(
                                    turn.data("xT", par, ct)[:, t * P:(t + 1) * P], xn[:, par, t, ct * P:(ct + 1) * P],
                                    core.ident[:])
                            last.then_inc(turn.filled("xT", par, ct), 1)
                for par in range(2):
                    for ct in range(CT):
                        pe.wait_ge(*turn.read(B // 2 - 1, "xT", par, ct))
                pe.wait_ge(w_loaded, 16)
                for n in range(2 * NP):
                    pe.wait_ge(*proj.free(0, "ql", n))
                    for ct in range(CT):
                        last = nc.tensor.matmul(proj.data("ql", n)[:], wqk[:, ct, n * P:(n + 1) * P], xsum[:, ct, :],
                                                start=ct == 0, stop=ct == CT - 1)
                    last.then_inc(proj.filled("ql", n), 1)
                for n in range(NP, 2 * NP):
                    pe.wait_ge(*proj.read(0, "ql", n))
                pe.wait_ge(i64_loaded, 16)
                for b in range(B + 1):
                    if b < B:
                        pe.wait_ge(*soft.free(0, "sim", b))
                        for j in range(NP):
                            for h in (slice(0, M), slice(M, 2 * M)):
                                last = nc.tensor.matmul(
                                    soft.data("sim", b)[h, j * M:(j + 1) * M], core.ql[h, j, b * M:(b + 1) * M],
                                    core.kl[h, j, b * M:(b + 1) * M], start=True, stop=True)
                        last.then_inc(soft.filled("sim", b), 1)
                    if b >= 1:
                        c = b - 1
                        pe.wait_ge(a_done, c + 1)
                        pe.wait_ge(*soft.free(0, "aT", c))
                        for j in range(NP):
                            for h in (slice(0, M), slice(M, 2 * M)):
                                last = nc.tensor.matmul(soft.data("aT", c)[h, j * M:(j + 1) * M], core.a[h, c, j, :],
                                                        core.i64[h, :], start=True, stop=True)
                        last.then_inc(soft.filled("aT", c), 1)


SLOTS = 4
GP = NP // 2
GROUPS = B * NP // GP


def pseudo_inverse(core, la, dram):
    nc, banks = core.nc, core.banks
    RESTORE = 2
    with ExitStack() as ctx:
        sem = lambda name: ctx.enter_context(nc.semaphore(name))
        grp = lambda name: sbuf(nc, ctx, name, [P, SLOTS, GP, M])
        i7, i15, i13 = (sbuf(nc, ctx, f"pi_i{n}", [P, GP, M]) for n in (7, 15, 13))
        wz = sbuf(nc, ctx, "pi_wz", [P, SLOTS, GP, 2, M])
        at, t1, t3, p, z = map(grp, ("pi_at", "pi_t1", "pi_t3", "pi_p", "pi_z"))
        inverse = grp("pi_inverse")
        taps = sbuf(nc, ctx, "taps", [P, HA, TAPS])
        shifted = sbuf(nc, ctx, "shifted_ident", [P, BAND + TAPS - 1])
        term = sbuf(nc, ctx, "band_term", [P, HA, BAND])
        taps_loaded, term_done, band_done = map(sem, ("taps_loaded", "band_term_done", "band_done"))
        eyes_done, zt0_done, at_done, t1_done, inv_done = map(
            sem, ("eyes_done", "zt0_done", "pi_at_done", "t1_done", "inv_done"))

        order = []
        for s in range(SLOTS):
            names = [("w0",)]
            for k in range(ITERS):
                names += [("t", k), ("u", k), ("wz", k)] + ([("w", k)] if k == RESTORE else [])
            order += [((*n, s), 2 * s + i % 2) for i, n in enumerate(names)]
        fills = Fills(banks, order, GROUPS // SLOTS)
        halves = [slice(0, M), slice(M, 2 * M)]

        group = lambda tensor, it, s: cols(tensor[:].rearrange("p b j m -> p (b j m)"), (it * SLOTS + s) * GP * M, GP * M).rearrange(
            "p (j m) -> p j m", m=M)
        half = lambda *name: fills.data(*name)[:, 0:GP * M].rearrange("p (j m) -> p j m", m=M)
        pair = lambda *name: fills.data(*name)[:].rearrange("p (j q m) -> p j q m", q=2, m=M)

        def w_written(it, k, s):
            return fills.read(it, *(("w0",) if k == 0 else ("w", k - 1) if k - 1 == RESTORE else ("wz", k - 1)), s)

        with nc.Block() as block:

            @block.sync
            def _(sp):
                sp.dma_start(taps[:].rearrange("p h k -> p (h k)"), dram["taps"].partition_broadcast(P)).then_inc(taps_loaded, 16)
                sp.dma_start(shifted[:], dram["shifted_ident"]).then_inc(taps_loaded, 16)

            @block.gpsimd
            def _(pool):
                diagonal = lambda k: shifted[:, k:k + BAND].unsqueeze(1).to_broadcast([P, HA, BAND])
                tap = lambda k: taps[:, :, k:k + 1].to_broadcast([P, HA, BAND])
                pool.wait_ge(taps_loaded, 32)
                nc.gpsimd.tensor_tensor(la.band[:], tap(0), diagonal(0), ALU.mult).then_inc(band_done, 1)
                for k in range(1, TAPS):
                    pool.wait_ge(band_done, k)
                    nc.gpsimd.tensor_tensor(term[:], tap(k), diagonal(k), ALU.mult).then_inc(term_done, 1)
                    pool.wait_ge(term_done, k)
                    nc.gpsimd.tensor_tensor(la.band[:], la.band[:], term[:], ALU.add).then_inc(band_done, 1)
                pool.wait_ge(band_done, TAPS)
                nc.gpsimd.tensor_tensor(la.band[:], la.band[:], diagonal(PAD), ALU.add).then_inc(band_done, 1)
                pool.wait_ge(band_done, TAPS + 1)

            @block.scalar
            def _(act):
                act.sem_inc(inv_done, 1)
                with act.Fori(0, GROUPS // SLOTS) as it:
                    for s in range(SLOTS):
                        nc.scalar.activation(at[:, s], group(core.aT, it, s), ACT.Copy).then_inc(at_done, 1)
                    for s in range(SLOTS):
                        act.wait_ge(*fills.full(it, "w0", s))
                        nc.scalar.activation(wz[:, s, :, 0, :], half("w0", s), ACT.Copy, scale=core.inv_bound[:, 0:1]).then_inc(
                            fills.released("w0", s), 1)
                    for k in range(ITERS):
                        for s in range(SLOTS):
                            act.wait_ge(*fills.full(it, "wz", k, s))
                            if k == ITERS - 1:
                                core.met(act, "act")
                                nc.scalar.activation(inverse[:, s], pair("wz", k, s)[:, :, 1, :], ACT.Copy).then_inc(
                                    fills.released("wz", k, s), 1)
                                act.wait_ge(*fills.read(it, "wz", k, s))
                                core.met(act, "act")
                                nc.scalar.activation(group(core.a, it, s), inverse[:, s], ACT.Copy).then_inc(inv_done, 1)
                            elif k == RESTORE:
                                nc.scalar.activation(z[:, s], pair("wz", k, s)[:, :, 0, :], ACT.Copy)
                                nc.scalar.activation(wz[:, s, :, 1, :], pair("wz", k, s)[:, :, 1, :], ACT.Copy).then_inc(
                                    fills.released("wz", k, s), 1)
                            else:
                                nc.scalar.activation(wz[:, s], pair("wz", k, s), ACT.Copy).then_inc(fills.released("wz", k, s), 1)
                        if k == RESTORE:
                            for s in range(SLOTS):
                                act.wait_ge(*fills.full(it, "w", k, s))
                                nc.scalar.activation(wz[:, s, :, 0, :], half("w", k, s), ACT.Copy).then_inc(
                                    fills.released("w", k, s), 1)

            @block.vector
            def _(dve):
                for tile, n in ((i7, 7.0), (i15, 15.0), (i13, 13.0 / 4)):
                    nc.vector.tensor_scalar(tile[:], core.i64[:].unsqueeze(1).to_broadcast([P, GP, M]), n, None, ALU.mult).then_inc(
                        eyes_done, 1)
                dve.wait_ge(eyes_done, 3)
                with dve.Fori(0, GROUPS // SLOTS) as it:
                    for s in range(SLOTS):
                        dve.wait_ge(inv_done, it * SLOTS + 1)
                        core.met(dve, "dve")
                        nc.vector.tensor_scalar(wz[:, s, :, 1, :], group(core.a, it, s), core.inv_bound[:, 0:1], None,
                                                ALU.mult).then_inc(zt0_done, 1)
                    for k in range(ITERS):
                        for s in range(SLOTS):
                            dve.wait_ge(*w_written(it, k, s))
                            nc.vector.tensor_tensor(t1[:, s], i7[:], wz[:, s, :, 0, :], ALU.subtract).then_inc(t1_done, 1)
                        for s in range(SLOTS):
                            dve.wait_ge(*fills.full(it, "t", k, s))
                            nc.vector.tensor_tensor(t3[:, s], i15[:], half("t", k, s), ALU.subtract).then_inc(
                                fills.released("t", k, s), 1)
                        for s in range(SLOTS):
                            dve.wait_ge(*fills.full(it, "u", k, s))
                            nc.vector.scalar_tensor_tensor(out=p[:, s], in0=half("u", k, s), scalar=-0.25, in1=i13[:],
                                                           op0=ALU.mult, op1=ALU.add).then_inc(fills.released("u", k, s), 1)

            @block.tensor
            def _(pe):
                def products(data, lhs, rhs):
                    for j in range(GP):
                        for h in halves:
                            last = nc.tensor.matmul(data[h, j * M:(j + 1) * M], lhs[h, j], rhs[h, j], start=True, stop=True)
                    return last

                with pe.Fori(0, GROUPS // SLOTS) as it:
                    for s in range(SLOTS):
                        pe.wait_ge(at_done, it * SLOTS + s + 1)
                        pe.wait_ge(*fills.free(it, "w0", s))
                        core.met(pe, "pe")
                        products(fills.data("w0", s), at[:, s], at[:, s]).then_inc(fills.filled("w0", s), 1)
                    for k in range(ITERS):
                        for s in range(SLOTS):
                            pe.wait_ge(t1_done, (it * ITERS + k) * SLOTS + s + 1)
                            pe.wait_ge(*fills.free(it, "t", k, s))
                            core.met(pe, "pe")
                            products(fills.data("t", k, s), wz[:, s, :, 0, :], t1[:, s]).then_inc(fills.filled("t", k, s), 1)
                        for s in range(SLOTS):
                            pe.wait_ge(*fills.read(it, "t", k, s))
                            pe.wait_ge(*fills.free(it, "u", k, s))
                            core.met(pe, "pe")
                            products(fills.data("u", k, s), wz[:, s, :, 0, :], t3[:, s]).then_inc(fills.filled("u", k, s), 1)
                        for s in range(SLOTS):
                            pe.wait_ge(*fills.read(it, "u", k, s))
                            if k == 0:
                                pe.wait_ge(zt0_done, it * SLOTS + s + 1)
                            pe.wait_ge(*fills.free(it, "wz", k, s))
                            core.met(pe, "pe")
                            data = pair("wz", k, s)
                            for j in range(GP):
                                for h in halves:
                                    if k == RESTORE:
                                        nc.tensor.matmul(data[h, j, 0], wz[h, s, j, 1, :], p[h, s, j, :], start=True, stop=True)
                                    if k in (RESTORE, ITERS - 1):
                                        last = nc.tensor.matmul(data[h, j, 1], p[h, s, j, :], wz[h, s, j, 1, :], start=True, stop=True)
                                    else:
                                        last = nc.tensor.matmul(data[h, j], p[h, s, j, :], wz[h, s, j], start=True, stop=True)
                            last.then_inc(fills.filled("wz", k, s), 1)
                        if k == RESTORE:
                            for s in range(SLOTS):
                                pe.wait_ge(*fills.read(it, "wz", k, s))
                                pe.wait_ge(*fills.free(it, "w", k, s))
                                core.met(pe, "pe")
                                products(fills.data("w", k, s), at[:, s], z[:, s]).then_inc(fills.filled("w", k, s), 1)


class AttentionA:

    def __init__(self, nc, ctx):
        self.wqT, self.wkT, self.wfc = (sbuf(nc, ctx, n, [P, NP, C]) for n in ("wqT", "wkT", "wfc"))
        self.wv = sbuf(nc, ctx, "wv_a", [P, CT, INNER])
        self.bias = sbuf(nc, ctx, "bias_fc", [P, C])
        self.band = sbuf(nc, ctx, "band", [P, HA, BAND])
        self.loaded = ctx.enter_context(nc.semaphore("weights_a_loaded"))
        self.loads = 0

    def load(self, eng, dram):
        rows = lambda ap: ap.rearrange("(j p) c -> p j c", p=P)
        for dst, src in (
                (self.wqT, rows(dram["wqT"])), (self.wkT, rows(dram["wkT"])), (self.wfc, rows(dram["w_fc"])),
                (self.wv, dram["w_qkv"][:, 2 * INNER:].rearrange("(k p) n -> p k n", p=P)),
                (self.bias, dram["b_fc"].partition_broadcast(P))):
            eng.dma_start(dst[:], src).then_inc(self.loaded, 16)
            self.loads += 16


def layer_a(core, la):
    nc, banks, x = core.nc, core.banks, core.x
    HH = NP // 2
    with ExitStack() as ctx:
        sem = lambda name: ctx.enter_context(nc.semaphore(name))
        buf = lambda name, shape: sbuf(nc, ctx, name, shape)
        stats, mv, rstd = buf("a_stats", [P, TT, 6]), buf("a_mv", [P, TT, 2]), buf("a_rstd", [P, TT])
        xn, xnT = buf("a_xn", [P, TT, C]), buf("a_xnT", [P, CT, T])
        kl_diag, ql_diag = buf("kl_diag", [P, NP, P]), buf("ql_diag", [P, NP, P])
        u, g = buf("u", [P, CT, INNER]), buf("g", [P, CT, INNER])
        fc = g[:].rearrange("p k (j c) -> p (k j) c", c=C)
        v = buf("v_a", [P, TT, INNER // 2])
        probs1 = buf("probs1", [P, TT, INNER])
        neg_max1, sum1, rcp1 = (buf(n, [P, 2 * TT, NP]) for n in ("neg_max1", "sum1", "rcp1"))
        e3, e3T = buf("e3", [P, 2, T]), buf("e3T", [P, 2, T])
        neg_max3, sum3, rcp3 = (buf(n, [P, NP]) for n in ("neg_max3", "sum3", "rcp3"))
        av3, avT, inverse = (buf(n, [P, NP, M]) for n in ("av3", "avT", "inverse_staged"))
        conv = buf("conv", [P, 2, T])
        names = ("stats_done", "mv_done", "var_done", "rstd_done", "xn_done", "staged", "diag_zeroed", "max1_done",
                 "exp1_done", "sum1_done", "rcp1_done", "probs1_done", "max3_done", "rcp3_done", "bias_added", "inverse_here")
        s = {n: sem("a_" + n) for n in names}

        order = [("xT", k) for k in range(CT)] + [("u", k) for k in range(4)] + [("g", k) for k in range(4)]
        for f in range(TT):
            order += [("v", 0, f), ("s1", f)]

        def s3_steps(half):
            for j in range(half * HH, (half + 1) * HH + 1):
                if j < (half + 1) * HH:
                    yield ("s3", j)
                    if half == 0:
                        yield ("s1", TT + j)
                if j > half * HH:
                    yield ("e3T", j - 1)
                    yield ("av3", j - 1)

        order += [n for n in s3_steps(0) if n[0] != "av3"] + [("v", 1, t) for t in range(TT)]
        order += [n for n in s3_steps(1) if n[0] != "av3"] + [("avT",)] + [("fc", k) for k in range(4)] + [("c", j) for j in range(NP)]
        fills = Fills(banks, [(n, i % 6) for i, n in enumerate(order)] + [(("av3", 0), 6), (("av3", 1), 7), (("y", 0), 6), (("y", 1), 7)], B)
        heads = lambda ap: ap.rearrange("p (j m) -> p j m", m=M)
        spread = lambda ap, n: ap.unsqueeze(2).to_broadcast([P, n, M])

        with nc.Block() as block:

            @block.sync
            def _(sp):
                sp.wait_ge(la.loaded, la.loads)

            @block.vector
            def _(dve):
                def statistics(n):
                    dve.wait_ge(s["xn_done"], n * TT)
                    core.met(dve, "dve")
                    for t in range(TT):
                        nc.vector.bn_stats(stats[:, t, :], cols(x, n * XB + t * C, C)).then_inc(s["stats_done"], 1)
                    for t in range(TT):
                        dve.wait_ge(s["stats_done"], n * TT + t + 1)
                        core.met(dve, "dve")
                        nc.vector.bn_aggr(mv[:, t, :], stats[:, t, :]).then_inc(s["mv_done"], 1)

                def normalise(n):
                    dve.wait_ge(s["rstd_done"], n + 1)
                    core.met(dve, "dve")
                    for t in range(TT):
                        nc.vector.tensor_scalar(xn[:, t, :], cols(x, n * XB + t * C, C), mv[:, t, 0:1], rstd[:, t:t + 1],
                                                ALU.subtract, ALU.mult).then_inc(s["xn_done"], 1)
                    for src, dst in ((core.kl, kl_diag), (core.ql, ql_diag)):
                        for h in (slice(0, M), slice(M, 2 * M)):
                            nc.vector.tensor_scalar(dst[h, :, h], src[h, :, bass.ds(n * M, M)], 1.0, None, ALU.mult).then_inc(
                                s["staged"], 1)

                def shift1(it, f):
                    dve.wait_ge(*fills.full(it, "s1", f))
                    core.met(dve, "dve")
                    scores = heads(fills.data("s1", f)[:])
                    t, half = f % TT, f // TT
                    nc.vector.tensor_reduce(neg_max1[:, f], scores, AX_X, ALU.max, negate=True).then_inc(s["max1_done"], 1)
                    dve.wait_ge(s["max1_done"], it * 2 * TT + f + 1)
                    nc.vector.tensor_tensor(heads(probs1[:, t, half * 512:(half + 1) * 512]), scores, spread(neg_max1[:, f], NP),
                                            ALU.add).then_inc(fills.released("s1", f), 1)

                def sums1(it, f):
                    t, half = f % TT, f // TT
                    dve.wait_ge(s["exp1_done"], it * 2 * TT + f + 1)
                    core.met(dve, "dve")
                    nc.vector.tensor_reduce(sum1[:, f], heads(probs1[:, t, half * 512:(half + 1) * 512]), AX_X, ALU.add).then_inc(
                        s["sum1_done"], 1)
                    dve.wait_ge(s["sum1_done"], it * 2 * TT + f + 1)
                    core.met(dve, "dve")
                    nc.vector.reciprocal(rcp1[:, f], sum1[:, f]).then_inc(s["rcp1_done"], 1)

                def max3(it, j):
                    dve.wait_ge(*fills.full(it, "s3", j))
                    core.met(dve, "dve")
                    nc.vector.tensor_reduce(neg_max3[:, j:j + 1], fills.data("s3", j)[:], AX_X, ALU.max, negate=True).then_inc(
                        s["max3_done"], 1)

                def scale3(it, half):
                    pairs = slice(half * HH, (half + 1) * HH)
                    for j in range(half * HH, (half + 1) * HH):
                        dve.wait_ge(*fills.read(it, "s3", j))
                    core.met(dve, "dve")
                    nc.vector.reciprocal(rcp3[:, pairs], sum3[:, pairs]).then_inc(s["rcp3_done"], 1)
                    dve.wait_ge(s["rcp3_done"], it * 2 + half + 1)
                    dve.wait_ge(*fills.full(it, "av3", half))
                    nc.vector.tensor_tensor(av3[:, pairs], heads(fills.data("av3", half)[:, 0:HH * M]), spread(rcp3[:, pairs], HH),
                                            ALU.mult).then_inc(fills.released("av3", half), 1)

                def batch(it, last):
                    if not last:
                        statistics(it + 1)
                    for f in range(TT):
                        shift1(it, f)
                        if f:
                            sums1(it, f - 1)
                    if not last:
                        normalise(it + 1)
                    nc.vector.tensor_scalar(inverse[:].rearrange("p j m -> p (j m)"),
                                            cols(core.a[:].rearrange("p b j m -> p (b j m)"), it * NP * M, NP * M), 1.0, None,
                                            ALU.mult).then_inc(s["inverse_here"], 1)
                    for j in range(HH):
                        max3(it, j)
                        shift1(it, TT + j)
                        sums1(it, TT + j - 1)
                    sums1(it, 2 * TT - 1)
                    scale3(it, 0)
                    for j in range(HH, NP):
                        max3(it, j)
                    scale3(it, 1)
                    dve.wait_ge(s["bias_added"], it * 2 + 2)
                    for k in range(2):
                        dve.wait_ge(*fills.full(it, "y", k))
                        xs = cols(x, it * XB + k * 512, 512)
                        nc.vector.tensor_tensor(xs, xs, fills.data("y", k)[:], ALU.add).then_inc(fills.released("y", k), 1)

                for diag in (kl_diag, ql_diag):
                    nc.vector.memset(diag[:], 0.0).then_inc(s["diag_zeroed"], 1)
                dve.wait_ge(s["diag_zeroed"], 2)
                statistics(0)
                normalise(0)
                with dve.Fori(0, B - 1) as it:
                    batch(it, False)
                batch(B - 1, True)

            @block.gpsimd
            def _(pool):
                def inverse_deviation(n):
                    pool.wait_ge(s["mv_done"], (n + 1) * TT)
                    core.met(pool, "pool")
                    nc.gpsimd.tensor_scalar(rstd[:], mv[:, :, 1], EPS, None, ALU.add).then_inc(s["var_done"], 1)
                    pool.wait_ge(s["var_done"], n + 1)
                    nc.gpsimd.tensor_tensor(rstd[:], rstd[:], core.neg_half[:], ALU.pow).then_inc(s["rstd_done"], 1)

                def batch(it, last):
                    if not last:
                        inverse_deviation(it + 1)
                    pool.wait_ge(s["xn_done"], it * TT + TT)
                    core.met(pool, "pool")
                    for k in range(2):
                        xs = cols(x, it * XB + k * 512, 512).rearrange("p (t c) -> p t c", c=C)
                        nc.gpsimd.tensor_tensor(xs, xs, la.bias[:].unsqueeze(1).to_broadcast([P, 2, C]), ALU.add).then_inc(
                            s["bias_added"], 1)
                    for f in range(2 * TT):
                        t, half = f % TT, f // TT
                        pool.wait_ge(s["rcp1_done"], it * 2 * TT + f + 1)
                        probs = heads(probs1[:, t, half * 512:(half + 1) * 512])
                        nc.gpsimd.tensor_tensor(probs, probs, spread(rcp1[:, f], NP), ALU.mult).then_inc(s["probs1_done"], 1)

                inverse_deviation(0)
                with pool.Fori(0, B - 1) as it:
                    batch(it, False)
                batch(B - 1, True)

            @block.scalar
            def _(act):
                def copy(it, dst, name):
                    act.wait_ge(*fills.full(it, *name))
                    nc.scalar.activation(dst, fills.data(*name)[:], ACT.Copy).then_inc(fills.released(*name), 1)

                def exp1(it, f):
                    t, half = f % TT, f // TT
                    act.wait_ge(*fills.read(it, "s1", f))
                    probs = probs1[:, t, half * 512:(half + 1) * 512]
                    nc.scalar.activation(probs, probs, ACT.Exp, scale=DA ** -0.5).then_inc(s["exp1_done"], 1)

                def exp3(it, j):
                    act.wait_ge(s["max3_done"], it * NP + j + 1)
                    nc.scalar.activation(e3[:, j % 2], fills.data("s3", j)[:], ACT.Exp, bias=neg_max3[:, j:j + 1],
                                         accum_out=sum3[:, j:j + 1]).then_inc(fills.released("s3", j), 1)

                def batch(it):
                    for k in range(CT):
                        copy(it, xnT[:, k], ("xT", k))
                    for name, dst in (("u", u), ("g", g)):
                        for k in range(4):
                            copy(it, dst[:, k // 2, k % 2 * 512:(k % 2 + 1) * 512], (name, k))
                    for f in range(TT):
                        copy(it, v[:, f], ("v", 0, f))
                        exp1(it, f)
                    for j in range(HH + 1):
                        if j < HH:
                            exp3(it, j)
                            exp1(it, TT + j)
                        if j:
                            copy(it, e3T[:, (j - 1) % 2], ("e3T", j - 1))
                    for t in range(TT):
                        copy(it, v[:, t], ("v", 1, t))
                    for j in range(HH, NP + 1):
                        if j < NP:
                            exp3(it, j)
                        if j > HH:
                            copy(it, e3T[:, (j - 1) % 2], ("e3T", j - 1))
                    copy(it, avT[:].rearrange("p j m -> p (j m)"), ("avT",))
                    for k in range(4):
                        copy(it, fc[:, 2 * k:2 * k + 2].rearrange("p j c -> p (j c)"), ("fc", k))
                    for j in range(NP):
                        copy(it, conv[:, j % 2], ("c", j))

                with act.Fori(0, B) as it:
                    batch(it)

            @block.tensor
            def _(pe):
                def begin(it, *name):
                    pe.wait_ge(*fills.free(it, *name))
                    core.met(pe, "pe")
                    return fills.data(*name)

                def from_xn(it, name, t, weight):
                    data = begin(it, *name)
                    for k in range(CT):
                        last = nc.tensor.matmul(data[:], xnT[:, k, t * P:(t + 1) * P], weight(k), start=k == 0, stop=k == CT - 1)
                    last.then_inc(fills.filled(*name), 1)

                def scores1(it, f):
                    t, half = f % TT, f // TT
                    from_xn(it, ("s1", f), t, lambda k: u[:, k, half * 512:(half + 1) * 512])

                def values(it, half):
                    for t in range(TT):
                        from_xn(it, ("v", half, t), t, lambda k: la.wv[:, k, half * 512:(half + 1) * 512])
                        if half == 0:
                            if t == 0:
                                for k in range(4):
                                    pe.wait_ge(*fills.read(it, "u", k))
                            scores1(it, t)

                def scores3(it, j):
                    data = begin(it, "s3", j)
                    for k in range(CT):
                        last = nc.tensor.matmul(data[:], g[:, k, j * P:(j + 1) * P], xnT[:, k, :], start=k == 0, stop=k == CT - 1)
                    last.then_inc(fills.filled("s3", j), 1)

                def turn3(it, j):
                    pe.wait_ge(*fills.read(it, "s3", j))
                    data = begin(it, "e3T", j)
                    for t in range(TT):
                        last = nc.tensor.transpose(data[:, t * P:(t + 1) * P], e3[:, j % 2, t * P:(t + 1) * P], core.ident[:])
                    last.then_inc(fills.filled("e3T", j), 1)

                def values3(it, j):
                    half, jj = j // HH, j % HH
                    if jj == 0:
                        for t in range(TT):
                            pe.wait_ge(*fills.read(it, "v", half, t))
                        begin(it, "av3", half)
                    data = fills.data("av3", half)
                    pe.wait_ge(*fills.read(it, "e3T", j))
                    core.met(pe, "pe")
                    for t in range(TT):
                        for hh in range(2):
                            last = nc.tensor.matmul(
                                data[hh * M:(hh + 1) * M, jj * M:(jj + 1) * M], e3T[:, j % 2, t * P + hh * M:t * P + (hh + 1) * M],
                                v[:, t, (2 * jj + hh) * DA:(2 * jj + hh + 1) * DA], start=t == 0, stop=t == TT - 1,
                                skip_group_check=True)
                    if jj == HH - 1:
                        last.then_inc(fills.filled("av3", half), 1)

                with pe.Fori(0, B) as it:
                    pe.wait_ge(s["xn_done"], it * TT + TT)
                    for k in range(CT):
                        data = begin(it, "xT", k)
                        for t in range(TT):
                            last = nc.tensor.transpose(data[:, t * P:(t + 1) * P], xn[:, t, k * P:(k + 1) * P], core.ident[:])
                        last.then_inc(fills.filled("xT", k), 1)
                    pe.wait_ge(s["staged"], it * 4 + 4)
                    for name, weight, diag in (("u", la.wqT, kl_diag), ("g", la.wkT, ql_diag)):
                        for k in range(4):
                            data = begin(it, name, k)
                            for j in range(HH):
                                pair = k % 2 * HH + j
                                last = nc.tensor.matmul(data[:, j * P:(j + 1) * P], weight[:, pair, k // 2 * P:(k // 2 + 1) * P],
                                                        diag[:, pair, :], start=True, stop=True)
                            last.then_inc(fills.filled(name, k), 1)
                    for k in range(CT):
                        pe.wait_ge(*fills.read(it, "xT", k))
                    values(it, 0)
                    for k in range(4):
                        pe.wait_ge(*fills.read(it, "g", k))
                    for n in s3_steps(0):
                        {"s3": scores3, "s1": scores1, "e3T": turn3, "av3": values3}[n[0]](it, n[1])
                    values(it, 1)
                    for n in s3_steps(1):
                        {"s3": scores3, "e3T": turn3, "av3": values3}[n[0]](it, n[1])
                    for half in range(2):
                        pe.wait_ge(*fills.read(it, "av3", half))
                    pe.wait_ge(s["inverse_here"], it + 1)
                    data = begin(it, "avT")
                    for j in range(NP):
                        for h in (slice(0, M), slice(M, 2 * M)):
                            last = nc.tensor.matmul(data[h, j * M:(j + 1) * M], av3[h, j, :], inverse[h, j, :], start=True, stop=True)
                    last.then_inc(fills.filled("avT"), 1)
                    pe.wait_ge(*fills.read(it, "avT"))
                    for k in range(4):
                        data = begin(it, "fc", k)
                        for jj in range(2):
                            for h in (slice(0, M), slice(M, 2 * M)):
                                last = nc.tensor.matmul(data[h, jj * C:(jj + 1) * C], avT[h, 2 * k + jj, :], la.wfc[h, 2 * k + jj, :],
                                                        start=True, stop=True)
                        last.then_inc(fills.filled("fc", k), 1)
                    pe.wait_ge(s["probs1_done"], it * 2 * TT + 2 * TT)
                    for j in range(NP + 1):
                        if j < NP:
                            data = begin(it, "c", j)
                            for t in range(TT):
                                lo, hi = max(0, t * P - PAD), min(T, (t + 1) * P + PAD)
                                off = lo - (t * P - PAD)
                                for hh in range(2):
                                    h = 2 * j + hh
                                    last = nc.tensor.matmul(
                                        data[hh * M:(hh + 1) * M, lo:hi], probs1[:, t, h * M:(h + 1) * M],
                                        la.band[:, h, off:off + hi - lo], start=t == 0, stop=t == TT - 1, skip_group_check=True)
                            last.then_inc(fills.filled("c", j), 1)
                        if j:
                            if j == 1:
                                for k in range(4):
                                    pe.wait_ge(*fills.read(it, "fc", k))
                                for k in range(2):
                                    begin(it, "y", k)
                            pe.wait_ge(*fills.read(it, "c", j - 1))
                            core.met(pe, "pe")
                            for t in range(TT):
                                last = nc.tensor.matmul(
                                    fills.data("y", t // 2)[:, t % 2 * C:(t % 2 + 1) * C], conv[:, (j - 1) % 2, t * P:(t + 1) * P],
                                    fc[:, j - 1, :], start=j == 1 and t % 2 == 0, stop=j == NP, skip_group_check=True)
                                if j == NP and t % 2 == 1:
                                    last.then_inc(fills.filled("y", t // 2), 1)


class FeedForward:

    def __init__(self, nc, ctx, run):
        self.run = run
        split = lambda name, shape: [sbuf(nc, ctx, f"{name}_{part}_{run}", shape, F32R) for part in ("hi", "lo")]
        self.k = split("k_rwkv", [P, 2, CT, HID])
        self.v = split("v_rwkv", [P, 2, HT, C])
        self.square = {n: split(n.lower() + "_ff", [P, CT, C]) for n in ("Wr", "Wv", "Wo", "W1", "W3", "WsW2")}
        self.router = split("router", [P, CT, 8])
        self.bias = sbuf(nc, ctx, f"bias_ff_{run}", [P, NH + 16])
        self.shares = sbuf(nc, ctx, f"shares_{run}", [P, EXPERTS])

    def bias_of(self, name, k):
        at = NH + 2 * ("Wr", "Wv", "WsW2", "W1").index(name) + k
        return self.bias[:, at:at + 1]


def prepare_ff(core, ff, dram):
    nc, banks = core.nc, core.banks
    RING = 4
    with ExitStack() as ctx:
        sem = lambda name: ctx.enter_context(nc.semaphore(f"{name}_{ff.run}"))
        buf = lambda name, shape: sbuf(nc, ctx, f"{name}_{ff.run}", shape)
        raw = buf("raw", [P, RING, HID])
        norms = buf("norms", [P, 4, CT])
        wsT, w2 = (buf(n, [P, CT, C]) for n in ("wsT", "w2"))
        product = buf("ws_w2", [P, CT, C])
        router = buf("router_raw", [P, CT, 8])
        offsets = buf("ln2_offsets", [P, CT, P])
        loaded = [sem(f"raw_loaded{r}") for r in range(RING)]
        small_loaded, hi_done, lo_done, used, offsets_done = map(
            sem, ("small_loaded", "w_hi_done", "w_lo_done", "w_biases_done", "offsets_done"))
        pieces = []
        halves = lambda tile, e, k: [w[:, e, k, :] for w in tile]
        for e in range(2):
            for k in range(CT):
                pieces.append((dram["K_rwkv"][e, k * P:(k + 1) * P, :], halves(ff.k, e, k), [(2, k, 0, HID)],
                               [(e * HT + s, s * P, k) for s in range(HT)]))
        for name, norm in (("Wr", 0), ("Wv", 0), ("W1", 2)):
            at = NH + 2 * ("Wr", "Wv", "WsW2", "W1").index(name)
            pieces.append((dram[name].rearrange("(k p) n -> p k n", p=P), [w[:].rearrange("p k n -> p (k n)") for w in ff.square[name]],
                           [(norm, k, k * C, C) for k in range(CT)],
                           [(at + o, k * C + o * P, k) for o in range(CT) for k in range(CT)]))
        for name in ("Wo", "W3"):
            pieces.append((dram[name].rearrange("(k p) n -> p k n", p=P), [w[:].rearrange("p k n -> p (k n)") for w in ff.square[name]],
                           [(None, None, 0, CT * C)], []))
        for e in range(2):
            for half in range(2):
                rows = slice(half * HID // 2, (half + 1) * HID // 2)
                tiles = slice(half * HT // 2, (half + 1) * HT // 2)
                pieces.append((dram["V_rwkv"][e, rows, :].rearrange("(s p) c -> p s c", p=P),
                               [w[:, e, tiles, :].rearrange("p s c -> p (s c)") for w in ff.v], [(None, None, 0, HID)], []))
        fills = Fills(banks, [(("product",), 0), (("bias",), 1), (("router",), 2)])
        biased = sum(1 for piece in pieces if piece[3])
        width = lambda piece: sum(part[3] for part in piece[2])
        norm_of = lambda norm, k: norms[:, norm, k:k + 1]
        parts = [(n, part) for n, piece in enumerate(pieces) for part in piece[2]]
        last_part = [max(i for i, (m, _) in enumerate(parts) if m == n) for n in range(len(pieces))]

        with nc.Block() as block:

            @block.sync
            def _(sp):
                for n, piece in enumerate(pieces):
                    if n >= RING:
                        sp.wait_ge(lo_done, last_part[n - RING] + 1)
                        sp.wait_ge(used, min(n - RING + 1, biased))
                    dst = raw[:, n % RING, 0:width(piece)]
                    if len(piece[0].shape) == 3:
                        dst = dst.rearrange("p (k n) -> p k n", k=piece[0].shape[1])
                    sp.dma_start(dst, piece[0]).then_inc(loaded[n % RING], 16)

            @block.gpsimd
            def _(pool):
                for n, name in enumerate(("ln1_w", "ln1_b", "ln2_w", "ln2_b")):
                    pool.dma_start(norms[:, n, :], dram[name]).then_inc(small_loaded, 16)
                for dst, name in ((wsT, "WsT"), (w2, "W2"), (router, "router")):
                    pool.dma_start(dst[:], dram[name].rearrange("(k p) n -> p k n", p=P)).then_inc(small_loaded, 16)
                pool.dma_start(ff.shares[:], dram["capital_shares"].partition_broadcast(P)).then_inc(small_loaded, 16)
                pool.wait_ge(small_loaded, 8 * 16)

            @block.scalar
            def _(act):
                act.wait_ge(small_loaded, 8 * 16)
                for i, (n, (norm, k, at, size)) in enumerate(parts):
                    act.wait_ge(loaded[n % RING], 16 * (n // RING + 1))
                    scale = 1.0 if norm is None else norm_of(norm, k)
                    nc.scalar.activation(pieces[n][1][0][:, at:at + size], raw[:, n % RING, at:at + size], ACT.Copy, scale=scale).then_inc(
                        hi_done, 1)
                act.wait_ge(*fills.full(0, "product"))
                nc.scalar.activation(product[:].rearrange("p k n -> p (k n)"), fills.data("product")[:], ACT.Copy).then_inc(fills.released("product"), 1)
                act.wait_ge(*fills.read(0, "product"))
                for k in range(CT):
                    nc.scalar.activation(ff.square["WsW2"][0][:, k, :], product[:, k, :], ACT.Copy, scale=norm_of(0, k)).then_inc(hi_done, 1)
                for k in range(CT):
                    nc.scalar.activation(ff.router[0][:, k, :], router[:, k, :], ACT.Copy, scale=norm_of(2, k)).then_inc(hi_done, 1)
                for name, at, size in (("bias", 0, NH + 8), ("router", NH + 8, 8)):
                    act.wait_ge(*fills.full(0, name))
                    nc.scalar.activation(ff.bias[:, at:at + size], fills.data(name)[:, 0:size], ACT.Copy).then_inc(fills.released(name), 1)
                    act.wait_ge(*fills.read(0, name))

            @block.vector
            def _(dve):
                def rest(hi, lo, src, norm, k):
                    nc.vector.scalar_tensor_tensor(out=lo, in0=src, scalar=1.0 if norm is None else norm_of(norm, k),
                                                   in1=hi.bitcast(F32), op0=ALU.mult, op1=ALU.subtract).then_inc(lo_done, 1)

                dve.wait_ge(small_loaded, 8 * 16)
                for k in range(CT):
                    nc.vector.tensor_scalar(offsets[:, k, :], core.ident[:], 0.0, norm_of(3, k), ALU.mult, ALU.add).then_inc(offsets_done, 1)
                for i, (n, (norm, k, at, size)) in enumerate(parts):
                    dve.wait_ge(hi_done, i + 1)
                    hi, lo = (w[:, at:at + size] for w in pieces[n][1])
                    rest(hi, lo, raw[:, n % RING, at:at + size], norm, k)
                for k in range(CT):
                    dve.wait_ge(hi_done, len(parts) + k + 1)
                    rest(*(w[:, k, :] for w in ff.square["WsW2"]), product[:, k, :], 0, k)
                for k in range(CT):
                    dve.wait_ge(hi_done, len(parts) + CT + k + 1)
                    rest(*(w[:, k, :] for w in ff.router), router[:, k, :], 2, k)
                dve.wait_ge(lo_done, len(parts) + 2 * CT)

            @block.tensor
            def _(pe):
                pe.wait_ge(small_loaded, 8 * 16)
                pe.wait_ge(*fills.free(0, "product"))
                for o in range(CT):
                    for k in range(CT):
                        last = nc.tensor.matmul(fills.data("product")[:, o * C:(o + 1) * C], wsT[:, k, o * P:(o + 1) * P], w2[:, k, :],
                                                start=k == 0, stop=k == CT - 1)
                last.then_inc(fills.filled("product"), 1)
                pe.wait_ge(offsets_done, CT)
                pe.wait_ge(*fills.free(0, "router"))
                for k in range(CT):
                    last = nc.tensor.matmul(fills.data("router")[:, 0:8], offsets[:, k, :], router[:, k, :], start=k == 0, stop=k == CT - 1)
                last.then_inc(fills.filled("router"), 1)
                pe.wait_ge(*fills.free(0, "bias"))
                data = fills.data("bias")
                first = True
                for n, piece in enumerate(pieces[:biased]):
                    pe.wait_ge(loaded[n % RING], 16 * (n // RING + 1))
                    norm = piece[2][0][0]
                    for column, at, k in piece[3]:
                        last = nc.tensor.matmul(data[:, column:column + 1], raw[:, n % RING, at:at + P], norm_of(norm + 1, k),
                                                start=first, stop=False, skip_group_check=True)
                        first = False
                    last.then_inc(used, 1)
                pe.wait_ge(*fills.read(0, "product"))
                at = NH + 2 * 2
                for o in range(CT):
                    for k in range(CT):
                        last = nc.tensor.matmul(data[:, at + o:at + o + 1], product[:, k, o * P:(o + 1) * P], norm_of(1, k),
                                                start=False, stop=k == CT - 1, skip_group_check=True)
                last.then_inc(fills.filled("bias"), 1)


TURN_SLOT, R_SLOT, V_SLOT, S_SLOT, ATT_SLOT, TURN2_SLOT = 3, 4, 5, 7, 9, 13
W3_SLOT = 3
AHEAD = 2
SQ_RING = AHEAD + 1


def feed_forward(core, ff, out_dram=None):
    nc, banks, x = core.nc, core.banks, core.x
    with ExitStack() as ctx:
        sem = lambda name: ctx.enter_context(nc.semaphore(f"{name}_{ff.run}"))
        buf = lambda name, shape, dtype=F32: sbuf(nc, ctx, f"{name}_{ff.run}", shape, dtype)
        split = lambda name, shape: [buf(f"{name}_{part}", shape, F32R) for part in ("hi", "lo")]
        stats, mv = buf("f_stats", [P, TT, 6]), buf("f_mv", [P, TT, 2])
        stats2, mv2 = buf("f_stats2", [P, TT, 6]), buf("f_mv2", [P, TT, 2])
        var1, rstd, part, part2, var2, rstd2, both = (
            buf(n, [P, TT]) for n in ("f_var1", "f_rstd", "f_part", "f_part2", "f_var2", "f_rstd2", "f_both"))
        var3, rstd3 = buf("f_var3", [P, TT]), buf("f_rstd3", [P, TT])
        xn, xq, x1 = (buf(n, [P, TT, C]) for n in ("f_xn", "f_xq", "f_x1"))
        hq = xq
        xT, hT, gT = (split(n, [P, CT, T]) for n in ("f_xT", "f_hT", "f_gT"))
        tT = gT
        gate, gate2, g = (buf(n, [P, CT, T]) for n in ("f_gate", "f_gate2", "f_g"))
        r, sq = buf("f_relu", [P, 2, T]), buf("f_square", [P, 2, T])
        h2 = split("f_hidden", [P, SQ_RING, T])
        logits, sig = buf("f_logits", [P, TT, 8]), buf("f_sig", [P, TT, 4])
        bids, win, one, conf = (buf(n, [P, TT, EXPERTS]) for n in ("f_bids", "f_win", "f_one", "f_conf"))
        top, wc, wc_eps, rcp, both_off = (buf(n, [P, TT]) for n in ("f_top", "f_wc", "f_wc_eps", "f_rcp", "f_taken"))
        coef = buf("f_coef", [P, TT, EXPERTS])
        names = ("stats_done", "mv_done", "norm_steps", "xn_done", "xq_done", "xT_hi", "gate_done", "gate2_done", "g_done", "g_hi", "g_lo",
                 "x1_done", "x1_added", "stats2_done", "mv2_done", "norm2_steps", "hq_done", "hT_hi", "h_ready", "t_done", "t_hi", "t_lo",
                 "square_hi", "square_done", "hidden_done", "route_steps", "sig_done", "x_steps")
        s = {n: sem("f_" + n) for n in names}
        stored = sem("stored")
        NORM_STEPS, ROUTE_STEPS = 7, 14
        X_STEPS = EXPERTS * TT

        def front_order():
            yield TURN_SLOT, [("xT", k) for k in range(CT)]
            yield R_SLOT, [("r", k) for k in range(CT)]
            for k in range(CT):
                yield V_SLOT + k, [("v", k)]
            for k in range(CT):
                yield S_SLOT + k, [("s", k)]
            yield ATT_SLOT, [("att", k) for k in range(2)]
            yield TURN2_SLOT, [("hT", k) for k in range(CT)]

        in_slot = dict(front_order())

        def place(heavy, front):
            order, side = [], 0
            names = [("u", 0), ("u", 1), ("route",)] if heavy else []
            for slot in range(NH):
                names += in_slot.get(slot, []) if front else []
            for n in names:
                order.append((n, 6 + side % 2))
                side += 1
            if heavy:
                order += [(("h", t), t % 2) for t in range(NH)]
                order += [(("w3", k), 4 + k) for k in range(2)]
                order += [(("e", e, k), 2 + 2 * e + k) for e in range(2) for k in range(2)]
            return order

        first = Fills(banks, place(False, True))
        loop = Fills(banks, place(True, True), B - 1)
        last_fills = Fills(banks, place(True, False))

        def rounds(eng, front, heavy):
            for slot in range(NH):
                front(first, 0, 0, slot)
            with eng.Fori(0, B - 1) as it:
                heavy(loop, it, it, -1)
                for slot in range(NH):
                    heavy(loop, it, it, slot)
                    front(loop, it, it + 1, slot)
            heavy(last_fills, 0, B - 1, -1)
            for slot in range(NH):
                heavy(last_fills, 0, B - 1, slot)

        with nc.Block() as block:

            if out_dram is not None:
                @block.sync
                def _(sp):
                    with sp.Fori(0, B) as it:
                        sp.wait_ge(s["x_steps"], it * X_STEPS + X_STEPS)
                        sp.dma_start(out_dram[bass.ds(it * T, T), :].rearrange("(t p) c -> p t c", p=P),
                                     cols(x, it * XB, XB).rearrange("p (t c) -> p t c", c=C)).then_inc(stored, 16)
                    sp.wait_ge(stored, 16 * B)

            @block.vector
            def _(dve):
                def two_parts(fl, it, name, hi_sem, count, hi, lo, done=None):
                    dve.wait_ge(hi_sem, count)
                    core.met(dve, "dve")
                    nc.vector.tensor_tensor(lo, fl.data(*name)[:], hi.bitcast(F32), ALU.subtract).then_inc(fl.released(*name), 1)

                def front(fl, it, n, slot):
                    if slot == 0:
                        dve.wait_ge(s["norm_steps"], n * NORM_STEPS)
                        core.met(dve, "dve")
                        for t in range(TT):
                            nc.vector.bn_stats(stats[:, t, :], cols(x, n * XB + t * C, C)).then_inc(s["stats_done"], 1)
                        for t in range(TT):
                            dve.wait_ge(s["stats_done"], n * TT + t + 1)
                            core.met(dve, "dve")
                            nc.vector.bn_aggr(mv[:, t, :], stats[:, t, :]).then_inc(s["mv_done"], 1)
                    if slot == 2:
                        dve.wait_ge(s["norm_steps"], n * NORM_STEPS + NORM_STEPS)
                        core.met(dve, "dve")
                        for t in range(TT):
                            xs = cols(x, n * XB + t * C, C)
                            nc.vector.tensor_scalar(xq[:, t, :], xs, mv[:, t, 0:1], both[:, t:t + 1], ALU.subtract, ALU.mult).then_inc(
                                s["xq_done"], 1)
                        for t in range(TT):
                            xs = cols(x, n * XB + t * C, C)
                            nc.vector.tensor_scalar(xn[:, t, :], xs, mv[:, t, 0:1], rstd[:, t:t + 1], ALU.subtract, ALU.mult).then_inc(
                                s["xn_done"], 1)
                    if slot == TURN_SLOT:
                        for k in range(CT):
                            two_parts(fl, it, ("xT", k), s["xT_hi"], n * CT + k + 1, xT[0][:, k], xT[1][:, k])
                    for k in range(CT):
                        if slot == V_SLOT + k:
                            dve.wait_ge(*fl.full(it, "v", k))
                            dve.wait_ge(s["gate_done"], n * CT + k + 1)
                            core.met(dve, "dve")
                            nc.vector.scalar_tensor_tensor(out=g[:, k], in0=fl.data("v", k)[:], scalar=ff.bias_of("Wv", k), in1=gate[:, k],
                                                           op0=ALU.add, op1=ALU.mult).then_inc(fl.released("v", k), 1)
                        if slot == V_SLOT + k + 1:
                            dve.wait_ge(s["g_hi"], n * CT + k + 1)
                            core.met(dve, "dve")
                            nc.vector.tensor_tensor(gT[1][:, k], g[:, k], gT[0][:, k].bitcast(F32), ALU.subtract).then_inc(s["g_lo"], 1)
                    if slot == ATT_SLOT:
                        dve.wait_ge(s["xn_done"], n * TT + TT)
                        dve.wait_ge(s["x1_added"], n * 2)
                        for k in range(2):
                            dve.wait_ge(*fl.full(it, "att", k))
                            core.met(dve, "dve")
                            nc.vector.tensor_tensor(x1[:, 2 * k:2 * k + 2, :], xn[:, 2 * k:2 * k + 2, :],
                                                    fl.data("att", k)[:].rearrange("p (t c) -> p t c", c=C), ALU.add).then_inc(
                                fl.released("att", k), 1)
                        for t in range(TT):
                            dve.wait_ge(*fl.read(it, "att", t // 2))
                            core.met(dve, "dve")
                            nc.vector.bn_stats(stats2[:, t, :], x1[:, t, :]).then_inc(s["stats2_done"], 1)
                        for t in range(TT):
                            dve.wait_ge(s["stats2_done"], n * TT + t + 1)
                            core.met(dve, "dve")
                            nc.vector.bn_aggr(mv2[:, t, :], stats2[:, t, :]).then_inc(s["mv2_done"], 1)
                    if slot == TURN2_SLOT - 1:
                        dve.wait_ge(s["norm2_steps"], n * 2 + 2)
                        core.met(dve, "dve")
                        for t in range(TT):
                            nc.vector.tensor_scalar(hq[:, t, :], x1[:, t, :], mv2[:, t, 0:1], rstd3[:, t:t + 1], ALU.subtract,
                                                    ALU.mult).then_inc(s["hq_done"], 1)
                    if slot == TURN2_SLOT:
                        for k in range(CT):
                            dve.wait_ge(s["hT_hi"], n * CT + k + 1)
                            core.met(dve, "dve")
                            nc.vector.tensor_tensor(hT[1][:, k], fl.data("hT", k)[:], hT[0][:, k].bitcast(F32), ALU.subtract).then_inc(
                                fl.released("hT", k), 1)

                def add_expert(fl, it, i, e, name, step):
                    dve.wait_ge(s["route_steps"], i * ROUTE_STEPS + ROUTE_STEPS)
                    if step == 0:
                        dve.wait_ge(s["x1_added"], i * 2 + 2)
                    else:
                        dve.wait_ge(s["x_steps"], i * X_STEPS + step * TT)
                    for t in range(TT):
                        bank = (*name, t // 2)
                        dve.wait_ge(*fl.full(it, *bank))
                        core.met(dve, "dve")
                        xs = cols(x, i * XB + t * C, C)
                        nc.vector.scalar_tensor_tensor(out=xs, in0=fl.data(*bank)[:, t % 2 * C:(t % 2 + 1) * C],
                                                       scalar=coef[:, t, e:e + 1], in1=xs, op0=ALU.mult, op1=ALU.add).then_inc(
                            s["x_steps"], 1)
                        if t % 2 == 1:
                            dve.wait_ge(s["x_steps"], i * X_STEPS + step * TT + t + 1)
                            dve.sem_inc(fl.released(*bank), 1)

                def route(fl, it, i):
                    step = 0

                    def after(instruction):
                        nonlocal step
                        step += 1
                        instruction.then_inc(s["route_steps"], 1)
                        dve.wait_ge(s["route_steps"], i * ROUTE_STEPS + step)
                        core.met(dve, "dve")

                    dve.wait_ge(*fl.full(it, "route"))
                    core.met(dve, "dve")
                    nc.vector.tensor_tensor(logits[:], fl.data("route")[:, 0:TT * 8].rearrange("p (t e) -> p t e", e=8),
                                            ff.bias[:, NH + 8:NH + 16].unsqueeze(1).to_broadcast([P, TT, 8]), ALU.add).then_inc(
                        fl.released("route"), 1)
                    dve.wait_ge(s["sig_done"], i + 1)
                    core.met(dve, "dve")
                    v = nc.vector
                    spread = lambda ap: ap.unsqueeze(2).to_broadcast([P, TT, EXPERTS])
                    conf_now = sig[:, :, 0:EXPERTS]
                    after(v.tensor_tensor(bids[:], conf_now, ff.shares[:].unsqueeze(1).to_broadcast([P, TT, EXPERTS]), ALU.mult))
                    after(v.tensor_tensor(bids[:], bids[:], spread(sig[:, :, 3]), ALU.mult))
                    after(v.tensor_tensor(bids[:], bids[:], logits[:, :, 4:7], ALU.add))
                    after(v.tensor_reduce(top[:], bids[:], AX_X, ALU.max))
                    after(v.tensor_tensor(win[:], bids[:], spread(top[:]), ALU.is_ge))
                    after(v.tensor_scalar(one[:, :, 0], win[:, :, 0], 1.0, None, ALU.mult))
                    after(v.tensor_tensor(one[:, :, 1], win[:, :, 1], win[:, :, 0], ALU.is_gt))
                    after(v.tensor_tensor(both_off[:], win[:, :, 0], win[:, :, 1], ALU.max))
                    after(v.tensor_tensor(one[:, :, 2], win[:, :, 2], both_off[:], ALU.is_gt))
                    after(v.tensor_tensor(conf[:], one[:], conf_now, ALU.mult))
                    after(v.tensor_reduce(wc[:], conf[:], AX_X, ALU.add))
                    after(v.tensor_scalar(wc_eps[:], wc[:], 1e-6, None, ALU.add))
                    after(v.reciprocal(rcp[:], wc_eps[:]))
                    after(v.tensor_tensor(coef[:], conf[:], spread(rcp[:]), ALU.mult))

                def heavy(fl, it, i, slot):
                    if slot == -1:
                        for k in range(CT):
                            dve.wait_ge(*fl.full(it, "u", k))
                            dve.wait_ge(s["gate2_done"], i * CT + k + 1)
                            core.met(dve, "dve")
                            nc.vector.scalar_tensor_tensor(out=g[:, k], in0=fl.data("u", k)[:], scalar=ff.bias_of("W1", k), in1=gate2[:, k],
                                                           op0=ALU.add, op1=ALU.mult).then_inc(fl.released("u", k), 1)
                        route(fl, it, i)
                    else:
                        dve.wait_ge(s["square_hi"], i * NH + slot + 1)
                        dve.wait_ge(s["square_done"], i * NH + slot + 1)
                        core.met(dve, "dve")
                        nc.vector.tensor_tensor(h2[1][:, slot % SQ_RING], sq[:, slot % 2], h2[0][:, slot % SQ_RING].bitcast(F32),
                                                ALU.subtract).then_inc(s["hidden_done"], 1)
                    if slot in (0, 1):
                        k = slot
                        dve.wait_ge(s["t_hi"], i * CT + k + 1)
                        core.met(dve, "dve")
                        nc.vector.tensor_tensor(tT[1][:, k], g[:, k], tT[0][:, k].bitcast(F32), ALU.subtract).then_inc(s["t_lo"], 1)
                    if slot == W3_SLOT + 1:
                        add_expert(fl, it, i, 2, ("w3",), 0)
                    if slot == HT:
                        add_expert(fl, it, i, 0, ("e", 0), 1)
                    if slot == NH - 1:
                        add_expert(fl, it, i, 1, ("e", 1), 2)

                rounds(dve, front, heavy)

            @block.gpsimd
            def _(pool):
                def front(fl, it, n, slot):
                    g_ = nc.gpsimd
                    if slot == 0:
                        step = 0

                        def after(instruction):
                            nonlocal step
                            step += 1
                            instruction.then_inc(s["norm_steps"], 1)
                            pool.wait_ge(s["norm_steps"], n * NORM_STEPS + step)
                            core.met(pool, "pool")

                        pool.wait_ge(s["mv_done"], n * TT + TT)
                        pool.wait_ge(s["xn_done"], n * TT)
                        core.met(pool, "pool")
                        after(g_.tensor_scalar(var1[:], mv[:, :, 1], EPS, None, ALU.add))
                        after(g_.tensor_tensor(rstd[:], var1[:], core.neg_half[:], ALU.pow))
                        after(g_.tensor_tensor(part[:], mv[:, :, 1], rstd[:], ALU.mult))
                        after(g_.tensor_tensor(part2[:], part[:], rstd[:], ALU.mult))
                        after(g_.tensor_scalar(var2[:], part2[:], EPS, None, ALU.add))
                        after(g_.tensor_tensor(rstd2[:], var2[:], core.neg_half[:], ALU.pow))
                        after(g_.tensor_tensor(both[:], rstd[:], rstd2[:], ALU.mult))
                    if slot == ATT_SLOT + 1:
                        pool.wait_ge(s["mv2_done"], n * TT + TT)
                        pool.wait_ge(s["hq_done"], n * TT)
                        core.met(pool, "pool")
                        g_.tensor_scalar(var3[:], mv2[:, :, 1], EPS, None, ALU.add).then_inc(s["norm2_steps"], 1)
                        pool.wait_ge(s["norm2_steps"], n * 2 + 1)
                        core.met(pool, "pool")
                        g_.tensor_tensor(rstd3[:], var3[:], core.neg_half[:], ALU.pow).then_inc(s["norm2_steps"], 1)
                        pool.wait_ge(s["xn_done"], n * TT + TT)
                        for k in range(2):
                            pool.wait_ge(*fl.read(it, "att", k))
                            core.met(pool, "pool")
                            xs = cols(x, n * XB + k * 512, 512)
                            g_.tensor_tensor(xs, xs, x1[:, 2 * k:2 * k + 2, :].rearrange("p t c -> p (t c)"), ALU.add).then_inc(s["x1_added"], 1)

                def square(fl, it, i, t):
                    pool.wait_ge(*fl.read(it, "h", t))
                    if t >= 2:
                        pool.wait_ge(s["hidden_done"], i * NH + t - 1)
                    core.met(pool, "pool")
                    nc.gpsimd.tensor_tensor(sq[:, t % 2], r[:, t % 2], r[:, t % 2], ALU.mult).then_inc(s["square_done"], 1)

                def heavy(fl, it, i, slot):
                    for t in range(AHEAD) if slot == -1 else [slot + AHEAD]:
                        if t < NH:
                            square(fl, it, i, t)

                rounds(pool, front, heavy)

            @block.scalar
            def _(act):
                def first_part(fl, it, name, dst, done):
                    act.wait_ge(*fl.full(it, *name))
                    nc.scalar.activation(dst, fl.data(*name)[:], ACT.Copy).then_inc(done, 1)

                def gated(fl, it, name, dst, bias, done):
                    act.wait_ge(*fl.full(it, *name))
                    nc.scalar.activation(dst, fl.data(*name)[:], ACT.Sigmoid, bias=bias).then_inc(fl.released(*name), 1)
                    act.wait_ge(*fl.read(it, *name))
                    act.sem_inc(done, 1)

                def front(fl, it, n, slot):
                    if slot == TURN_SLOT:
                        for k in range(CT):
                            first_part(fl, it, ("xT", k), xT[0][:, k], s["xT_hi"])
                    if slot == R_SLOT:
                        for k in range(CT):
                            gated(fl, it, ("r", k), gate[:, k], ff.bias_of("Wr", k), s["gate_done"])
                    for k in range(CT):
                        if slot == V_SLOT + k:
                            act.wait_ge(*fl.read(it, "v", k))
                            nc.scalar.activation(gT[0][:, k], g[:, k], ACT.Copy).then_inc(s["g_hi"], 1)
                        if slot == S_SLOT + k:
                            gated(fl, it, ("s", k), gate2[:, k], ff.bias_of("WsW2", k), s["gate2_done"])
                    if slot == TURN2_SLOT:
                        for k in range(CT):
                            first_part(fl, it, ("hT", k), hT[0][:, k], s["hT_hi"])

                def hidden(fl, it, i, t):
                    if t >= 2:
                        act.wait_ge(s["square_done"], i * NH + t - 1)
                    act.wait_ge(*fl.full(it, "h", t))
                    nc.scalar.activation(r[:, t % 2], fl.data("h", t)[:], ACT.Relu, bias=ff.bias[:, t:t + 1]).then_inc(fl.released("h", t), 1)
                    act.wait_ge(*fl.read(it, "h", t))
                    nc.scalar.activation(h2[0][:, t % SQ_RING], r[:, t % 2], ACT.Square).then_inc(s["square_hi"], 1)

                def heavy(fl, it, i, slot):
                    if slot == -1:
                        for k in range(CT):
                            hidden(fl, it, i, k)
                            act.wait_ge(*fl.read(it, "u", k))
                            nc.scalar.activation(tT[0][:, k], g[:, k], ACT.Copy).then_inc(s["t_hi"], 1)
                        act.wait_ge(*fl.read(it, "route"))
                        nc.scalar.activation(sig[:], logits[:, :, 0:4], ACT.Sigmoid).then_inc(s["sig_done"], 1)
                    elif slot + AHEAD < NH:
                        hidden(fl, it, i, slot + AHEAD)

                rounds(act, front, heavy)

            @block.tensor
            def _(pe):
                def begin(fl, it, *name):
                    pe.wait_ge(*fl.free(it, *name))
                    core.met(pe, "pe")
                    return fl.data(*name)

                PASSES = ((0, 0), (0, 1), (1, 0))

                def to_features(fl, it, name, weight, src, o):
                    data = begin(fl, it, *name)
                    steps = [(k, a, b) for k in range(CT) for a, b in PASSES]
                    for n, (k, a, b) in enumerate(steps):
                        last = nc.tensor.matmul(data[:], weight[a](k, o), src[b][:, k], start=n == 0, stop=n == len(steps) - 1)
                    last.then_inc(fl.filled(*name), 1)

                square = lambda name: [lambda k, o, w=w: w[:, k, o * P:(o + 1) * P] for w in ff.square[name]]

                def to_tokens(fl, it, name, src, weight):
                    steps = [(k, a, b) for k in range(CT) for a, b in PASSES]
                    for bank in range(2):
                        data = begin(fl, it, name, bank)
                        for t in (2 * bank, 2 * bank + 1):
                            for n, (k, a, b) in enumerate(steps):
                                last = nc.tensor.matmul(data[:, t % 2 * C:(t % 2 + 1) * C], src[a][:, k, t * P:(t + 1) * P],
                                                        ff.square[weight][b][:, k, :], start=n == 0, stop=n == len(steps) - 1)
                        last.then_inc(fl.filled(name, bank), 1)

                def turn(fl, it, name, src):
                    for k in range(CT):
                        data = begin(fl, it, name, k)
                        for t in range(TT):
                            last = nc.tensor.transpose(data[:, t * P:(t + 1) * P], src[:, t, k * P:(k + 1) * P], core.ident[:])
                        last.then_inc(fl.filled(name, k), 1)

                def front(fl, it, n, slot):
                    if slot == TURN_SLOT:
                        pe.wait_ge(s["xq_done"], n * TT + TT)
                        turn(fl, it, "xT", xq)
                    if slot == R_SLOT:
                        for k in range(CT):
                            pe.wait_ge(*fl.read(it, "xT", k))
                        for k in range(CT):
                            to_features(fl, it, ("r", k), square("Wr"), xT, k)
                    for k in range(CT):
                        if slot == V_SLOT + k:
                            to_features(fl, it, ("v", k), square("Wv"), xT, k)
                        if slot == S_SLOT + k:
                            to_features(fl, it, ("s", k), square("WsW2"), xT, k)
                    if slot == ATT_SLOT:
                        pe.wait_ge(s["g_lo"], n * CT + CT)
                        to_tokens(fl, it, "att", gT, "Wo")
                    if slot == TURN2_SLOT:
                        pe.wait_ge(s["hq_done"], n * TT + TT)
                        turn(fl, it, "hT", hq)
                        for k in range(CT):
                            pe.wait_ge(*fl.read(it, "hT", k))
                        pe.sem_inc(s["h_ready"], 1)

                def hidden(fl, it, t):
                    e, c = t // HT, t % HT
                    to_features(fl, it, ("h", t), [lambda k, o, w=w: w[:, e, k, c * P:(c + 1) * P] for w in ff.k], hT, 0)

                def second(fl, it, i, t):
                    e, c = t // HT, t % HT
                    pe.wait_ge(s["hidden_done"], i * NH + t + 1)
                    if c == 0:
                        for bank in range(2):
                            begin(fl, it, "e", e, bank)
                    core.met(pe, "pe")
                    for tok in range(TT):
                        for n, (a, b) in enumerate(PASSES):
                            last = nc.tensor.matmul(
                                fl.data("e", e, tok // 2)[:, tok % 2 * C:(tok % 2 + 1) * C], h2[a][:, t % SQ_RING, tok * P:(tok + 1) * P],
                                ff.v[b][:, e, c, :], start=c == 0 and n == 0 and tok % 2 == 0, stop=c == HT - 1 and n == 2,
                                skip_group_check=True)
                        if c == HT - 1 and tok % 2 == 1:
                            last.then_inc(fl.filled("e", e, tok // 2), 1)

                def heavy(fl, it, i, slot):
                    if slot == -1:
                        for k in range(CT):
                            hidden(fl, it, k)
                            to_features(fl, it, ("u", k), square("W1"), hT, k)
                        data = begin(fl, it, "route")
                        steps = [(k, a, b) for k in range(CT) for a, b in PASSES]
                        for t in range(TT):
                            for n, (k, a, b) in enumerate(steps):
                                last = nc.tensor.matmul(data[:, t * 8:(t + 1) * 8], hT[a][:, k, t * P:(t + 1) * P], ff.router[b][:, k, :],
                                                        start=n == 0, stop=n == len(steps) - 1)
                        last.then_inc(fl.filled("route"), 1)
                        return
                    if slot + AHEAD < NH:
                        hidden(fl, it, slot + AHEAD)
                    second(fl, it, i, slot)
                    if slot == W3_SLOT:
                        pe.wait_ge(s["t_lo"], i * CT + CT)
                        to_tokens(fl, it, "w3", tT, "W3")

                rounds(pe, front, heavy)


NQUADS = HB // QUAD
PAIRS_B = HB // 2
PAIRS_T = PAIRS_B // CT
SLOTS_B = HB + 5
XT_SLOT, QK0_SLOT, QK1_SLOT, V0_SLOT, SEL0_SLOT = 3, 6, 16, 18, 20
SCORES = ((0, 3, 0), (1, 2, 0), (1, 0, 3 * P), (2, 1, 0))
SCORE_COLS = {3: 0, 2: 4 * P, 0: 7 * P, 1: 8 * P}
TURNED = ((0, 0, 0), (1, 1, 0), (1, 3, 3 * P), (2, 2, 0))
TURNED_COLS = {0: 0, 1: 4 * P, 3: 7 * P, 2: 8 * P}
HEAD_COLS = 10 * P
BANK_COLS = ((0, 4 * P), (4 * P, 4 * P), (8 * P, 2 * P))


def layer_b(core, dram):
    nc, banks, x = core.nc, core.banks, core.x
    with ExitStack() as ctx:
        sem = lambda name: ctx.enter_context(nc.semaphore(name))
        buf = lambda name, shape, dtype=F32: sbuf(nc, ctx, name, shape, dtype)
        wq, wk, wv, wo = (buf(n, [P, CT, C]) for n in ("wq_b", "wk_b", "wv_b", "wo_b"))
        cos, sin = buf("cos", [P, T]), buf("sin", [P, T])
        select = buf("select", [P, 2, 2, PAIRS_T, P], F32R)
        ident16, causal16 = buf("ident16", [P, P], BF16), buf("causal16", [P, P], BF16)
        stats, mv, var1, rstd = buf("b_stats", [P, TT, 6]), buf("b_mv", [P, TT, 2]), buf("b_var", [P, TT]), buf("b_rstd", [P, TT])
        xn, xnT = buf("b_xn", [P, TT, C]), buf("b_xnT", [P, CT, T])
        straight, swapped, turned, rotated = (buf(n, [P, 2, T]) for n in ("b_straight", "b_swapped", "b_turned", "b_rotated"))
        qk = [[buf(f"b_{side}_{part}", [P, CT, T], F32R) for part in ("hi", "lo")] for side in ("q", "k")]
        stacked = [buf(f"b_{side}_stacked", [P, 2, T], F32R) for side in ("q", "k")]
        v = buf("b_v", [P, TT, HB, 2 * DB])
        probs = buf("b_probs", [P, 2, HEAD_COLS])
        probsT = buf("b_probsT", [P, 2 * QUAD, HEAD_COLS])
        neg_max = buf("b_neg_max", [P, 2, TT])
        oT = buf("b_oT", [P, 2, T])
        rcp, att, attT = buf("b_rcp", [P, TT, QUAD]), buf("b_att", [P, TT, C]), buf("b_attT", [P, CT, T])
        names = ("loaded", "consts_done", "ones_done", "stats_done", "mv_done", "var_done", "rstd_done", "xn_done", "swap_done", "turn_done", "rot_done",
                 "hi_done", "lo_done", "max_done", "rcp_done")
        s = {n: sem("b_" + n) for n in names}

        def fill_order(heavy, front):
            order, side = [], 0

            def add(name, b=None):
                nonlocal side
                if b is None:
                    b, side = 6 + side % 2, side + 1
                order.append((name, b))

            for slot in range(SLOTS_B):
                if heavy and slot < HB:
                    for b in range(3):
                        add(("s", slot, b), b)
                if heavy and 1 <= slot <= HB:
                    for b in range(3):
                        add(("t", slot - 1, b), 3 + b % 2)
                if heavy and slot % 2 == 0 and slot // 2 + 1 < PAIRS_B:
                    for side_ in range(2):
                        add(("sel", side_, slot // 2 + 1))
                for quad in range(NQUADS):
                    if heavy and slot == 4 * quad + 5:
                        add(("pv", quad), 5)
                    if heavy and slot == 4 * quad + 6:
                        add(("o", quad), 5)
                if heavy and slot == HB + 3:
                    for k in range(CT):
                        add(("attT", k), 3 + k)
                if heavy and slot == HB + 4:
                    for k in range(2):
                        add(("out", k), 3 + k)
                if front and slot == XT_SLOT:
                    for k in range(CT):
                        add(("xT", k))
                for f, at in ((0, QK0_SLOT), (1, QK1_SLOT)):
                    if front and slot == at:
                        for side_ in range(2):
                            add(("qk", side_, f))
                if front and slot == V0_SLOT:
                    for k in range(2):
                        add(("v", k))
                if front and slot == SEL0_SLOT:
                    for side_ in range(2):
                        add(("sel", side_, 0))
            return order

        with ExitStack() as setup:
            raw = sbuf(nc, setup, "b_raw", [P, 16 * P])
            raw_mask = sbuf(nc, setup, "b_raw_mask", [P, P])
            with nc.Block() as block:

                @block.sync
                def _(sp):
                    for dst, name in ((wq, "WqT"), (wk, "WkT"), (wv, "WvT"), (wo, "WoT")):
                        sp.dma_start(dst[:], dram[name].rearrange("(k p) n -> p k n", p=P)).then_inc(s["loaded"], 16)
                    for dst, name in ((cos, "cos"), (sin, "sin"), (raw, "select"), (raw_mask, "causal")):
                        sp.dma_start(dst[:], dram[name]).then_inc(s["loaded"], 16)
                    sp.wait_ge(s["loaded"], 8 * 16)

                @block.scalar
                def _(act):
                    act.wait_ge(s["loaded"], 8 * 16)
                    nc.scalar.activation(select[:].rearrange("p a b c d -> p (a b c d)"), raw[:], ACT.Copy).then_inc(s["consts_done"], 1)
                    nc.scalar.activation(ident16[:], core.ident[:], ACT.Copy).then_inc(s["consts_done"], 1)
                    nc.scalar.activation(causal16[:], raw_mask[:], ACT.Copy).then_inc(s["consts_done"], 1)
                    act.wait_ge(s["consts_done"], 3)

                @block.vector
                def _(dve):
                    nc.vector.memset(v[:, :, :, DB:], 0.0).then_inc(s["ones_done"], 1)
                    dve.wait_ge(s["ones_done"], 1)
                    nc.vector.memset(v[:, :, :, DB:DB + 1], 1.0).then_inc(s["ones_done"], 1)
                    dve.wait_ge(s["ones_done"], 2)

        first = Fills(banks, fill_order(False, True))
        loop = Fills(banks, fill_order(True, True), B - 1)
        last_fills = Fills(banks, fill_order(True, False))

        def rounds(eng, front, heavy):
            for slot in range(SLOTS_B):
                front(first, 0, 0, slot)
            with eng.Fori(0, B - 1) as it:
                for slot in range(SLOTS_B):
                    heavy(loop, it, it, slot)
                    front(loop, it, it + 1, slot)
            for slot in range(SLOTS_B):
                heavy(last_fills, 0, B - 1, slot)

        with nc.Block() as block:

            @block.vector
            def _(dve):
                def ready(*waits):
                    for wait in waits:
                        dve.wait_ge(*wait)
                    core.met(dve, "dve")

                def front(fl, it, n, slot):
                    if slot == 0:
                        ready((s["xn_done"], n * TT))
                        for t in range(TT):
                            nc.vector.bn_stats(stats[:, t, :], cols(x, n * XB + t * C, C)).then_inc(s["stats_done"], 1)
                        for t in range(TT):
                            ready((s["stats_done"], n * TT + t + 1))
                            nc.vector.bn_aggr(mv[:, t, :], stats[:, t, :]).then_inc(s["mv_done"], 1)
                    if slot == 2:
                        ready((s["rstd_done"], n + 1))
                        for t in range(TT):
                            nc.vector.tensor_scalar(xn[:, t, :], cols(x, n * XB + t * C, C), mv[:, t, 0:1], rstd[:, t:t + 1],
                                                    ALU.subtract, ALU.mult).then_inc(s["xn_done"], 1)
                    for f, at in ((0, QK0_SLOT), (1, QK1_SLOT)):
                        if slot == at:
                            for side in range(2):
                                ready(fl.full(it, "qk", side, f), (s["rot_done"], n * 4 + f * 2))
                                nc.vector.tensor_tensor(straight[:, side], fl.data("qk", side, f)[:], cos[:], ALU.mult)
                                nc.vector.stream_shuffle(swapped[:, side], fl.data("qk", side, f)[:], [i ^ 1 for i in range(32)]).then_inc(
                                    fl.released("qk", side, f), 1)

                def heavy(fl, it, i, slot):
                    if slot < HB:
                        for place, (b, t, at) in enumerate(SCORES):
                            ready(fl.full(it, "s", slot, b))
                            nc.vector.tensor_reduce(neg_max[:, slot % 2, place:place + 1], fl.data("s", slot, b)[:, at:at + (t + 1) * P],
                                                    AX_X, ALU.max, negate=True).then_inc(s["max_done"], 1)
                    if 1 <= slot <= HB:
                        for b in (0, 2):
                            ready(fl.full(it, "t", slot - 1, b))
                            at, size = BANK_COLS[b]
                            nc.vector.tensor_scalar(probsT[:, (slot - 1) % (2 * QUAD), at:at + size], fl.data("t", slot - 1, b)[:, 0:size],
                                                    1.0, None, ALU.mult).then_inc(fl.released("t", slot - 1, b), 1)
                    for quad in range(NQUADS):
                        if slot == 4 * quad + 6:
                            ready(fl.full(it, "o", quad))
                            o = fl.data("o", quad)[:].rearrange("p (t h d) -> p t h d", t=TT, h=QUAD)
                            nc.vector.reciprocal(rcp[:], o[:, :, :, DB]).then_inc(s["rcp_done"], 1)
                            ready((s["rcp_done"], i * NQUADS + quad + 1))
                            nc.vector.tensor_tensor(
                                att[:, :, quad * QUAD * DB:(quad + 1) * QUAD * DB].rearrange("p t (h d) -> p t h d", h=QUAD),
                                o[:, :, :, 0:DB], rcp[:].unsqueeze(3).to_broadcast([P, TT, QUAD, DB]), ALU.mult).then_inc(
                                fl.released("o", quad), 1)
                    if slot == HB + 4:
                        for k in range(2):
                            ready(fl.full(it, "out", k))
                            xs = cols(x, i * XB + k * 512, 512)
                            nc.vector.tensor_tensor(xs, xs, fl.data("out", k)[:], ALU.add).then_inc(fl.released("out", k), 1)

                rounds(dve, front, heavy)

            @block.gpsimd
            def _(pool):
                def ready(*waits):
                    for wait in waits:
                        pool.wait_ge(*wait)
                    core.met(pool, "pool")

                def front(fl, it, n, slot):
                    g = nc.gpsimd
                    if slot == 1:
                        ready((s["mv_done"], n * TT + TT), (s["xn_done"], n * TT))
                        g.tensor_scalar(var1[:], mv[:, :, 1], EPS, None, ALU.add).then_inc(s["var_done"], 1)
                        ready((s["var_done"], n + 1))
                        g.tensor_tensor(rstd[:], var1[:], core.neg_half[:], ALU.pow).then_inc(s["rstd_done"], 1)
                    for f, at in ((0, QK0_SLOT), (1, QK1_SLOT)):
                        if slot == at:
                            for side in range(2):
                                step = n * 4 + f * 2 + side + 1
                                ready(fl.read(it, "qk", side, f), (s["lo_done"], n * 4 + f * 2))
                                g.tensor_tensor(turned[:, side], swapped[:, side], sin[:], ALU.mult).then_inc(s["turn_done"], 1)
                                ready((s["turn_done"], step))
                                g.tensor_tensor(rotated[:, side], straight[:, side], turned[:, side], ALU.add).then_inc(s["rot_done"], 1)
                            for side in range(2):
                                ready((s["hi_done"], n * 4 + f * 2 + side + 1))
                                hi, lo = qk[side]
                                g.tensor_tensor(lo[:, f], rotated[:, side], hi[:, f].bitcast(F32), ALU.subtract).then_inc(s["lo_done"], 1)

                def heavy(fl, it, i, slot):
                    pass

                rounds(pool, front, heavy)

            @block.scalar
            def _(act):
                def copy(fl, it, dst, name, size=T):
                    act.wait_ge(*fl.full(it, *name))
                    nc.scalar.activation(dst, fl.data(*name)[:, 0:size], ACT.Copy).then_inc(fl.released(*name), 1)

                def select_copies(fl, it, pair):
                    for side in range(2):
                        copy(fl, it, stacked[side][:, pair % 2], ("sel", side, pair))

                def front(fl, it, n, slot):
                    if slot == XT_SLOT:
                        for k in range(CT):
                            copy(fl, it, xnT[:, k], ("xT", k))
                    for f, at in ((0, QK0_SLOT + 2), (1, QK1_SLOT + 2)):
                        if slot == at:
                            for side in range(2):
                                act.wait_ge(s["rot_done"], n * 4 + f * 2 + side + 1)
                                nc.scalar.activation(qk[side][0][:, f], rotated[:, side], ACT.Copy).then_inc(s["hi_done"], 1)
                    if slot == V0_SLOT:
                        for k in range(2):
                            act.wait_ge(*fl.full(it, "v", k))
                            for t in range(2):
                                done = nc.scalar.activation(v[:, 2 * k + t, :, 0:DB],
                                                            fl.data("v", k)[:, t * C:(t + 1) * C].rearrange("p (h d) -> p h d", d=DB), ACT.Copy)
                            done.then_inc(fl.released("v", k), 1)
                    if slot == SEL0_SLOT:
                        select_copies(fl, it, 0)

                def heavy(fl, it, i, slot):
                    if slot < HB:
                        h = slot
                        for place, (b, t, at) in enumerate(SCORES):
                            size, to = (t + 1) * P, SCORE_COLS[t]
                            act.wait_ge(s["max_done"], i * HB * TT + h * TT + (1, 3, 3, 4)[place])
                            done = nc.scalar.activation(probs[:, h % 2, to:to + size], fl.data("s", h, b)[:, at:at + size], ACT.Exp,
                                                        bias=neg_max[:, h % 2, place:place + 1])
                            if place != 1:
                                done.then_inc(fl.released("s", h, b), 1)
                    if 1 <= slot <= HB:
                        at, size = BANK_COLS[1]
                        copy(fl, it, probsT[:, (slot - 1) % (2 * QUAD), at:at + size], ("t", slot - 1, 1), size)
                    if slot % 2 == 0 and slot // 2 + 1 < PAIRS_B:
                        select_copies(fl, it, slot // 2 + 1)
                    for quad in range(NQUADS):
                        if slot == 4 * quad + 5:
                            copy(fl, it, oT[:, quad % 2], ("pv", quad))
                    if slot == HB + 3:
                        for k in range(CT):
                            copy(fl, it, attT[:, k], ("attT", k))

                rounds(act, front, heavy)

            @block.tensor
            def _(pe):
                def begin(fl, it, *name):
                    pe.wait_ge(*fl.free(it, *name))
                    core.met(pe, "pe")
                    return fl.data(*name)

                def stack(fl, it, pair):
                    f, j = pair // PAIRS_T, pair % PAIRS_T
                    for side in range(2):
                        data = begin(fl, it, "sel", side, pair)
                        for part in range(2):
                            last = nc.tensor.matmul(data[:], select[:, side, part, j, :], qk[side][part][:, f], start=part == 0, stop=part == 1)
                        last.then_inc(fl.filled("sel", side, pair), 1)

                def front(fl, it, n, slot):
                    if slot == XT_SLOT:
                        pe.wait_ge(s["xn_done"], n * TT + TT)
                        for k in range(CT):
                            data = begin(fl, it, "xT", k)
                            for t in range(TT):
                                last = nc.tensor.transpose(data[:, t * P:(t + 1) * P], xn[:, t, k * P:(k + 1) * P], core.ident[:])
                            last.then_inc(fl.filled("xT", k), 1)
                    for f, at in ((0, QK0_SLOT), (1, QK1_SLOT)):
                        if slot == at:
                            for k in range(CT):
                                pe.wait_ge(*fl.read(it, "xT", k))
                            for side, weight in enumerate((wq, wk)):
                                data = begin(fl, it, "qk", side, f)
                                for k in range(CT):
                                    last = nc.tensor.matmul(data[:], weight[:, k, f * P:(f + 1) * P], xnT[:, k], start=k == 0, stop=k == CT - 1)
                                last.then_inc(fl.filled("qk", side, f), 1)
                    if slot == V0_SLOT:
                        for b in range(2):
                            data = begin(fl, it, "v", b)
                            for t in (2 * b, 2 * b + 1):
                                for k in range(CT):
                                    last = nc.tensor.matmul(data[:, t % 2 * C:(t % 2 + 1) * C], xnT[:, k, t * P:(t + 1) * P], wv[:, k, :],
                                                            start=k == 0, stop=k == CT - 1)
                            last.then_inc(fl.filled("v", b), 1)
                    if slot == SEL0_SLOT:
                        pe.wait_ge(s["lo_done"], n * 4 + 2)
                        stack(fl, it, 0)
                        for side in range(2):
                            pe.wait_ge(*fl.read(it, "sel", side, 0))
                        core.met(pe, "pe")

                def heavy(fl, it, i, slot):
                    if slot < HB:
                        h, pair = slot, slot // 2
                        rows = slice(h % 2 * 64, h % 2 * 64 + 64)
                        if h % 2 == 0 and pair:
                            for side in range(2):
                                pe.wait_ge(*fl.read(it, "sel", side, pair))
                        for place, (b, t, at) in enumerate(SCORES):
                            data = fl.data("s", h, b) if place == 2 else begin(fl, it, "s", h, b)
                            nc.tensor.matmul(data[:, at:at + (t + 1) * P], stacked[0][rows, pair % 2, t * P:(t + 1) * P],
                                             stacked[1][rows, pair % 2, 0:(t + 1) * P], start=place != 2, stop=False, skip_group_check=True)
                            last = nc.tensor.matmul(data[:, at + t * P:at + (t + 1) * P], ident16[:], causal16[:], start=False, stop=True,
                                                    skip_group_check=True)
                            if place != 1:
                                last.then_inc(fl.filled("s", h, b), 1)
                    if 1 <= slot <= HB:
                        h = slot - 1
                        for b in range(3):
                            pe.wait_ge(*fl.read(it, "s", h, b))
                        for b in range(3):
                            data = begin(fl, it, "t", h, b)
                            for bank, kt, at in TURNED:
                                if bank == b:
                                    for q in range(kt, TT):
                                        src = SCORE_COLS[q] + kt * P
                                        last = nc.tensor.transpose(data[:, at + (q - kt) * P:at + (q - kt + 1) * P],
                                                                   probs[:, h % 2, src:src + P], core.ident[:])
                            last.then_inc(fl.filled("t", h, b), 1)
                    if slot % 2 == 0 and slot // 2 + 1 < PAIRS_B:
                        if slot // 2 + 1 == PAIRS_T:
                            pe.wait_ge(s["lo_done"], i * 4 + 4)
                        stack(fl, it, slot // 2 + 1)
                    for quad in range(NQUADS):
                        if slot == 4 * quad + 5:
                            heads = range(quad * QUAD, (quad + 1) * QUAD)
                            for b in (1, 2):
                                pe.wait_ge(*fl.read(it, "t", heads[-1], b))
                            data = begin(fl, it, "pv", quad)
                            for kt in range(TT):
                                at, size = TURNED_COLS[kt], T - kt * P
                                for n, h in enumerate(heads):
                                    last = nc.tensor.matmul(data[n * 32:(n + 1) * 32, kt * P:], v[:, kt, h, :],
                                                            probsT[:, h % (2 * QUAD), at:at + size], start=kt == 0, stop=kt == TT - 1,
                                                            skip_group_check=True)
                            last.then_inc(fl.filled("pv", quad), 1)
                        if slot == 4 * quad + 6:
                            pe.wait_ge(*fl.read(it, "pv", quad))
                            data = begin(fl, it, "o", quad)
                            for t in range(TT):
                                last = nc.tensor.transpose(data[:, t * P:(t + 1) * P], oT[:, quad % 2, t * P:(t + 1) * P], core.ident[:])
                            last.then_inc(fl.filled("o", quad), 1)
                    if slot == HB + 3:
                        pe.wait_ge(*fl.read(it, "o", NQUADS - 1))
                        for k in range(CT):
                            data = begin(fl, it, "attT", k)
                            for t in range(TT):
                                last = nc.tensor.transpose(data[:, t * P:(t + 1) * P], att[:, t, k * P:(k + 1) * P], core.ident[:])
                            last.then_inc(fl.filled("attT", k), 1)
                    if slot == HB + 4:
                        for k in range(CT):
                            pe.wait_ge(*fl.read(it, "attT", k))
                        for b in range(2):
                            data = begin(fl, it, "out", b)
                            for t in (2 * b, 2 * b + 1):
                                for k in range(CT):
                                    last = nc.tensor.matmul(data[:, t % 2 * C:(t % 2 + 1) * C], attT[:, k, t * P:(t + 1) * P], wo[:, k, :],
                                                            start=k == 0, stop=k == CT - 1)
                            last.then_inc(fl.filled("out", b), 1)

                rounds(pe, front, heavy)


def program(nc, dram, out_dram):
    with ExitStack() as ctx:
        core = Core(nc, ctx)
        with ExitStack() as layer:
            la = AttentionA(nc, layer)
            core.ql, core.kl = (sbuf(nc, layer, n, [P, NP, B * M]) for n in ("ql", "kl"))
            core.a = sbuf(nc, layer, "a", [P, B, NP, M])
            with ExitStack() as part:
                core.i64 = sbuf(nc, part, "i64", [P, M])
                core.aT = sbuf(nc, part, "aT", [P, B, NP, M])
                core.inv_bound = sbuf(nc, part, "inv_bound", [P, 1])
                landmarks(core, la, dram)
                pseudo_inverse(core, la, dram)
            layer_a(core, la)
        with ExitStack() as layer:
            ff = FeedForward(nc, layer, 0)
            prepare_ff(core, ff, dram)
            feed_forward(core, ff)
        layer_b(core, dram)
        with ExitStack() as layer:
            ff = FeedForward(nc, layer, 1)
            prepare_ff(core, ff, dram)
            feed_forward(core, ff, out_dram)


def shape_constants():
    ident = np.eye(P, dtype=np.float32)
    shifted = np.zeros((P, BAND + TAPS - 1), np.float32)
    shifted[np.arange(P), np.arange(P) + TAPS - 1] = 1
    feature = np.arange(P) % DB
    frequency = np.float32(1) / np.float32(10000) ** (np.arange(0, DB, 2, dtype=np.float32) / np.float32(DB))
    angle = np.arange(T, dtype=np.float32)[None, :] * frequency[feature // 2][:, None]
    sign = np.where(feature % 2 == 0, np.float32(-1), np.float32(1))[:, None]
    select = np.zeros((P, 2, 2, PAIRS_T, P), np.float32)
    for side, parts in enumerate(((0, 1, 0, 1), (0, 0, 1, 1))):
        for j in range(PAIRS_T):
            for head in range(2):
                for copy, part in enumerate(parts):
                    for d in range(DB):
                        select[(2 * j + head) * DB + d, side, part, j, head * 64 + copy * DB + d] = DB ** -0.5 if side == 0 else 1
    return {
        "ident": ident,
        "i64": np.concatenate([np.eye(M, dtype=np.float32)] * 2),
        "shifted_ident": shifted,
        "cos": np.cos(angle).astype(np.float32),
        "sin": (np.sin(angle) * sign).astype(np.float32),
        "select": select.reshape(P, -1),
        "causal": np.where(np.arange(P)[None, :] > np.arange(P)[:, None], np.float32(-1e30), np.float32(0)),
    }


def kernel(**inputs):
    import concourse.bacc as bacc
    from concourse.bass_utils import run_bass_kernel_spmd

    a = {n[len("L0_attn_a_"):]: np.asarray(v) for n, v in inputs.items() if n.startswith("L0_attn_a_")}
    b = {n[len("L0_attn_b_"):]: np.asarray(v) for n, v in inputs.items() if n.startswith("L0_attn_b_")}
    f = {n[len("L0_ffn_"):]: np.asarray(v) for n, v in inputs.items() if n.startswith("L0_ffn_")}

    by_partition = lambda v: v.reshape(CT, P).T
    router = np.concatenate(
        [f["conf_rwkv"].T, f["conf_trans"][:, None], f["w_diff"][:, None], f["W_aff"], np.zeros((C, 1), np.float32)], axis=1)
    arrays = {
        "x": a["x"].reshape(B * T, C), "w_qkv": a["w_qkv"], "wqT": a["w_qkv"][:, :INNER].T, "wkT": a["w_qkv"][:, INNER:2 * INNER].T,
        "taps": a["w_conv"].reshape(HA * TAPS), "w_fc": a["w_fc"], "b_fc": a["b_fc"],
        "WqT": b["Wq"].T, "WkT": b["Wk"].T, "WvT": b["Wv"].T, "WoT": b["Wo"].T,
        "capital_shares": f["capital_shares"], "router": router, "WsT": f["Ws"].T,
        **{n: by_partition(f[n]) for n in ("ln1_w", "ln1_b", "ln2_w", "ln2_b")},
        **{n: f[n] for n in ("Wr", "Wv", "Wo", "W1", "W2", "W3", "K_rwkv", "V_rwkv")},
        **shape_constants(),
    }
    nc = bacc.Bacc("TRN2", target_bir_lowering=False, num_devices=1)
    staged, dram = {}, {}
    for name, array in arrays.items():
        staged[f"in_{name}_dram"] = np.ascontiguousarray(array)
        dram[name] = nc.dram_tensor(f"in_{name}_dram", array.shape, mybir.dt.from_np(array.dtype), kind="ExternalInput").ap()
    out = nc.dram_tensor("out_0_dram", (B * T, C), F32, kind="ExternalOutput").ap()
    program(nc, dram, out)
    result = run_bass_kernel_spmd(nc, [staged], core_ids=[0])
    return result.results[0]["out_0_dram"].reshape(B, T, C)
```

```python
from contextlib import ExitStack

import concourse.bass as bass
import numpy as np
from concourse import mybir
from concourse.alu_op_type import AluOpType as ALU

F32 = mybir.dt.float32
F32R = mybir.dt.float32r
BF16 = mybir.dt.bfloat16
ACT = mybir.ActivationFunctionType
AX_X = mybir.AxisListType.X
MAX_ALL = bass.bass_isa.ReduceOp.max

P = 128
B, T, C = 8, 512, 256
TT = T // P
CT = C // P
XB = TT * C
EPS = 1e-5

HA, DA, M = 16, 64, 64
LG = T // M
NP = HA // 2
INNER = HA * DA
ITERS = 6
TAPS = 13
PAD = TAPS // 2
BAND = P + TAPS - 1

HB, DB = 16, 16
QUAD = 4

EXPERTS = 3
HID = 4 * C
HT = HID // P
NH = 2 * HT


def cols(tensor, start, n):
    return tensor[:, bass.ds(start, n)]


class Banks:

    def __init__(self, nc, ctx):
        self.data = [ctx.enter_context(nc.psum_tensor(f"bank{b}", [P, T], F32)) for b in range(8)]
        self.bank_full = [ctx.enter_context(nc.semaphore(f"bank_full{b}")) for b in range(8)]
        self.bank_free = [ctx.enter_context(nc.semaphore(f"bank_free{b}")) for b in range(8)]
        self.used = [0] * 8


class Fills:

    def __init__(self, banks, order, rounds=1):
        self.banks = banks
        self.before = list(banks.used)
        self.each = [0] * 8
        self.place = {}
        for name, b in order:
            self.place[name] = (b, self.each[b])
            self.each[b] += 1
        banks.used = [u + n * rounds for u, n in zip(banks.used, self.each)]

    def data(self, *name):
        return self.banks.data[self.place[name][0]]

    def filled(self, *name):
        return self.banks.bank_full[self.place[name][0]]

    def released(self, *name):
        return self.banks.bank_free[self.place[name][0]]

    def full(self, it, *name):
        b, k = self.place[name]
        return self.banks.bank_full[b], self.before[b] + it * self.each[b] + k + 1

    def read(self, it, *name):
        b, k = self.place[name]
        return self.banks.bank_free[b], self.before[b] + it * self.each[b] + k + 2

    def free(self, it, *name):
        b, k = self.place[name]
        return self.banks.bank_free[b], self.before[b] + it * self.each[b] + k + 1


class Core:

    def __init__(self, nc, ctx):
        self.nc = nc
        self.banks = Banks(nc, ctx)
        self.x = ctx.enter_context(nc.sbuf_tensor("x_tokens", [P, B * XB], F32))
        self.ident = ctx.enter_context(nc.sbuf_tensor("ident", [P, P], F32))
        self.neg_half = ctx.enter_context(nc.sbuf_tensor("neg_half", [P, TT], F32))
        self.setup_done = ctx.enter_context(nc.semaphore("setup_done"))
        self.ident_loaded = ctx.enter_context(nc.semaphore("ident_loaded"))
        self.waits_met = {
            e: ctx.enter_context(nc.semaphore(f"waits_met_{e}")) for e in ("pe", "act", "dve", "pool", "sp")
        }

    def met(self, eng, name):
        eng.sem_inc(self.waits_met[name], 1)


def sbuf(nc, ctx, name, shape, dtype=F32):
    return ctx.enter_context(nc.sbuf_tensor(name, shape, dtype))


def landmarks(core, la, dram):
    nc, banks, x = core.nc, core.banks, core.x
    with ExitStack() as ctx:
        sem = lambda name: ctx.enter_context(nc.semaphore(name))
        wqk = sbuf(nc, ctx, "wqk", [P, CT, 2 * INNER])
        stats = sbuf(nc, ctx, "lm_stats", [P, 2, TT, 6])
        mv = sbuf(nc, ctx, "lm_mv", [P, 2, TT, 2])
        rstd = sbuf(nc, ctx, "lm_rstd", [P, 2, TT])
        xn = sbuf(nc, ctx, "lm_xn", [P, 2, TT, C])
        xsum = sbuf(nc, ctx, "lm_xsum", [P, CT, B * M])
        neg_max = sbuf(nc, ctx, "lm_neg_max", [P, B, NP])
        row_sum = sbuf(nc, ctx, "lm_row_sum", [P, B, NP])
        row_rcp = sbuf(nc, ctx, "lm_row_rcp", [P, B, NP])
        sums = sbuf(nc, ctx, "lm_sums", [P, 2, B, NP])
        top = sbuf(nc, ctx, "lm_top", [P, 2])
        top_all = sbuf(nc, ctx, "lm_top_all", [P, 2])
        bound = sbuf(nc, ctx, "lm_bound", [P, 1])

        x_loaded = [sem("x_loaded0"), sem("x_loaded1")]
        w_loaded = sem("wqk_loaded")
        i64_loaded, stored = sem("i64_loaded"), sem("landmarks_stored")
        ql, kl = (sbuf(nc, ctx, n, [P, NP, B * M]) for n in ("ql", "kl"))
        a, aT = (sbuf(nc, ctx, n, [P, B, NP, M]) for n in ("a", "aT"))
        stats_done, mv_done, var_done, rstd_done, xn_done = map(
            sem, ("lm_stats_done", "lm_mv_done", "lm_var_done", "lm_rstd_done", "lm_xn_done"))
        max_done, exp_done, sum_done, rcp_done, a_done, sums_done = map(
            sem, ("lm_max_done", "lm_exp_done", "lm_sum_done", "lm_rcp_done", "a_done", "sums_done"))
        top_done, top_all_done, bound_done = map(sem, ("top_done", "top_all_done", "bound_done"))

        turn = Fills(banks, [(("xT", par, ct), 2 * par + ct) for par in range(2) for ct in range(CT)], B // 2)
        proj = Fills(banks, [(("ql", n), n % 8) for n in range(2 * NP)])
        soft = Fills(banks, [f for b in range(B) for f in ((("sim", b), b % 4), (("aT", b), 4 + b % 4))])

        with nc.Block() as block:

            @block.sync
            def _(sp):
                for free in banks.bank_free:
                    sp.sem_inc(free, 1)

        with nc.Block() as block:

            @block.sync
            def _(sp):
                sp.dma_start(core.ident[:], dram["ident"]).then_inc(core.ident_loaded, 16)
                sp.dma_start(la.i64[:], dram["i64"]).then_inc(i64_loaded, 16)
                def load(it, par):
                    b = it * 2 + par
                    sp.dma_start(
                        cols(x, b * XB, XB).rearrange("p (t c) -> p t c", c=C),
                        dram["x"][bass.ds(b * T, T), :].rearrange("(t p) c -> p t c", p=P),
                    ).then_inc(x_loaded[par], 16)

                load(0, 0)
                load(0, 1)
                la.load(sp, dram)
                with sp.Fori(1, B // 2) as it:
                    for par in range(2):
                        sp.wait_ge(x_loaded[par], it * 16)
                        core.met(sp, "sp")
                        load(it, par)
                for n in range(2 * NP - 8, 2 * NP):
                    sp.wait_ge(*proj.read(0, "ql", n))
                for b in range(B):
                    for src, dst in ((ql, la.ql), (kl, la.kl)):
                        sp.dma_start(dst[b].rearrange("p (j m) -> p j m", m=M), src[:, :, b * M:(b + 1) * M]).then_inc(stored, 16)
                for b in range(B):
                    sp.wait_ge(a_done, b + 1)
                    sp.dma_start(la.a[b], a[:, b].rearrange("p j m -> p (j m)")).then_inc(stored, 16)
                    sp.wait_ge(*soft.read(0, "aT", b))
                    sp.dma_start(la.aT[b], aT[:, b].rearrange("p j m -> p (j m)")).then_inc(stored, 16)
                sp.wait_ge(stored, 4 * B * 16)
                sp.wait_ge(la.loaded, la.loads)

            @block.scalar
            def _(act):
                act.dma_start(wqk[:], dram["w_qkv"][:, 0:2 * INNER].rearrange("(k p) n -> p k n", p=P)).then_inc(w_loaded, 16)
                for n in range(2 * NP):
                    act.wait_ge(*proj.full(0, "ql", n))
                    dst, scale = (ql, DA ** -0.5 / LG) if n < NP else (kl, 1.0 / LG)
                    nc.scalar.activation(dst[:, n % NP, :], proj.data("ql", n)[:], ACT.Copy, scale=scale).then_inc(
                        proj.released("ql", n), 1)
                for b in range(B + 1):
                    if b < B:
                        act.wait_ge(*soft.read(0, "sim", b))
                        nc.scalar.activation(a[:, b], a[:, b], ACT.Exp).then_inc(exp_done, 1)
                    if b >= 1:
                        act.wait_ge(*soft.full(0, "aT", b - 1))
                        nc.scalar.activation(
                            aT[:, b - 1], soft.data("aT", b - 1)[:].rearrange("p (j m) -> p j m", m=M), ACT.Copy
                        ).then_inc(soft.released("aT", b - 1), 1)

            @block.gpsimd
            def _(pool):
                nc.gpsimd.memset(core.neg_half[:], -0.5).then_inc(core.setup_done, 1)
                pool.wait_ge(core.setup_done, 1)
                with pool.Fori(0, B // 2) as it:
                    for par in range(2):
                        pool.wait_ge(mv_done, it * 2 * TT + (par + 1) * TT)
                        core.met(pool, "pool")
                        nc.gpsimd.tensor_scalar(rstd[:, par, :], mv[:, par, :, 1], EPS, None, ALU.add).then_inc(var_done, 1)
                        pool.wait_ge(var_done, it * 2 + par + 1)
                        nc.gpsimd.tensor_tensor(rstd[:, par, :], rstd[:, par, :], core.neg_half[:], ALU.pow).then_inc(
                            rstd_done, 1)
                pool.wait_ge(top_done, 2)
                nc.gpsimd.partition_all_reduce(top_all[:], top[:], P, MAX_ALL).then_inc(top_all_done, 1)

            @block.vector
            def _(dve):
                with dve.Fori(0, B // 2) as it:
                    for par in range(2):
                        dve.wait_ge(x_loaded[par], it * 16 + 16)
                        core.met(dve, "dve")
                        for t in range(TT):
                            nc.vector.bn_stats(stats[:, par, t, :], cols(x, (it * 2 + par) * XB + t * C, C)).then_inc(stats_done, 1)
                        for t in range(TT):
                            dve.wait_ge(stats_done, it * 2 * TT + par * TT + t + 1)
                            core.met(dve, "dve")
                            nc.vector.bn_aggr(mv[:, par, t, :], stats[:, par, t, :]).then_inc(mv_done, 1)
                    for par in range(2):
                        dve.wait_ge(rstd_done, it * 2 + par + 1)
                        core.met(dve, "dve")
                        for t in range(TT):
                            nc.vector.tensor_scalar(
                                xn[:, par, t, :], cols(x, (it * 2 + par) * XB + t * C, C),
                                mv[:, par, t, 0:1], rstd[:, par, t:t + 1], ALU.subtract, ALU.mult).then_inc(xn_done, 1)
                    for par in range(2):
                        for ct in range(CT):
                            dve.wait_ge(*turn.full(it, "xT", par, ct))
                            core.met(dve, "dve")
                            nc.vector.tensor_reduce(
                                xsum[:, ct, bass.ds((it * 2 + par) * M, M)],
                                turn.data("xT", par, ct)[:].rearrange("p (m l) -> p m l", l=LG),
                                AX_X, ALU.add).then_inc(turn.released("xT", par, ct), 1)
                grid = lambda ap: ap[:].rearrange("p (j m) -> p j m", m=M)
                spread = lambda ap: ap.unsqueeze(2).to_broadcast([P, NP, M])
                for b in range(B + 2):
                    if b < B:
                        dve.wait_ge(*soft.full(0, "sim", b))
                        nc.vector.tensor_reduce(neg_max[:, b], grid(soft.data("sim", b)), AX_X, ALU.max, negate=True).then_inc(max_done, 1)
                        dve.wait_ge(max_done, b + 1)
                        nc.vector.tensor_tensor(a[:, b], grid(soft.data("sim", b)), spread(neg_max[:, b]), ALU.add).then_inc(soft.released("sim", b), 1)
                    if 1 <= b <= B:
                        c = b - 1
                        dve.wait_ge(exp_done, c + 1)
                        nc.vector.tensor_reduce(row_sum[:, c], a[:, c], AX_X, ALU.add).then_inc(sum_done, 1)
                        dve.wait_ge(sum_done, c + 1)
                        nc.vector.reciprocal(row_rcp[:, c], row_sum[:, c]).then_inc(rcp_done, 1)
                        dve.wait_ge(rcp_done, c + 1)
                        nc.vector.tensor_tensor(a[:, c], a[:, c], spread(row_rcp[:, c]), ALU.mult).then_inc(a_done, 1)
                        dve.wait_ge(a_done, c + 1)
                        nc.vector.tensor_reduce(sums[:, 0, c], a[:, c], AX_X, ALU.add).then_inc(sums_done, 1)
                    if b >= 2:
                        c = b - 2
                        dve.wait_ge(*soft.read(0, "aT", c))
                        nc.vector.tensor_reduce(sums[:, 1, c], aT[:, c], AX_X, ALU.add).then_inc(sums_done, 1)
                dve.wait_ge(sums_done, 2 * B)
                for side in range(2):
                    nc.vector.tensor_reduce(top[:, side:side + 1], sums[:, side].rearrange("p b j -> p (b j)"), AX_X, ALU.max).then_inc(top_done, 1)
                dve.wait_ge(top_all_done, 1)
                nc.vector.tensor_tensor(bound[:], top_all[:, 0:1], top_all[:, 1:2], ALU.mult).then_inc(bound_done, 1)
                dve.wait_ge(bound_done, 1)
                nc.vector.reciprocal(la.inv_bound[:], bound[:]).then_inc(bound_done, 1)
                dve.wait_ge(bound_done, 2)

            @block.tensor
            def _(pe):
                pe.wait_ge(core.ident_loaded, 16)
                with pe.Fori(0, B // 2) as it:
                    for par in range(2):
                        pe.wait_ge(xn_done, it * 2 * TT + (par + 1) * TT)
                        for ct in range(CT):
                            pe.wait_ge(*turn.free(it, "xT", par, ct))
                            core.met(pe, "pe")
                            for t in range(TT):
                                last = nc.tensor.transpose(
                                    turn.data("xT", par, ct)[:, t * P:(t + 1) * P], xn[:, par, t, ct * P:(ct + 1) * P],
                                    core.ident[:])
                            last.then_inc(turn.filled("xT", par, ct), 1)
                for par in range(2):
                    for ct in range(CT):
                        pe.wait_ge(*turn.read(B // 2 - 1, "xT", par, ct))
                pe.wait_ge(w_loaded, 16)
                for n in range(2 * NP):
                    pe.wait_ge(*proj.free(0, "ql", n))
                    for ct in range(CT):
                        last = nc.tensor.matmul(proj.data("ql", n)[:], wqk[:, ct, n * P:(n + 1) * P], xsum[:, ct, :],
                                                start=ct == 0, stop=ct == CT - 1)
                    last.then_inc(proj.filled("ql", n), 1)
                for n in range(NP, 2 * NP):
                    pe.wait_ge(*proj.read(0, "ql", n))
                pe.wait_ge(i64_loaded, 16)
                for b in range(B + 1):
                    if b < B:
                        pe.wait_ge(*soft.free(0, "sim", b))
                        for j in range(NP):
                            for h in (slice(0, M), slice(M, 2 * M)):
                                last = nc.tensor.matmul(
                                    soft.data("sim", b)[h, j * M:(j + 1) * M], ql[h, j, b * M:(b + 1) * M],
                                    kl[h, j, b * M:(b + 1) * M], start=True, stop=True)
                        last.then_inc(soft.filled("sim", b), 1)
                    if b >= 1:
                        c = b - 1
                        pe.wait_ge(a_done, c + 1)
                        pe.wait_ge(*soft.free(0, "aT", c))
                        for j in range(NP):
                            for h in (slice(0, M), slice(M, 2 * M)):
                                last = nc.tensor.matmul(soft.data("aT", c)[h, j * M:(j + 1) * M], a[h, c, j, :],
                                                        la.i64[h, :], start=True, stop=True)
                        last.then_inc(soft.filled("aT", c), 1)


class AttentionA:

    def __init__(self, nc, ctx):
        self.wqT, self.wkT, self.wfc = (sbuf(nc, ctx, n, [P, NP, C]) for n in ("wqT", "wkT", "wfc"))
        self.wv = sbuf(nc, ctx, "wv_a", [P, CT, INNER])
        self.bias = sbuf(nc, ctx, "bias_fc", [P, C])
        self.inv_bound = sbuf(nc, ctx, "inv_bound", [P, 1])
        self.i64 = sbuf(nc, ctx, "i64", [P, M])
        self.ql, self.kl, self.a, self.aT = (
            nc.dram_tensor(f"scratch_{n}", (B, P, NP * M), F32, kind="Internal").ap() for n in ("ql", "kl", "a", "aT"))
        self.loaded = ctx.enter_context(nc.semaphore("weights_a_loaded"))
        self.loads = 0

    def load(self, eng, dram):
        rows = lambda ap: ap.rearrange("(j p) c -> p j c", p=P)
        for dst, src in (
                (self.wqT, rows(dram["wqT"])), (self.wkT, rows(dram["wkT"])), (self.wfc, rows(dram["w_fc"])),
                (self.wv, dram["w_qkv"][:, 2 * INNER:].rearrange("(k p) n -> p k n", p=P)),
                (self.bias, dram["b_fc"].partition_broadcast(P))):
            eng.dma_start(dst[:], src).then_inc(self.loaded, 16)
            self.loads += 16


GP = NP // 2
GROUPS = NP // GP
RESTORE = 2
INVERSE_STEPS = [("w0",)] + [
    n for k in range(ITERS) for n in [("t", k), ("u", k), ("wz", k)] + ([("w", k)] if k == RESTORE else [])]


def layer_a(core, la, dram):
    nc, banks, x = core.nc, core.banks, core.x
    HH = NP // 2
    with ExitStack() as ctx:
        sem = lambda name: ctx.enter_context(nc.semaphore(name))
        buf = lambda name, shape: sbuf(nc, ctx, name, shape)
        stats, mv, rstd = buf("a_stats", [P, TT, 6]), buf("a_mv", [P, TT, 2]), buf("a_rstd", [P, TT])
        xn, xnT = buf("a_xn", [P, TT, C]), buf("a_xnT", [P, CT, T])
        kl_diag, ql_diag = buf("kl_diag", [P, NP, P]), buf("ql_diag", [P, NP, P])
        u, g = buf("u", [P, CT, INNER]), buf("g", [P, CT, INNER])
        fc = g[:].rearrange("p k (j c) -> p (k j) c", c=C)
        v = buf("v_a", [P, TT, INNER // 2])
        probs1 = buf("probs1", [P, TT, INNER])
        neg_max1, sum1, rcp1 = (buf(n, [P, 2 * TT, NP]) for n in ("neg_max1", "sum1", "rcp1"))
        e3, e3T = buf("e3", [P, 2, T]), buf("e3T", [P, 2, T])
        neg_max3, sum3, rcp3 = (buf(n, [P, NP]) for n in ("neg_max3", "sum3", "rcp3"))
        av3, avT, inverse = (buf(n, [P, NP, M]) for n in ("av3", "avT", "inverse"))
        band, band_term = buf("band", [P, HA, BAND]), buf("band_term", [P, HA, BAND])
        taps, shifted = buf("taps", [P, HA, TAPS]), buf("shifted_ident", [P, BAND + TAPS - 1])
        i7, i15, i13 = (buf(f"i{n}", [P, GP, M]) for n in (7, 15, 13))
        a_in, at = buf("a_in", [P, NP, M]), buf("at", [P, NP, M])
        wz = buf("wz", [P, GROUPS, GP, 2, M])
        t1, t3, p, z = (buf(n, [P, GROUPS, GP, M]) for n in ("pi_t1", "pi_t3", "pi_p", "pi_z"))
        conv = buf("conv", [P, 2, T])
        names = ("stats_done", "mv_done", "var_done", "rstd_done", "xn_done", "landmarks_loaded", "diag_zeroed", "max1_done",
                 "exp1_done", "sum1_done", "rcp1_done", "probs1_done", "max3_done", "rcp3_done", "bias_added", "taps_loaded",
                 "term_done", "band_done", "eyes_done", "a_loaded", "t1_done")
        s = {n: sem("a_" + n) for n in names}

        order = [("xT", k) for k in range(CT)] + [("u", k) for k in range(4)] + [("g", k) for k in range(4)]
        for f in range(TT):
            order += [("v", 0, f), ("s1", f)]

        def s3_steps(half):
            for j in range(half * HH, (half + 1) * HH + 1):
                if j < (half + 1) * HH:
                    yield ("s3", j)
                    if half == 0:
                        yield ("s1", TT + j)
                if j > half * HH:
                    yield ("e3T", j - 1)
                    yield ("av3", j - 1)

        order += [n for n in s3_steps(0) if n[0] != "av3"] + [("v", 1, t) for t in range(TT)]
        order += [n for n in s3_steps(1) if n[0] != "av3"] + [("avT",)] + [("fc", k) for k in range(4)] + [("c", j) for j in range(NP)]
        fills = Fills(banks, [(n, i % 4) for i, n in enumerate(order)] + [(("av3", 0), 4), (("av3", 1), 5), (("y", 0), 4), (("y", 1), 5)], B)
        inverse_order = [((*n, g), 6 + g) for n in INVERSE_STEPS for g in range(GROUPS)]
        first_inverse, next_inverse = Fills(banks, inverse_order), Fills(banks, inverse_order, B - 1)
        heads = lambda ap: ap.rearrange("p (j m) -> p j m", m=M)
        spread = lambda ap, n: ap.unsqueeze(2).to_broadcast([P, n, M])
        halves = (slice(0, M), slice(M, 2 * M))
        group = lambda tensor, g: tensor[:, g * GP:(g + 1) * GP, :]
        single = lambda fl, *n: fl.data(*n)[:, 0:GP * M].rearrange("p (j m) -> p j m", m=M)
        double = lambda fl, *n: fl.data(*n)[:].rearrange("p (j q m) -> p j q m", q=2, m=M)

        def rounds(eng, batch, step):
            for i in range(len(INVERSE_STEPS)):
                step(first_inverse, 0, 0, i)
            with eng.Fori(0, B - 1) as it:
                batch(it, False, lambda i: step(next_inverse, it, it + 1, i))
            batch(B - 1, True, lambda i: None)

        with nc.Block() as block:

            @block.sync
            def _(sp):
                def load_landmarks(n):
                    for src, dst in ((la.kl, kl_diag), (la.ql, ql_diag)):
                        for h in halves:
                            sp.dma_start(dst[h, :, h], src[bass.ds(n, 1), h, :].rearrange("b p (j m) -> (b p) j m", m=M)).then_inc(
                                s["landmarks_loaded"], 16)

                def load_a(n):
                    for src, dst in ((la.a, a_in), (la.aT, at)):
                        sp.dma_start(dst[:].rearrange("p j m -> p (j m)"), src[bass.ds(n, 1), :, :].rearrange("b p c -> (b p) c")).then_inc(
                            s["a_loaded"], 16)

                load_a(0)
                sp.dma_start(taps[:].rearrange("p h k -> p (h k)"), dram["taps"].partition_broadcast(P)).then_inc(s["taps_loaded"], 16)
                sp.dma_start(shifted[:], dram["shifted_ident"]).then_inc(s["taps_loaded"], 16)
                sp.wait_ge(s["diag_zeroed"], 2)
                load_landmarks(0)
                for g in range(GROUPS):
                    sp.wait_ge(*first_inverse.full(0, "w", RESTORE, g))
                load_a(1)
                def reached(semaphore, value):
                    sp.wait_ge(semaphore, value)
                    core.met(sp, "sp")

                with sp.Fori(0, B - 2) as it:
                    for k in range(4):
                        reached(*fills.full(it, "g", k))
                    load_landmarks(it + 1)
                    for g in range(GROUPS):
                        reached(*next_inverse.full(it, "w", RESTORE, g))
                    load_a(it + 2)
                for k in range(4):
                    sp.wait_ge(*fills.full(B - 2, "g", k))
                load_landmarks(B - 1)
                sp.wait_ge(s["landmarks_loaded"], B * 64)
                sp.wait_ge(s["a_loaded"], B * 32)

            @block.vector
            def _(dve):
                def statistics(n):
                    dve.wait_ge(s["xn_done"], n * TT)
                    core.met(dve, "dve")
                    for t in range(TT):
                        nc.vector.bn_stats(stats[:, t, :], cols(x, n * XB + t * C, C)).then_inc(s["stats_done"], 1)
                    for t in range(TT):
                        dve.wait_ge(s["stats_done"], n * TT + t + 1)
                        core.met(dve, "dve")
                        nc.vector.bn_aggr(mv[:, t, :], stats[:, t, :]).then_inc(s["mv_done"], 1)

                def normalise(n):
                    dve.wait_ge(s["rstd_done"], n + 1)
                    core.met(dve, "dve")
                    for t in range(TT):
                        nc.vector.tensor_scalar(xn[:, t, :], cols(x, n * XB + t * C, C), mv[:, t, 0:1], rstd[:, t:t + 1],
                                                ALU.subtract, ALU.mult).then_inc(s["xn_done"], 1)

                def shift1(it, f):
                    dve.wait_ge(*fills.full(it, "s1", f))
                    core.met(dve, "dve")
                    scores = heads(fills.data("s1", f)[:])
                    t, half = f % TT, f // TT
                    nc.vector.tensor_reduce(neg_max1[:, f], scores, AX_X, ALU.max, negate=True).then_inc(s["max1_done"], 1)
                    dve.wait_ge(s["max1_done"], it * 2 * TT + f + 1)
                    nc.vector.tensor_tensor(heads(probs1[:, t, half * 512:(half + 1) * 512]), scores, spread(neg_max1[:, f], NP),
                                            ALU.add).then_inc(fills.released("s1", f), 1)

                def sums1(it, f):
                    t, half = f % TT, f // TT
                    dve.wait_ge(s["exp1_done"], it * 2 * TT + f + 1)
                    core.met(dve, "dve")
                    nc.vector.tensor_reduce(sum1[:, f], heads(probs1[:, t, half * 512:(half + 1) * 512]), AX_X, ALU.add).then_inc(
                        s["sum1_done"], 1)
                    dve.wait_ge(s["sum1_done"], it * 2 * TT + f + 1)
                    core.met(dve, "dve")
                    nc.vector.reciprocal(rcp1[:, f], sum1[:, f]).then_inc(s["rcp1_done"], 1)

                def max3(it, j):
                    dve.wait_ge(*fills.full(it, "s3", j))
                    core.met(dve, "dve")
                    nc.vector.tensor_reduce(neg_max3[:, j:j + 1], fills.data("s3", j)[:], AX_X, ALU.max, negate=True).then_inc(
                        s["max3_done"], 1)

                def scale3(it, half):
                    pairs = slice(half * HH, (half + 1) * HH)
                    for j in range(half * HH, (half + 1) * HH):
                        dve.wait_ge(*fills.read(it, "s3", j))
                    core.met(dve, "dve")
                    nc.vector.reciprocal(rcp3[:, pairs], sum3[:, pairs]).then_inc(s["rcp3_done"], 1)
                    dve.wait_ge(s["rcp3_done"], it * 2 + half + 1)
                    dve.wait_ge(*fills.full(it, "av3", half))
                    nc.vector.tensor_tensor(av3[:, pairs], heads(fills.data("av3", half)[:, 0:HH * M]), spread(rcp3[:, pairs], HH),
                                            ALU.mult).then_inc(fills.released("av3", half), 1)

                def step(fl, it, n, i):
                    name = INVERSE_STEPS[i]
                    for g in range(GROUPS):
                        if name[0] == "w0":
                            dve.wait_ge(*fl.full(it, *name, g))
                            dve.wait_ge(s["a_loaded"], n * 32 + 32)
                            core.met(dve, "dve")
                            nc.vector.tensor_scalar(wz[:, g, :, 1, :], group(a_in, g), la.inv_bound[:, 0:1], None, ALU.mult)
                    for g in range(GROUPS):
                        if name[0] == "t":
                            dve.wait_ge(*fl.full(it, *name, g))
                            nc.vector.tensor_tensor(t3[:, g], i15[:], single(fl, *name, g), ALU.subtract).then_inc(
                                fl.released(*name, g), 1)
                        elif name[0] == "u":
                            dve.wait_ge(*fl.full(it, *name, g))
                            core.met(dve, "dve")
                            nc.vector.scalar_tensor_tensor(out=p[:, g], in0=single(fl, *name, g), scalar=-0.25, in1=i13[:],
                                                           op0=ALU.mult, op1=ALU.add).then_inc(fl.released(*name, g), 1)
                        elif name in (("wz", RESTORE), ("wz", ITERS - 1)):
                            pass
                        else:
                            dve.wait_ge(*fl.read(it, *name, g))
                            nc.vector.tensor_tensor(t1[:, g], i7[:], wz[:, g, :, 0, :], ALU.subtract).then_inc(s["t1_done"], 1)

                def batch(it, last, mark):
                    if not last:
                        statistics(it + 1)
                    mark(0)
                    mark(1)
                    for f in range(TT):
                        shift1(it, f)
                        if f:
                            sums1(it, f - 1)
                        mark(2 + f)
                    if not last:
                        normalise(it + 1)
                    for j in range(HH):
                        max3(it, j)
                        shift1(it, TT + j)
                        sums1(it, TT + j - 1)
                        mark(6 + j)
                    sums1(it, 2 * TT - 1)
                    scale3(it, 0)
                    mark(10)
                    mark(11)
                    for j in range(HH, NP):
                        max3(it, j)
                        mark(12 + j - HH)
                    scale3(it, 1)
                    for i in range(16, 20):
                        mark(i)
                    dve.wait_ge(s["bias_added"], it * 2 + 2)
                    for k in range(2):
                        dve.wait_ge(*fills.full(it, "y", k))
                        xs = cols(x, it * XB + k * 512, 512)
                        nc.vector.tensor_tensor(xs, xs, fills.data("y", k)[:], ALU.add).then_inc(fills.released("y", k), 1)

                for diag in (kl_diag, ql_diag):
                    nc.vector.memset(diag[:], 0.0).then_inc(s["diag_zeroed"], 1)
                for tile, n in ((i7, 7.0), (i15, 15.0), (i13, 13.0 / 4)):
                    nc.vector.tensor_scalar(tile[:], la.i64[:].unsqueeze(1).to_broadcast([P, GP, M]), n, None, ALU.mult).then_inc(
                        s["eyes_done"], 1)
                dve.wait_ge(s["eyes_done"], 3)
                statistics(0)
                normalise(0)
                rounds(dve, batch, step)

            @block.gpsimd
            def _(pool):
                def inverse_deviation(n):
                    pool.wait_ge(s["mv_done"], (n + 1) * TT)
                    core.met(pool, "pool")
                    nc.gpsimd.tensor_scalar(rstd[:], mv[:, :, 1], EPS, None, ALU.add).then_inc(s["var_done"], 1)
                    pool.wait_ge(s["var_done"], n + 1)
                    nc.gpsimd.tensor_tensor(rstd[:], rstd[:], core.neg_half[:], ALU.pow).then_inc(s["rstd_done"], 1)

                def batch(it, last, mark):
                    if not last:
                        inverse_deviation(it + 1)
                    pool.wait_ge(s["xn_done"], it * TT + TT)
                    core.met(pool, "pool")
                    for k in range(2):
                        xs = cols(x, it * XB + k * 512, 512).rearrange("p (t c) -> p t c", c=C)
                        nc.gpsimd.tensor_tensor(xs, xs, la.bias[:].unsqueeze(1).to_broadcast([P, 2, C]), ALU.add).then_inc(
                            s["bias_added"], 1)
                    for f in range(2 * TT):
                        t, half = f % TT, f // TT
                        pool.wait_ge(s["rcp1_done"], it * 2 * TT + f + 1)
                        probs = heads(probs1[:, t, half * 512:(half + 1) * 512])
                        nc.gpsimd.tensor_tensor(probs, probs, spread(rcp1[:, f], NP), ALU.mult).then_inc(s["probs1_done"], 1)

                inverse_deviation(0)
                diagonal = lambda k: shifted[:, k:k + BAND].unsqueeze(1).to_broadcast([P, HA, BAND])
                tap = lambda k: taps[:, :, k:k + 1].to_broadcast([P, HA, BAND])
                pool.wait_ge(s["taps_loaded"], 32)
                nc.gpsimd.tensor_tensor(band[:], tap(0), diagonal(0), ALU.mult).then_inc(s["band_done"], 1)
                for k in range(1, TAPS):
                    pool.wait_ge(s["band_done"], k)
                    nc.gpsimd.tensor_tensor(band_term[:], tap(k), diagonal(k), ALU.mult).then_inc(s["term_done"], 1)
                    pool.wait_ge(s["term_done"], k)
                    nc.gpsimd.tensor_tensor(band[:], band[:], band_term[:], ALU.add).then_inc(s["band_done"], 1)
                pool.wait_ge(s["band_done"], TAPS)
                nc.gpsimd.tensor_tensor(band[:], band[:], diagonal(PAD), ALU.add).then_inc(s["band_done"], 1)
                rounds(pool, batch, lambda fl, it, n, i: None)

            @block.scalar
            def _(act):
                def copy(it, dst, name):
                    act.wait_ge(*fills.full(it, *name))
                    nc.scalar.activation(dst, fills.data(*name)[:], ACT.Copy).then_inc(fills.released(*name), 1)

                def exp1(it, f):
                    t, half = f % TT, f // TT
                    act.wait_ge(*fills.read(it, "s1", f))
                    probs = probs1[:, t, half * 512:(half + 1) * 512]
                    nc.scalar.activation(probs, probs, ACT.Exp, scale=DA ** -0.5).then_inc(s["exp1_done"], 1)

                def exp3(it, j):
                    act.wait_ge(s["max3_done"], it * NP + j + 1)
                    nc.scalar.activation(e3[:, j % 2], fills.data("s3", j)[:], ACT.Exp, bias=neg_max3[:, j:j + 1],
                                         accum_out=sum3[:, j:j + 1]).then_inc(fills.released("s3", j), 1)

                def step(fl, it, n, i):
                    name = INVERSE_STEPS[i]
                    for g in range(GROUPS):
                        if name[0] in ("t", "u"):
                            continue
                        act.wait_ge(*fl.full(it, *name, g))
                        if name[0] == "w0":
                            nc.scalar.activation(wz[:, g, :, 0, :], single(fl, *name, g), ACT.Copy, scale=la.inv_bound[:, 0:1]).then_inc(
                                fl.released(*name, g), 1)
                        elif name[0] == "w":
                            nc.scalar.activation(wz[:, g, :, 0, :], single(fl, *name, g), ACT.Copy).then_inc(fl.released(*name, g), 1)
                        elif name[1] == ITERS - 1:
                            nc.scalar.activation(group(inverse, g), double(fl, *name, g)[:, :, 1, :], ACT.Copy).then_inc(
                                fl.released(*name, g), 1)
                        elif name[1] == RESTORE:
                            nc.scalar.activation(z[:, g], double(fl, *name, g)[:, :, 0, :], ACT.Copy)
                            nc.scalar.activation(wz[:, g, :, 1, :], double(fl, *name, g)[:, :, 1, :], ACT.Copy).then_inc(
                                fl.released(*name, g), 1)
                        else:
                            nc.scalar.activation(wz[:, g], double(fl, *name, g), ACT.Copy).then_inc(fl.released(*name, g), 1)

                def batch(it, last, mark):
                    for k in range(CT):
                        copy(it, xnT[:, k], ("xT", k))
                    for m, (name, dst) in enumerate((("u", u), ("g", g))):
                        for k in range(4):
                            copy(it, dst[:, k // 2, k % 2 * 512:(k % 2 + 1) * 512], (name, k))
                        mark(m)
                    for f in range(TT):
                        copy(it, v[:, f], ("v", 0, f))
                        exp1(it, f)
                        mark(2 + f)
                    for j in range(HH + 1):
                        if j < HH:
                            exp3(it, j)
                            exp1(it, TT + j)
                        if j:
                            copy(it, e3T[:, (j - 1) % 2], ("e3T", j - 1))
                        if j < HH:
                            mark(6 + j)
                    for t in range(TT):
                        copy(it, v[:, t], ("v", 1, t))
                        if t in (0, 2):
                            mark(10 + t // 2)
                    for j in range(HH, NP + 1):
                        if j < NP:
                            exp3(it, j)
                        if j > HH:
                            copy(it, e3T[:, (j - 1) % 2], ("e3T", j - 1))
                        if j < NP:
                            mark(12 + j - HH)
                    copy(it, avT[:].rearrange("p j m -> p (j m)"), ("avT",))
                    for k in range(4):
                        copy(it, fc[:, 2 * k:2 * k + 2].rearrange("p j c -> p (j c)"), ("fc", k))
                    mark(16)
                    for j in range(NP):
                        copy(it, conv[:, j % 2], ("c", j))
                        if j in (2, 4, 6):
                            mark(16 + j // 2)

                rounds(act, batch, step)

            @block.tensor
            def _(pe):
                def begin_in(fl, it, *name):
                    pe.wait_ge(*fl.free(it, *name))
                    core.met(pe, "pe")
                    return fl.data(*name)

                def begin(it, *name):
                    return begin_in(fills, it, *name)

                def from_xn(it, name, t, weight):
                    data = begin(it, *name)
                    for k in range(CT):
                        last = nc.tensor.matmul(data[:], xnT[:, k, t * P:(t + 1) * P], weight(k), start=k == 0, stop=k == CT - 1)
                    last.then_inc(fills.filled(*name), 1)

                def scores1(it, f):
                    t, half = f % TT, f // TT
                    from_xn(it, ("s1", f), t, lambda k: u[:, k, half * 512:(half + 1) * 512])

                def values(it, half, mark):
                    for t in range(TT):
                        from_xn(it, ("v", half, t), t, lambda k: la.wv[:, k, half * 512:(half + 1) * 512])
                        if half == 0:
                            if t == 0:
                                for k in range(4):
                                    pe.wait_ge(*fills.read(it, "u", k))
                                core.met(pe, "pe")
                            scores1(it, t)
                            mark(2 + t)
                        elif t in (0, 2):
                            mark(10 + t // 2)

                def scores3(it, j):
                    data = begin(it, "s3", j)
                    for k in range(CT):
                        last = nc.tensor.matmul(data[:], g[:, k, j * P:(j + 1) * P], xnT[:, k, :], start=k == 0, stop=k == CT - 1)
                    last.then_inc(fills.filled("s3", j), 1)

                def turn3(it, j):
                    pe.wait_ge(*fills.read(it, "s3", j))
                    data = begin(it, "e3T", j)
                    for t in range(TT):
                        last = nc.tensor.transpose(data[:, t * P:(t + 1) * P], e3[:, j % 2, t * P:(t + 1) * P], core.ident[:])
                    last.then_inc(fills.filled("e3T", j), 1)

                def values3(it, j):
                    half, jj = j // HH, j % HH
                    if jj == 0:
                        for t in range(TT):
                            pe.wait_ge(*fills.read(it, "v", half, t))
                        core.met(pe, "pe")
                        begin(it, "av3", half)
                    data = fills.data("av3", half)
                    pe.wait_ge(*fills.read(it, "e3T", j))
                    core.met(pe, "pe")
                    for t in range(TT):
                        for hh in range(2):
                            last = nc.tensor.matmul(
                                data[hh * M:(hh + 1) * M, jj * M:(jj + 1) * M], e3T[:, j % 2, t * P + hh * M:t * P + (hh + 1) * M],
                                v[:, t, (2 * jj + hh) * DA:(2 * jj + hh + 1) * DA], start=t == 0, stop=t == TT - 1,
                                skip_group_check=True)
                    if jj == HH - 1:
                        last.then_inc(fills.filled("av3", half), 1)

                def products(data, lhs, rhs):
                    for j in range(GP):
                        for h in halves:
                            last = nc.tensor.matmul(data[h, j * M:(j + 1) * M], lhs[h, j], rhs[h, j], start=True, stop=True)
                    return last

                def step(fl, it, n, i):
                    name = INVERSE_STEPS[i]
                    for g in range(GROUPS):
                        k = name[-1]
                        if name[0] == "w0":
                            pe.wait_ge(s["a_loaded"], n * 32 + 32)
                        if name[0] == "t":
                            pe.wait_ge(s["t1_done"], (n * ITERS + k) * GROUPS + g + 1)
                        data = begin_in(fl, it, *name, g)
                        if name[0] == "w0":
                            last = products(data, group(at, g), group(at, g))
                        elif name[0] == "t":
                            last = products(data, wz[:, g, :, 0, :], t1[:, g])
                        elif name[0] == "u":
                            last = products(data, wz[:, g, :, 0, :], t3[:, g])
                        elif name[0] == "w":
                            last = products(data, group(at, g), z[:, g])
                        else:
                            pairs = double(fl, *name, g)
                            for j in range(GP):
                                for h in halves:
                                    if k == RESTORE:
                                        nc.tensor.matmul(pairs[h, j, 0], wz[h, g, j, 1, :], p[h, g, j, :], start=True, stop=True)
                                    if k in (RESTORE, ITERS - 1):
                                        last = nc.tensor.matmul(pairs[h, j, 1], p[h, g, j, :], wz[h, g, j, 1, :], start=True, stop=True)
                                    else:
                                        last = nc.tensor.matmul(pairs[h, j], p[h, g, j, :], wz[h, g, j], start=True, stop=True)
                        last.then_inc(fl.filled(*name, g), 1)

                def batch(it, last_batch, mark):
                    pe.wait_ge(s["xn_done"], it * TT + TT)
                    for k in range(CT):
                        data = begin(it, "xT", k)
                        for t in range(TT):
                            last = nc.tensor.transpose(data[:, t * P:(t + 1) * P], xn[:, t, k * P:(k + 1) * P], core.ident[:])
                        last.then_inc(fills.filled("xT", k), 1)
                    pe.wait_ge(s["landmarks_loaded"], it * 64 + 64)
                    for name, weight, diag in (("u", la.wqT, kl_diag), ("g", la.wkT, ql_diag)):
                        for k in range(4):
                            data = begin(it, name, k)
                            for j in range(HH):
                                pair = k % 2 * HH + j
                                last = nc.tensor.matmul(data[:, j * P:(j + 1) * P], weight[:, pair, k // 2 * P:(k // 2 + 1) * P],
                                                        diag[:, pair, :], start=True, stop=True)
                            last.then_inc(fills.filled(name, k), 1)
                        mark(0 if name == "u" else 1)
                    for k in range(CT):
                        pe.wait_ge(*fills.read(it, "xT", k))
                    core.met(pe, "pe")
                    values(it, 0, mark)
                    for k in range(4):
                        pe.wait_ge(*fills.read(it, "g", k))
                    core.met(pe, "pe")
                    for n in s3_steps(0):
                        {"s3": scores3, "s1": scores1, "e3T": turn3, "av3": values3}[n[0]](it, n[1])
                        if n[0] == "s1":
                            mark(6 + n[1] - TT)
                    values(it, 1, mark)
                    for n in s3_steps(1):
                        {"s3": scores3, "e3T": turn3, "av3": values3}[n[0]](it, n[1])
                        if n[0] == "s3":
                            mark(12 + n[1] - HH)
                    for half in range(2):
                        pe.wait_ge(*fills.read(it, "av3", half))
                    for g in range(GROUPS):
                        if last_batch:
                            pe.wait_ge(*next_inverse.read(B - 2, "wz", ITERS - 1, g))
                        else:
                            pe.wait_ge(*next_inverse.free(it, "w0", g))
                    data = begin(it, "avT")
                    for j in range(NP):
                        for h in (slice(0, M), slice(M, 2 * M)):
                            last = nc.tensor.matmul(data[h, j * M:(j + 1) * M], av3[h, j, :], inverse[h, j, :], start=True, stop=True)
                    last.then_inc(fills.filled("avT"), 1)
                    pe.wait_ge(*fills.read(it, "avT"))
                    for k in range(4):
                        data = begin(it, "fc", k)
                        for jj in range(2):
                            for h in (slice(0, M), slice(M, 2 * M)):
                                last = nc.tensor.matmul(data[h, jj * C:(jj + 1) * C], avT[h, 2 * k + jj, :], la.wfc[h, 2 * k + jj, :],
                                                        start=True, stop=True)
                        last.then_inc(fills.filled("fc", k), 1)
                    mark(16)
                    pe.wait_ge(s["probs1_done"], it * 2 * TT + 2 * TT)
                    pe.wait_ge(s["band_done"], TAPS + 1)
                    core.met(pe, "pe")
                    for j in range(NP + 1):
                        if j < NP:
                            data = begin(it, "c", j)
                            for t in range(TT):
                                lo, hi = max(0, t * P - PAD), min(T, (t + 1) * P + PAD)
                                off = lo - (t * P - PAD)
                                for hh in range(2):
                                    h = 2 * j + hh
                                    last = nc.tensor.matmul(
                                        data[hh * M:(hh + 1) * M, lo:hi], probs1[:, t, h * M:(h + 1) * M],
                                        band[:, h, off:off + hi - lo], start=t == 0, stop=t == TT - 1, skip_group_check=True)
                            last.then_inc(fills.filled("c", j), 1)
                        if j:
                            if j == 1:
                                for k in range(4):
                                    pe.wait_ge(*fills.read(it, "fc", k))
                                core.met(pe, "pe")
                                for k in range(2):
                                    begin(it, "y", k)
                            pe.wait_ge(*fills.read(it, "c", j - 1))
                            core.met(pe, "pe")
                            for t in range(TT):
                                last = nc.tensor.matmul(
                                    fills.data("y", t // 2)[:, t % 2 * C:(t % 2 + 1) * C], conv[:, (j - 1) % 2, t * P:(t + 1) * P],
                                    fc[:, j - 1, :], start=j == 1 and t % 2 == 0, stop=j == NP, skip_group_check=True)
                                if j == NP and t % 2 == 1:
                                    last.then_inc(fills.filled("y", t // 2), 1)
                            if j in (3, 5, 7):
                                mark(16 + j // 2)

                rounds(pe, batch, step)


class FeedForward:

    def __init__(self, nc, ctx, run):
        self.run = run
        split = lambda name, shape: [sbuf(nc, ctx, f"{name}_{part}_{run}", shape, F32R) for part in ("hi", "lo")]
        self.k = split("k_rwkv", [P, 2, CT, HID])
        self.v = split("v_rwkv", [P, 2, HT, C])
        self.square = {n: split(n.lower() + "_ff", [P, CT, C]) for n in ("Wr", "Wv", "Wo", "W1", "W3", "WsW2")}
        self.router = split("router", [P, CT, 8])
        self.bias = sbuf(nc, ctx, f"bias_ff_{run}", [P, NH + 16])
        self.shares = sbuf(nc, ctx, f"shares_{run}", [P, EXPERTS])

    def bias_of(self, name, k):
        at = NH + 2 * ("Wr", "Wv", "WsW2", "W1").index(name) + k
        return self.bias[:, at:at + 1]


def prepare_ff(core, ff, dram):
    nc, banks = core.nc, core.banks
    RING = 4
    with ExitStack() as ctx:
        sem = lambda name: ctx.enter_context(nc.semaphore(f"{name}_{ff.run}"))
        buf = lambda name, shape: sbuf(nc, ctx, f"{name}_{ff.run}", shape)
        raw = buf("raw", [P, RING, HID])
        norms = buf("norms", [P, 4, CT])
        wsT, w2 = (buf(n, [P, CT, C]) for n in ("wsT", "w2"))
        product = buf("ws_w2", [P, CT, C])
        router = buf("router_raw", [P, CT, 8])
        offsets = buf("ln2_offsets", [P, CT, P])
        loaded = [sem(f"raw_loaded{r}") for r in range(RING)]
        small_loaded, hi_done, lo_done, used, offsets_done = map(
            sem, ("small_loaded", "w_hi_done", "w_lo_done", "w_biases_done", "offsets_done"))
        pieces = []
        halves = lambda tile, e, k: [w[:, e, k, :] for w in tile]
        for e in range(2):
            for k in range(CT):
                pieces.append((dram["K_rwkv"][e, k * P:(k + 1) * P, :], halves(ff.k, e, k), [(2, k, 0, HID)],
                               [(e * HT + s, s * P, k) for s in range(HT)]))
        for name, norm in (("Wr", 0), ("Wv", 0), ("W1", 2)):
            at = NH + 2 * ("Wr", "Wv", "WsW2", "W1").index(name)
            pieces.append((dram[name].rearrange("(k p) n -> p k n", p=P), [w[:].rearrange("p k n -> p (k n)") for w in ff.square[name]],
                           [(norm, k, k * C, C) for k in range(CT)],
                           [(at + o, k * C + o * P, k) for o in range(CT) for k in range(CT)]))
        for name in ("Wo", "W3"):
            pieces.append((dram[name].rearrange("(k p) n -> p k n", p=P), [w[:].rearrange("p k n -> p (k n)") for w in ff.square[name]],
                           [(None, None, 0, CT * C)], []))
        for e in range(2):
            for half in range(2):
                rows = slice(half * HID // 2, (half + 1) * HID // 2)
                tiles = slice(half * HT // 2, (half + 1) * HT // 2)
                pieces.append((dram["V_rwkv"][e, rows, :].rearrange("(s p) c -> p s c", p=P),
                               [w[:, e, tiles, :].rearrange("p s c -> p (s c)") for w in ff.v], [(None, None, 0, HID)], []))
        fills = Fills(banks, [(("product",), 0), (("bias",), 1), (("router",), 2)])
        biased = sum(1 for piece in pieces if piece[3])
        width = lambda piece: sum(part[3] for part in piece[2])
        norm_of = lambda norm, k: norms[:, norm, k:k + 1]
        parts = [(n, part) for n, piece in enumerate(pieces) for part in piece[2]]
        last_part = [max(i for i, (m, _) in enumerate(parts) if m == n) for n in range(len(pieces))]

        with nc.Block() as block:

            @block.sync
            def _(sp):
                for n, piece in enumerate(pieces):
                    if n >= RING:
                        sp.wait_ge(lo_done, last_part[n - RING] + 1)
                        sp.wait_ge(used, min(n - RING + 1, biased))
                    dst = raw[:, n % RING, 0:width(piece)]
                    if len(piece[0].shape) == 3:
                        dst = dst.rearrange("p (k n) -> p k n", k=piece[0].shape[1])
                    sp.dma_start(dst, piece[0]).then_inc(loaded[n % RING], 16)

            @block.gpsimd
            def _(pool):
                for n, name in enumerate(("ln1_w", "ln1_b", "ln2_w", "ln2_b")):
                    pool.dma_start(norms[:, n, :], dram[name]).then_inc(small_loaded, 16)
                for dst, name in ((wsT, "WsT"), (w2, "W2"), (router, "router")):
                    pool.dma_start(dst[:], dram[name].rearrange("(k p) n -> p k n", p=P)).then_inc(small_loaded, 16)
                pool.dma_start(ff.shares[:], dram["capital_shares"].partition_broadcast(P)).then_inc(small_loaded, 16)
                pool.wait_ge(small_loaded, 8 * 16)

            @block.scalar
            def _(act):
                act.wait_ge(small_loaded, 8 * 16)
                for i, (n, (norm, k, at, size)) in enumerate(parts):
                    act.wait_ge(loaded[n % RING], 16 * (n // RING + 1))
                    scale = 1.0 if norm is None else norm_of(norm, k)
                    nc.scalar.activation(pieces[n][1][0][:, at:at + size], raw[:, n % RING, at:at + size], ACT.Copy, scale=scale).then_inc(
                        hi_done, 1)
                act.wait_ge(*fills.full(0, "product"))
                nc.scalar.activation(product[:].rearrange("p k n -> p (k n)"), fills.data("product")[:], ACT.Copy).then_inc(fills.released("product"), 1)
                act.wait_ge(*fills.read(0, "product"))
                for k in range(CT):
                    nc.scalar.activation(ff.square["WsW2"][0][:, k, :], product[:, k, :], ACT.Copy, scale=norm_of(0, k)).then_inc(hi_done, 1)
                for k in range(CT):
                    nc.scalar.activation(ff.router[0][:, k, :], router[:, k, :], ACT.Copy, scale=norm_of(2, k)).then_inc(hi_done, 1)
                for name, at, size in (("bias", 0, NH + 8), ("router", NH + 8, 8)):
                    act.wait_ge(*fills.full(0, name))
                    nc.scalar.activation(ff.bias[:, at:at + size], fills.data(name)[:, 0:size], ACT.Copy).then_inc(fills.released(name), 1)
                    act.wait_ge(*fills.read(0, name))

            @block.vector
            def _(dve):
                def rest(hi, lo, src, norm, k):
                    nc.vector.scalar_tensor_tensor(out=lo, in0=src, scalar=1.0 if norm is None else norm_of(norm, k),
                                                   in1=hi.bitcast(F32), op0=ALU.mult, op1=ALU.subtract).then_inc(lo_done, 1)

                dve.wait_ge(small_loaded, 8 * 16)
                for k in range(CT):
                    nc.vector.tensor_scalar(offsets[:, k, :], core.ident[:], 0.0, norm_of(3, k), ALU.mult, ALU.add).then_inc(offsets_done, 1)
                for i, (n, (norm, k, at, size)) in enumerate(parts):
                    dve.wait_ge(hi_done, i + 1)
                    hi, lo = (w[:, at:at + size] for w in pieces[n][1])
                    rest(hi, lo, raw[:, n % RING, at:at + size], norm, k)
                for k in range(CT):
                    dve.wait_ge(hi_done, len(parts) + k + 1)
                    rest(*(w[:, k, :] for w in ff.square["WsW2"]), product[:, k, :], 0, k)
                for k in range(CT):
                    dve.wait_ge(hi_done, len(parts) + CT + k + 1)
                    rest(*(w[:, k, :] for w in ff.router), router[:, k, :], 2, k)
                dve.wait_ge(lo_done, len(parts) + 2 * CT)

            @block.tensor
            def _(pe):
                pe.wait_ge(small_loaded, 8 * 16)
                pe.wait_ge(*fills.free(0, "product"))
                for o in range(CT):
                    for k in range(CT):
                        last = nc.tensor.matmul(fills.data("product")[:, o * C:(o + 1) * C], wsT[:, k, o * P:(o + 1) * P], w2[:, k, :],
                                                start=k == 0, stop=k == CT - 1)
                last.then_inc(fills.filled("product"), 1)
                pe.wait_ge(offsets_done, CT)
                pe.wait_ge(*fills.free(0, "router"))
                for k in range(CT):
                    last = nc.tensor.matmul(fills.data("router")[:, 0:8], offsets[:, k, :], router[:, k, :], start=k == 0, stop=k == CT - 1)
                last.then_inc(fills.filled("router"), 1)
                pe.wait_ge(*fills.free(0, "bias"))
                data = fills.data("bias")
                first = True
                for n, piece in enumerate(pieces[:biased]):
                    pe.wait_ge(loaded[n % RING], 16 * (n // RING + 1))
                    norm = piece[2][0][0]
                    for column, at, k in piece[3]:
                        last = nc.tensor.matmul(data[:, column:column + 1], raw[:, n % RING, at:at + P], norm_of(norm + 1, k),
                                                start=first, stop=False, skip_group_check=True)
                        first = False
                    last.then_inc(used, 1)
                pe.wait_ge(*fills.read(0, "product"))
                at = NH + 2 * 2
                for o in range(CT):
                    for k in range(CT):
                        last = nc.tensor.matmul(data[:, at + o:at + o + 1], product[:, k, o * P:(o + 1) * P], norm_of(1, k),
                                                start=False, stop=k == CT - 1, skip_group_check=True)
                last.then_inc(fills.filled("bias"), 1)


TURN_SLOT, R_SLOT, V_SLOT, S_SLOT, ATT_SLOT, TURN2_SLOT = 3, 4, 5, 7, 9, 13
W3_SLOT = 3
AHEAD = 2
SQ_RING = AHEAD + 1


def feed_forward(core, ff, out_dram=None):
    nc, banks, x = core.nc, core.banks, core.x
    with ExitStack() as ctx:
        sem = lambda name: ctx.enter_context(nc.semaphore(f"{name}_{ff.run}"))
        buf = lambda name, shape, dtype=F32: sbuf(nc, ctx, f"{name}_{ff.run}", shape, dtype)
        split = lambda name, shape: [buf(f"{name}_{part}", shape, F32R) for part in ("hi", "lo")]
        stats, mv = buf("f_stats", [P, TT, 6]), buf("f_mv", [P, TT, 2])
        stats2, mv2 = buf("f_stats2", [P, TT, 6]), buf("f_mv2", [P, TT, 2])
        var1, rstd, part, part2, var2, rstd2, both = (
            buf(n, [P, TT]) for n in ("f_var1", "f_rstd", "f_part", "f_part2", "f_var2", "f_rstd2", "f_both"))
        var3, rstd3 = buf("f_var3", [P, TT]), buf("f_rstd3", [P, TT])
        xn, xq, x1 = (buf(n, [P, TT, C]) for n in ("f_xn", "f_xq", "f_x1"))
        hq = xq
        xT, hT, gT = (split(n, [P, CT, T]) for n in ("f_xT", "f_hT", "f_gT"))
        tT = gT
        gate, gate2, g = (buf(n, [P, CT, T]) for n in ("f_gate", "f_gate2", "f_g"))
        r, sq = buf("f_relu", [P, 2, T]), buf("f_square", [P, 2, T])
        h2 = split("f_hidden", [P, SQ_RING, T])
        logits, sig = buf("f_logits", [P, TT, 8]), buf("f_sig", [P, TT, 4])
        bids, win, one, conf = (buf(n, [P, TT, EXPERTS]) for n in ("f_bids", "f_win", "f_one", "f_conf"))
        top, wc, wc_eps, rcp, both_off = (buf(n, [P, TT]) for n in ("f_top", "f_wc", "f_wc_eps", "f_rcp", "f_taken"))
        coef = buf("f_coef", [P, TT, EXPERTS])
        names = ("stats_done", "mv_done", "norm_steps", "xn_done", "xq_done", "xT_hi", "gate_done", "gate2_done", "g_done", "g_hi", "g_lo",
                 "x1_done", "x1_added", "stats2_done", "mv2_done", "norm2_steps", "hq_done", "hT_hi", "t_done", "t_hi", "t_lo",
                 "square_hi", "square_done", "hidden_done", "route_steps", "sig_done", "x_steps")
        s = {n: sem("f_" + n) for n in names}
        stored = sem("stored")
        NORM_STEPS, ROUTE_STEPS = 7, 14
        X_STEPS = EXPERTS * TT

        def front_order():
            yield TURN_SLOT, [("xT", k) for k in range(CT)]
            yield R_SLOT, [("r", k) for k in range(CT)]
            for k in range(CT):
                yield V_SLOT + k, [("v", k)]
            for k in range(CT):
                yield S_SLOT + k, [("s", k)]
            yield ATT_SLOT, [("att", k) for k in range(2)]
            yield TURN2_SLOT, [("hT", k) for k in range(CT)]

        in_slot = dict(front_order())

        def place(heavy, front):
            order, side = [], 0
            names = [("u", 0), ("u", 1), ("route",)] if heavy else []
            for slot in range(NH):
                names += in_slot.get(slot, []) if front else []
            for n in names:
                order.append((n, 6 + side % 2))
                side += 1
            if heavy:
                order += [(("h", t), t % 2) for t in range(NH)]
                order += [(("w3", k), 4 + k) for k in range(2)]
                order += [(("e", e, k), 2 + 2 * e + k) for e in range(2) for k in range(2)]
            return order

        first = Fills(banks, place(False, True))
        loop = Fills(banks, place(True, True), B - 1)
        last_fills = Fills(banks, place(True, False))

        def rounds(eng, front, heavy):
            for slot in range(NH):
                front(first, 0, 0, slot)
            with eng.Fori(0, B - 1) as it:
                heavy(loop, it, it, -1)
                for slot in range(NH):
                    heavy(loop, it, it, slot)
                    front(loop, it, it + 1, slot)
            heavy(last_fills, 0, B - 1, -1)
            for slot in range(NH):
                heavy(last_fills, 0, B - 1, slot)

        with nc.Block() as block:

            if out_dram is not None:
                @block.sync
                def _(sp):
                    with sp.Fori(0, B) as it:
                        sp.wait_ge(s["x_steps"], it * X_STEPS + X_STEPS)
                        sp.dma_start(out_dram[bass.ds(it * T, T), :].rearrange("(t p) c -> p t c", p=P),
                                     cols(x, it * XB, XB).rearrange("p (t c) -> p t c", c=C)).then_inc(stored, 16)
                    sp.wait_ge(stored, 16 * B)

            @block.vector
            def _(dve):
                def two_parts(fl, it, name, hi_sem, count, hi, lo, done=None):
                    dve.wait_ge(hi_sem, count)
                    core.met(dve, "dve")
                    nc.vector.tensor_tensor(lo, fl.data(*name)[:], hi.bitcast(F32), ALU.subtract).then_inc(fl.released(*name), 1)

                def front(fl, it, n, slot):
                    if slot == 0:
                        dve.wait_ge(s["norm_steps"], n * NORM_STEPS)
                        core.met(dve, "dve")
                        for t in range(TT):
                            nc.vector.bn_stats(stats[:, t, :], cols(x, n * XB + t * C, C)).then_inc(s["stats_done"], 1)
                        for t in range(TT):
                            dve.wait_ge(s["stats_done"], n * TT + t + 1)
                            core.met(dve, "dve")
                            nc.vector.bn_aggr(mv[:, t, :], stats[:, t, :]).then_inc(s["mv_done"], 1)
                    if slot == 2:
                        dve.wait_ge(s["norm_steps"], n * NORM_STEPS + NORM_STEPS)
                        core.met(dve, "dve")
                        for t in range(TT):
                            xs = cols(x, n * XB + t * C, C)
                            nc.vector.tensor_scalar(xq[:, t, :], xs, mv[:, t, 0:1], both[:, t:t + 1], ALU.subtract, ALU.mult).then_inc(
                                s["xq_done"], 1)
                        for t in range(TT):
                            xs = cols(x, n * XB + t * C, C)
                            nc.vector.tensor_scalar(xn[:, t, :], xs, mv[:, t, 0:1], rstd[:, t:t + 1], ALU.subtract, ALU.mult).then_inc(
                                s["xn_done"], 1)
                    if slot == TURN_SLOT:
                        for k in range(CT):
                            two_parts(fl, it, ("xT", k), s["xT_hi"], n * CT + k + 1, xT[0][:, k], xT[1][:, k])
                    for k in range(CT):
                        if slot == V_SLOT + k:
                            dve.wait_ge(*fl.full(it, "v", k))
                            dve.wait_ge(s["gate_done"], n * CT + k + 1)
                            core.met(dve, "dve")
                            nc.vector.scalar_tensor_tensor(out=g[:, k], in0=fl.data("v", k)[:], scalar=ff.bias_of("Wv", k), in1=gate[:, k],
                                                           op0=ALU.add, op1=ALU.mult).then_inc(fl.released("v", k), 1)
                        if slot == V_SLOT + k + 1:
                            dve.wait_ge(s["g_hi"], n * CT + k + 1)
                            core.met(dve, "dve")
                            nc.vector.tensor_tensor(gT[1][:, k], g[:, k], gT[0][:, k].bitcast(F32), ALU.subtract).then_inc(s["g_lo"], 1)
                    if slot == ATT_SLOT:
                        dve.wait_ge(s["xn_done"], n * TT + TT)
                        dve.wait_ge(s["x1_added"], n * 2)
                        for k in range(2):
                            dve.wait_ge(*fl.full(it, "att", k))
                            core.met(dve, "dve")
                            nc.vector.tensor_tensor(x1[:, 2 * k:2 * k + 2, :], xn[:, 2 * k:2 * k + 2, :],
                                                    fl.data("att", k)[:].rearrange("p (t c) -> p t c", c=C), ALU.add).then_inc(
                                fl.released("att", k), 1)
                        for t in range(TT):
                            dve.wait_ge(*fl.read(it, "att", t // 2))
                            core.met(dve, "dve")
                            nc.vector.bn_stats(stats2[:, t, :], x1[:, t, :]).then_inc(s["stats2_done"], 1)
                        for t in range(TT):
                            dve.wait_ge(s["stats2_done"], n * TT + t + 1)
                            core.met(dve, "dve")
                            nc.vector.bn_aggr(mv2[:, t, :], stats2[:, t, :]).then_inc(s["mv2_done"], 1)
                    if slot == TURN2_SLOT - 1:
                        dve.wait_ge(s["norm2_steps"], n * 2 + 2)
                        core.met(dve, "dve")
                        for t in range(TT):
                            nc.vector.tensor_scalar(hq[:, t, :], x1[:, t, :], mv2[:, t, 0:1], rstd3[:, t:t + 1], ALU.subtract,
                                                    ALU.mult).then_inc(s["hq_done"], 1)
                    if slot == TURN2_SLOT:
                        for k in range(CT):
                            dve.wait_ge(s["hT_hi"], n * CT + k + 1)
                            core.met(dve, "dve")
                            nc.vector.tensor_tensor(hT[1][:, k], fl.data("hT", k)[:], hT[0][:, k].bitcast(F32), ALU.subtract).then_inc(
                                fl.released("hT", k), 1)

                def add_expert(fl, it, i, e, name, step):
                    dve.wait_ge(s["route_steps"], i * ROUTE_STEPS + ROUTE_STEPS)
                    if step == 0:
                        dve.wait_ge(s["x1_added"], i * 2 + 2)
                    else:
                        dve.wait_ge(s["x_steps"], i * X_STEPS + step * TT)
                    for t in range(TT):
                        bank = (*name, t // 2)
                        dve.wait_ge(*fl.full(it, *bank))
                        core.met(dve, "dve")
                        xs = cols(x, i * XB + t * C, C)
                        nc.vector.scalar_tensor_tensor(out=xs, in0=fl.data(*bank)[:, t % 2 * C:(t % 2 + 1) * C],
                                                       scalar=coef[:, t, e:e + 1], in1=xs, op0=ALU.mult, op1=ALU.add).then_inc(
                            s["x_steps"], 1)
                        if t % 2 == 1:
                            dve.wait_ge(s["x_steps"], i * X_STEPS + step * TT + t + 1)
                            dve.sem_inc(fl.released(*bank), 1)

                def route_logits(fl, it, i):
                    dve.wait_ge(*fl.full(it, "route"))
                    core.met(dve, "dve")
                    nc.vector.tensor_tensor(logits[:], fl.data("route")[:, 0:TT * 8].rearrange("p (t e) -> p t e", e=8),
                                            ff.bias[:, NH + 8:NH + 16].unsqueeze(1).to_broadcast([P, TT, 8]), ALU.add).then_inc(
                        fl.released("route"), 1)

                def route(fl, it, i):
                    step = 0

                    def after(instruction):
                        nonlocal step
                        step += 1
                        instruction.then_inc(s["route_steps"], 1)
                        dve.wait_ge(s["route_steps"], i * ROUTE_STEPS + step)
                        core.met(dve, "dve")

                    dve.wait_ge(s["sig_done"], i + 1)
                    core.met(dve, "dve")
                    v = nc.vector
                    spread = lambda ap: ap.unsqueeze(2).to_broadcast([P, TT, EXPERTS])
                    conf_now = sig[:, :, 0:EXPERTS]
                    after(v.tensor_tensor(bids[:], conf_now, ff.shares[:].unsqueeze(1).to_broadcast([P, TT, EXPERTS]), ALU.mult))
                    after(v.tensor_tensor(bids[:], bids[:], spread(sig[:, :, 3]), ALU.mult))
                    after(v.tensor_tensor(bids[:], bids[:], logits[:, :, 4:7], ALU.add))
                    after(v.tensor_reduce(top[:], bids[:], AX_X, ALU.max))
                    after(v.tensor_tensor(win[:], bids[:], spread(top[:]), ALU.is_ge))
                    after(v.tensor_scalar(one[:, :, 0], win[:, :, 0], 1.0, None, ALU.mult))
                    after(v.tensor_tensor(one[:, :, 1], win[:, :, 1], win[:, :, 0], ALU.is_gt))
                    after(v.tensor_tensor(both_off[:], win[:, :, 0], win[:, :, 1], ALU.max))
                    after(v.tensor_tensor(one[:, :, 2], win[:, :, 2], both_off[:], ALU.is_gt))
                    after(v.tensor_tensor(conf[:], one[:], conf_now, ALU.mult))
                    after(v.tensor_reduce(wc[:], conf[:], AX_X, ALU.add))
                    after(v.tensor_scalar(wc_eps[:], wc[:], 1e-6, None, ALU.add))
                    after(v.reciprocal(rcp[:], wc_eps[:]))
                    after(v.tensor_tensor(coef[:], conf[:], spread(rcp[:]), ALU.mult))

                def heavy(fl, it, i, slot):
                    if slot + 1 < NH:
                        t = slot + 1
                        dve.wait_ge(s["square_hi"], i * NH + t + 1)
                        dve.wait_ge(s["square_done"], i * NH + t + 1)
                        core.met(dve, "dve")
                        nc.vector.tensor_tensor(h2[1][:, t % SQ_RING], sq[:, t % 2], h2[0][:, t % SQ_RING].bitcast(F32),
                                                ALU.subtract).then_inc(s["hidden_done"], 1)
                    if slot == 0:
                        for k in range(CT):
                            dve.wait_ge(*fl.full(it, "u", k))
                            dve.wait_ge(s["gate2_done"], i * CT + k + 1)
                            core.met(dve, "dve")
                            nc.vector.scalar_tensor_tensor(out=g[:, k], in0=fl.data("u", k)[:], scalar=ff.bias_of("W1", k), in1=gate2[:, k],
                                                           op0=ALU.add, op1=ALU.mult).then_inc(fl.released("u", k), 1)
                    if slot == 1:
                        route_logits(fl, it, i)
                        for k in range(CT):
                            dve.wait_ge(s["t_hi"], i * CT + k + 1)
                            core.met(dve, "dve")
                            nc.vector.tensor_tensor(tT[1][:, k], g[:, k], tT[0][:, k].bitcast(F32), ALU.subtract).then_inc(s["t_lo"], 1)
                    if slot == 3:
                        route(fl, it, i)
                    if slot == W3_SLOT + 1:
                        add_expert(fl, it, i, 2, ("w3",), 0)
                    if slot == HT:
                        add_expert(fl, it, i, 0, ("e", 0), 1)
                    if slot == NH - 1:
                        add_expert(fl, it, i, 1, ("e", 1), 2)

                rounds(dve, front, heavy)

            @block.gpsimd
            def _(pool):
                def front(fl, it, n, slot):
                    g_ = nc.gpsimd
                    if slot == 0:
                        step = 0

                        def after(instruction):
                            nonlocal step
                            step += 1
                            instruction.then_inc(s["norm_steps"], 1)
                            pool.wait_ge(s["norm_steps"], n * NORM_STEPS + step)
                            core.met(pool, "pool")

                        pool.wait_ge(s["mv_done"], n * TT + TT)
                        pool.wait_ge(s["xn_done"], n * TT)
                        core.met(pool, "pool")
                        after(g_.tensor_scalar(var1[:], mv[:, :, 1], EPS, None, ALU.add))
                        after(g_.tensor_tensor(rstd[:], var1[:], core.neg_half[:], ALU.pow))
                        after(g_.tensor_tensor(part[:], mv[:, :, 1], rstd[:], ALU.mult))
                        after(g_.tensor_tensor(part2[:], part[:], rstd[:], ALU.mult))
                        after(g_.tensor_scalar(var2[:], part2[:], EPS, None, ALU.add))
                        after(g_.tensor_tensor(rstd2[:], var2[:], core.neg_half[:], ALU.pow))
                        after(g_.tensor_tensor(both[:], rstd[:], rstd2[:], ALU.mult))
                    if slot == ATT_SLOT + 1:
                        pool.wait_ge(s["mv2_done"], n * TT + TT)
                        pool.wait_ge(s["hq_done"], n * TT)
                        core.met(pool, "pool")
                        g_.tensor_scalar(var3[:], mv2[:, :, 1], EPS, None, ALU.add).then_inc(s["norm2_steps"], 1)
                        pool.wait_ge(s["norm2_steps"], n * 2 + 1)
                        core.met(pool, "pool")
                        g_.tensor_tensor(rstd3[:], var3[:], core.neg_half[:], ALU.pow).then_inc(s["norm2_steps"], 1)
                        pool.wait_ge(s["xn_done"], n * TT + TT)
                        for k in range(2):
                            pool.wait_ge(*fl.read(it, "att", k))
                            core.met(pool, "pool")
                            xs = cols(x, n * XB + k * 512, 512)
                            g_.tensor_tensor(xs, xs, x1[:, 2 * k:2 * k + 2, :].rearrange("p t c -> p (t c)"), ALU.add).then_inc(s["x1_added"], 1)

                def square(fl, it, i, t):
                    pool.wait_ge(*fl.read(it, "h", t))
                    if t >= 2:
                        pool.wait_ge(s["hidden_done"], i * NH + t - 1)
                    core.met(pool, "pool")
                    nc.gpsimd.tensor_tensor(sq[:, t % 2], r[:, t % 2], r[:, t % 2], ALU.mult).then_inc(s["square_done"], 1)

                def heavy(fl, it, i, slot):
                    for t in range(AHEAD) if slot == -1 else [slot + AHEAD]:
                        if t < NH:
                            square(fl, it, i, t)

                rounds(pool, front, heavy)

            @block.scalar
            def _(act):
                def first_part(fl, it, name, dst, done):
                    act.wait_ge(*fl.full(it, *name))
                    nc.scalar.activation(dst, fl.data(*name)[:], ACT.Copy).then_inc(done, 1)

                def gated(fl, it, name, dst, bias, done):
                    act.wait_ge(*fl.full(it, *name))
                    nc.scalar.activation(dst, fl.data(*name)[:], ACT.Sigmoid, bias=bias).then_inc(fl.released(*name), 1)
                    act.wait_ge(*fl.read(it, *name))
                    act.sem_inc(done, 1)

                def front(fl, it, n, slot):
                    if slot == TURN_SLOT:
                        for k in range(CT):
                            first_part(fl, it, ("xT", k), xT[0][:, k], s["xT_hi"])
                    if slot == R_SLOT:
                        for k in range(CT):
                            gated(fl, it, ("r", k), gate[:, k], ff.bias_of("Wr", k), s["gate_done"])
                    for k in range(CT):
                        if slot == V_SLOT + k:
                            act.wait_ge(*fl.read(it, "v", k))
                            nc.scalar.activation(gT[0][:, k], g[:, k], ACT.Copy).then_inc(s["g_hi"], 1)
                        if slot == S_SLOT + k:
                            gated(fl, it, ("s", k), gate2[:, k], ff.bias_of("WsW2", k), s["gate2_done"])
                    if slot == TURN2_SLOT:
                        for k in range(CT):
                            first_part(fl, it, ("hT", k), hT[0][:, k], s["hT_hi"])

                def hidden(fl, it, i, t):
                    if t >= 2:
                        act.wait_ge(s["square_done"], i * NH + t - 1)
                    act.wait_ge(*fl.full(it, "h", t))
                    nc.scalar.activation(r[:, t % 2], fl.data("h", t)[:], ACT.Relu, bias=ff.bias[:, t:t + 1]).then_inc(fl.released("h", t), 1)
                    act.wait_ge(*fl.read(it, "h", t))
                    nc.scalar.activation(h2[0][:, t % SQ_RING], r[:, t % 2], ACT.Square).then_inc(s["square_hi"], 1)

                def heavy(fl, it, i, slot):
                    if slot == -1:
                        for t in range(AHEAD):
                            hidden(fl, it, i, t)
                    elif slot + AHEAD < NH:
                        hidden(fl, it, i, slot + AHEAD)
                    if slot == 0:
                        for k in range(CT):
                            act.wait_ge(*fl.read(it, "u", k))
                            nc.scalar.activation(tT[0][:, k], g[:, k], ACT.Copy).then_inc(s["t_hi"], 1)
                    if slot == 2:
                        act.wait_ge(*fl.read(it, "route"))
                        nc.scalar.activation(sig[:], logits[:, :, 0:4], ACT.Sigmoid).then_inc(s["sig_done"], 1)

                rounds(act, front, heavy)

            @block.tensor
            def _(pe):
                def begin(fl, it, *name):
                    pe.wait_ge(*fl.free(it, *name))
                    core.met(pe, "pe")
                    return fl.data(*name)

                PASSES = ((0, 0), (0, 1), (1, 0))

                def to_features(fl, it, name, weight, src, o):
                    data = begin(fl, it, *name)
                    steps = [(k, a, b) for k in range(CT) for a, b in PASSES]
                    for n, (k, a, b) in enumerate(steps):
                        last = nc.tensor.matmul(data[:], weight[a](k, o), src[b][:, k], start=n == 0, stop=n == len(steps) - 1)
                    last.then_inc(fl.filled(*name), 1)

                square = lambda name: [lambda k, o, w=w: w[:, k, o * P:(o + 1) * P] for w in ff.square[name]]

                def to_tokens(fl, it, name, src, weight):
                    steps = [(k, a, b) for k in range(CT) for a, b in PASSES]
                    for bank in range(2):
                        data = begin(fl, it, name, bank)
                        for t in (2 * bank, 2 * bank + 1):
                            for n, (k, a, b) in enumerate(steps):
                                last = nc.tensor.matmul(data[:, t % 2 * C:(t % 2 + 1) * C], src[a][:, k, t * P:(t + 1) * P],
                                                        ff.square[weight][b][:, k, :], start=n == 0, stop=n == len(steps) - 1)
                        last.then_inc(fl.filled(name, bank), 1)

                def turn(fl, it, name, src):
                    for k in range(CT):
                        data = begin(fl, it, name, k)
                        for t in range(TT):
                            last = nc.tensor.transpose(data[:, t * P:(t + 1) * P], src[:, t, k * P:(k + 1) * P], core.ident[:])
                        last.then_inc(fl.filled(name, k), 1)

                def front(fl, it, n, slot):
                    if slot == TURN_SLOT:
                        pe.wait_ge(s["xq_done"], n * TT + TT)
                        turn(fl, it, "xT", xq)
                    if slot == R_SLOT:
                        for k in range(CT):
                            pe.wait_ge(*fl.read(it, "xT", k))
                        for k in range(CT):
                            to_features(fl, it, ("r", k), square("Wr"), xT, k)
                    for k in range(CT):
                        if slot == V_SLOT + k:
                            to_features(fl, it, ("v", k), square("Wv"), xT, k)
                        if slot == S_SLOT + k:
                            to_features(fl, it, ("s", k), square("WsW2"), xT, k)
                    if slot == ATT_SLOT:
                        pe.wait_ge(s["g_lo"], n * CT + CT)
                        to_tokens(fl, it, "att", gT, "Wo")
                    if slot == TURN2_SLOT:
                        pe.wait_ge(s["hq_done"], n * TT + TT)
                        turn(fl, it, "hT", hq)
                    if slot == NH - 1:
                        for k in range(CT):
                            pe.wait_ge(*fl.read(it, "hT", k))
                        core.met(pe, "pe")

                def hidden(fl, it, t):
                    e, c = t // HT, t % HT
                    to_features(fl, it, ("h", t), [lambda k, o, w=w: w[:, e, k, c * P:(c + 1) * P] for w in ff.k], hT, 0)

                def second(fl, it, i, t):
                    e, c = t // HT, t % HT
                    pe.wait_ge(s["hidden_done"], i * NH + t + 1)
                    if c == 0:
                        for bank in range(2):
                            begin(fl, it, "e", e, bank)
                    core.met(pe, "pe")
                    for tok in range(TT):
                        for n, (a, b) in enumerate(PASSES):
                            last = nc.tensor.matmul(
                                fl.data("e", e, tok // 2)[:, tok % 2 * C:(tok % 2 + 1) * C], h2[a][:, t % SQ_RING, tok * P:(tok + 1) * P],
                                ff.v[b][:, e, c, :], start=c == 0 and n == 0 and tok % 2 == 0, stop=c == HT - 1 and n == 2,
                                skip_group_check=True)
                        if c == HT - 1 and tok % 2 == 1:
                            last.then_inc(fl.filled("e", e, tok // 2), 1)

                def heavy(fl, it, i, slot):
                    if slot == -1:
                        for k in range(CT):
                            hidden(fl, it, k)
                            to_features(fl, it, ("u", k), square("W1"), hT, k)
                        return
                    if slot + AHEAD < NH:
                        hidden(fl, it, slot + AHEAD)
                    second(fl, it, i, slot)
                    if slot == 0:
                        data = begin(fl, it, "route")
                        steps = [(k, a, b) for k in range(CT) for a, b in PASSES]
                        for t in range(TT):
                            for n, (k, a, b) in enumerate(steps):
                                last = nc.tensor.matmul(data[:, t * 8:(t + 1) * 8], hT[a][:, k, t * P:(t + 1) * P], ff.router[b][:, k, :],
                                                        start=n == 0, stop=n == len(steps) - 1)
                        last.then_inc(fl.filled("route"), 1)
                    if slot == W3_SLOT:
                        pe.wait_ge(s["t_lo"], i * CT + CT)
                        to_tokens(fl, it, "w3", tT, "W3")

                rounds(pe, front, heavy)


NQUADS = HB // QUAD
PAIRS_B = HB // 2
PAIRS_T = PAIRS_B // CT
LAG = 2
SLOTS_B = HB + LAG + 4
XT_SLOT, QK0_SLOT, QK1_SLOT, V0_SLOT, SEL0_SLOT = 3, 6, 19, 18, 20
SCORES = ((0, 3, 0), (1, 2, 0), (1, 0, 3 * P), (2, 1, 0))
SCORE_COLS = {3: 0, 2: 4 * P, 0: 7 * P, 1: 8 * P}
TURNED = ((0, 0, 0), (1, 1, 0), (1, 3, 3 * P), (2, 2, 0))
TURNED_COLS = {0: 0, 1: 4 * P, 3: 7 * P, 2: 8 * P}
HEAD_COLS = 10 * P
BANK_COLS = ((0, 4 * P), (4 * P, 4 * P), (8 * P, 2 * P))


def layer_b(core, dram):
    nc, banks, x = core.nc, core.banks, core.x
    with ExitStack() as ctx:
        sem = lambda name: ctx.enter_context(nc.semaphore(name))
        buf = lambda name, shape, dtype=F32: sbuf(nc, ctx, name, shape, dtype)
        wq, wk, wv, wo = (buf(n, [P, CT, C]) for n in ("wq_b", "wk_b", "wv_b", "wo_b"))
        cos, sin = buf("cos", [P, T]), buf("sin", [P, T])
        select = buf("select", [P, 2, 2, PAIRS_T, P], F32R)
        ident16, causal16 = buf("ident16", [P, P], BF16), buf("causal16", [P, P], BF16)
        stats, mv, var1, rstd = buf("b_stats", [P, TT, 6]), buf("b_mv", [P, TT, 2]), buf("b_var", [P, TT]), buf("b_rstd", [P, TT])
        xn, xnT = buf("b_xn", [P, TT, C]), buf("b_xnT", [P, CT, T])
        straight, swapped, turned, rotated = (buf(n, [P, 2, T]) for n in ("b_straight", "b_swapped", "b_turned", "b_rotated"))
        qk = [[buf(f"b_{side}_{part}", [P, CT, T], F32R) for part in ("hi", "lo")] for side in ("q", "k")]
        stacked = [buf(f"b_{side}_stacked", [P, 2, T], F32R) for side in ("q", "k")]
        v = buf("b_v", [P, TT, HB, 2 * DB])
        probs = buf("b_probs", [P, LAG + 1, HEAD_COLS])
        probsT = buf("b_probsT", [P, 2 * QUAD, HEAD_COLS])
        neg_max = buf("b_neg_max", [P, 2, TT])
        oT = buf("b_oT", [P, 2, T])
        rcp, att, attT = buf("b_rcp", [P, TT, QUAD]), buf("b_att", [P, TT, C]), buf("b_attT", [P, CT, T])
        names = ("loaded", "consts_done", "ones_done", "stats_done", "mv_done", "var_done", "rstd_done", "xn_done", "swap_done", "turn_done", "rot_done",
                 "hi_done", "lo_done", "max_done", "rcp_done")
        s = {n: sem("b_" + n) for n in names}

        def fill_order(heavy, front):
            order, side = [], 0

            def add(name, b=None):
                nonlocal side
                if b is None:
                    b, side = 6 + side % 2, side + 1
                order.append((name, b))

            for slot in range(SLOTS_B):
                if heavy and slot < HB:
                    for b in range(3):
                        add(("s", slot, b), b)
                if heavy and LAG <= slot < HB + LAG:
                    for b in range(3):
                        add(("t", slot - LAG, b), 3 + b)
                if heavy and slot % 2 == 0 and slot // 2 + 1 < PAIRS_B:
                    for side_ in range(2):
                        add(("sel", side_, slot // 2 + 1))
                for quad in range(NQUADS):
                    if heavy and slot == QUAD * (quad + 1) + LAG:
                        add(("pv", quad))
                    if heavy and slot == QUAD * (quad + 1) + LAG + 1:
                        add(("o", quad))
                if heavy and slot == HB + LAG + 2:
                    for k in range(CT):
                        add(("attT", k), 3 + k)
                if heavy and slot == HB + LAG + 3:
                    for k in range(2):
                        add(("out", k), 3 + k)
                if front and slot == XT_SLOT:
                    for k in range(CT):
                        add(("xT", k))
                for f, at in ((0, QK0_SLOT), (1, QK1_SLOT)):
                    if front and slot == at:
                        for side_ in range(2):
                            add(("qk", side_, f))
                if front and slot == V0_SLOT:
                    for k in range(2):
                        add(("v", k))
                if front and slot == SEL0_SLOT:
                    for side_ in range(2):
                        add(("sel", side_, 0))
            return order

        with ExitStack() as setup:
            raw = sbuf(nc, setup, "b_raw", [P, 16 * P])
            raw_mask = sbuf(nc, setup, "b_raw_mask", [P, P])
            with nc.Block() as block:

                @block.sync
                def _(sp):
                    for dst, name in ((wq, "WqT"), (wk, "WkT"), (wv, "WvT"), (wo, "WoT")):
                        sp.dma_start(dst[:], dram[name].rearrange("(k p) n -> p k n", p=P)).then_inc(s["loaded"], 16)
                    for dst, name in ((cos, "cos"), (sin, "sin"), (raw, "select"), (raw_mask, "causal")):
                        sp.dma_start(dst[:], dram[name]).then_inc(s["loaded"], 16)
                    sp.wait_ge(s["loaded"], 8 * 16)

                @block.scalar
                def _(act):
                    act.wait_ge(s["loaded"], 8 * 16)
                    nc.scalar.activation(select[:].rearrange("p a b c d -> p (a b c d)"), raw[:], ACT.Copy).then_inc(s["consts_done"], 1)
                    nc.scalar.activation(ident16[:], core.ident[:], ACT.Copy).then_inc(s["consts_done"], 1)
                    nc.scalar.activation(causal16[:], raw_mask[:], ACT.Copy).then_inc(s["consts_done"], 1)
                    act.wait_ge(s["consts_done"], 3)

                @block.vector
                def _(dve):
                    nc.vector.memset(v[:, :, :, DB:], 0.0).then_inc(s["ones_done"], 1)
                    dve.wait_ge(s["ones_done"], 1)
                    nc.vector.memset(v[:, :, :, DB:DB + 1], 1.0).then_inc(s["ones_done"], 1)
                    dve.wait_ge(s["ones_done"], 2)

        first = Fills(banks, fill_order(False, True))
        loop = Fills(banks, fill_order(True, True), B - 1)
        last_fills = Fills(banks, fill_order(True, False))

        def rounds(eng, front, heavy):
            for slot in range(SLOTS_B):
                front(first, 0, 0, slot)
            with eng.Fori(0, B - 1) as it:
                for slot in range(SLOTS_B):
                    heavy(loop, it, it, slot)
                    front(loop, it, it + 1, slot)
            for slot in range(SLOTS_B):
                heavy(last_fills, 0, B - 1, slot)

        with nc.Block() as block:

            @block.vector
            def _(dve):
                def ready(*waits):
                    for wait in waits:
                        dve.wait_ge(*wait)
                    core.met(dve, "dve")

                def front(fl, it, n, slot):
                    if slot == 0:
                        ready((s["xn_done"], n * TT))
                        for t in range(TT):
                            nc.vector.bn_stats(stats[:, t, :], cols(x, n * XB + t * C, C)).then_inc(s["stats_done"], 1)
                        for t in range(TT):
                            ready((s["stats_done"], n * TT + t + 1))
                            nc.vector.bn_aggr(mv[:, t, :], stats[:, t, :]).then_inc(s["mv_done"], 1)
                    if slot == 2:
                        ready((s["rstd_done"], n + 1))
                        for t in range(TT):
                            nc.vector.tensor_scalar(xn[:, t, :], cols(x, n * XB + t * C, C), mv[:, t, 0:1], rstd[:, t:t + 1],
                                                    ALU.subtract, ALU.mult).then_inc(s["xn_done"], 1)
                    for f, at in ((0, QK0_SLOT), (1, QK1_SLOT)):
                        if slot == at:
                            for side in range(2):
                                ready(fl.full(it, "qk", side, f), (s["rot_done"], n * 4 + f * 2))
                                nc.vector.tensor_tensor(straight[:, side], fl.data("qk", side, f)[:], cos[:], ALU.mult)
                                nc.vector.stream_shuffle(swapped[:, side], fl.data("qk", side, f)[:], [i ^ 1 for i in range(32)]).then_inc(
                                    fl.released("qk", side, f), 1)

                def heavy(fl, it, i, slot):
                    if slot < HB:
                        for place, (b, t, at) in enumerate(SCORES):
                            ready(fl.full(it, "s", slot, b))
                            nc.vector.tensor_reduce(neg_max[:, slot % 2, place:place + 1], fl.data("s", slot, b)[:, at:at + (t + 1) * P],
                                                    AX_X, ALU.max, negate=True).then_inc(s["max_done"], 1)
                    if LAG <= slot < HB + LAG:
                        for b in (0, 2):
                            ready(fl.full(it, "t", slot - LAG, b))
                            at, size = BANK_COLS[b]
                            nc.vector.tensor_scalar(probsT[:, (slot - LAG) % (2 * QUAD), at:at + size], fl.data("t", slot - LAG, b)[:, 0:size],
                                                    1.0, None, ALU.mult).then_inc(fl.released("t", slot - LAG, b), 1)
                    for quad in range(NQUADS):
                        if slot == QUAD * (quad + 1) + LAG + 1:
                            ready(fl.full(it, "o", quad))
                            o = fl.data("o", quad)[:].rearrange("p (t h d) -> p t h d", t=TT, h=QUAD)
                            nc.vector.reciprocal(rcp[:], o[:, :, :, DB]).then_inc(s["rcp_done"], 1)
                            ready((s["rcp_done"], i * NQUADS + quad + 1))
                            nc.vector.tensor_tensor(
                                att[:, :, quad * QUAD * DB:(quad + 1) * QUAD * DB].rearrange("p t (h d) -> p t h d", h=QUAD),
                                o[:, :, :, 0:DB], rcp[:].unsqueeze(3).to_broadcast([P, TT, QUAD, DB]), ALU.mult).then_inc(
                                fl.released("o", quad), 1)
                    if slot == HB + LAG + 3:
                        for k in range(2):
                            ready(fl.full(it, "out", k))
                            xs = cols(x, i * XB + k * 512, 512)
                            nc.vector.tensor_tensor(xs, xs, fl.data("out", k)[:], ALU.add).then_inc(fl.released("out", k), 1)

                rounds(dve, front, heavy)

            @block.gpsimd
            def _(pool):
                def ready(*waits):
                    for wait in waits:
                        pool.wait_ge(*wait)
                    core.met(pool, "pool")

                def front(fl, it, n, slot):
                    g = nc.gpsimd
                    if slot == 1:
                        ready((s["mv_done"], n * TT + TT), (s["xn_done"], n * TT))
                        g.tensor_scalar(var1[:], mv[:, :, 1], EPS, None, ALU.add).then_inc(s["var_done"], 1)
                        ready((s["var_done"], n + 1))
                        g.tensor_tensor(rstd[:], var1[:], core.neg_half[:], ALU.pow).then_inc(s["rstd_done"], 1)
                    for f, at in ((0, QK0_SLOT), (1, QK1_SLOT)):
                        if slot == at:
                            for side in range(2):
                                step = n * 4 + f * 2 + side + 1
                                ready(fl.read(it, "qk", side, f), (s["lo_done"], n * 4 + f * 2))
                                g.tensor_tensor(turned[:, side], swapped[:, side], sin[:], ALU.mult).then_inc(s["turn_done"], 1)
                                ready((s["turn_done"], step))
                                g.tensor_tensor(rotated[:, side], straight[:, side], turned[:, side], ALU.add).then_inc(s["rot_done"], 1)
                            for side in range(2):
                                ready((s["hi_done"], n * 4 + f * 2 + side + 1))
                                hi, lo = qk[side]
                                g.tensor_tensor(lo[:, f], rotated[:, side], hi[:, f].bitcast(F32), ALU.subtract).then_inc(s["lo_done"], 1)

                def heavy(fl, it, i, slot):
                    pass

                rounds(pool, front, heavy)

            @block.scalar
            def _(act):
                def copy(fl, it, dst, name, size=T):
                    act.wait_ge(*fl.full(it, *name))
                    nc.scalar.activation(dst, fl.data(*name)[:, 0:size], ACT.Copy).then_inc(fl.released(*name), 1)

                def select_copies(fl, it, pair):
                    for side in range(2):
                        copy(fl, it, stacked[side][:, pair % 2], ("sel", side, pair))

                def front(fl, it, n, slot):
                    if slot == XT_SLOT:
                        for k in range(CT):
                            copy(fl, it, xnT[:, k], ("xT", k))
                    for f, at in ((0, QK0_SLOT + 2), (1, QK1_SLOT + 2)):
                        if slot == at:
                            for side in range(2):
                                act.wait_ge(s["rot_done"], n * 4 + f * 2 + side + 1)
                                nc.scalar.activation(qk[side][0][:, f], rotated[:, side], ACT.Copy).then_inc(s["hi_done"], 1)
                    if slot == V0_SLOT:
                        for k in range(2):
                            act.wait_ge(*fl.full(it, "v", k))
                            for t in range(2):
                                done = nc.scalar.activation(v[:, 2 * k + t, :, 0:DB],
                                                            fl.data("v", k)[:, t * C:(t + 1) * C].rearrange("p (h d) -> p h d", d=DB), ACT.Copy)
                            done.then_inc(fl.released("v", k), 1)
                    if slot == SEL0_SLOT:
                        select_copies(fl, it, 0)

                def heavy(fl, it, i, slot):
                    if slot < HB:
                        h = slot
                        for place, (b, t, at) in enumerate(SCORES):
                            size, to = (t + 1) * P, SCORE_COLS[t]
                            act.wait_ge(s["max_done"], i * HB * TT + h * TT + (1, 3, 3, 4)[place])
                            done = nc.scalar.activation(probs[:, h % (LAG + 1), to:to + size], fl.data("s", h, b)[:, at:at + size], ACT.Exp,
                                                        bias=neg_max[:, h % 2, place:place + 1])
                            if place != 1:
                                done.then_inc(fl.released("s", h, b), 1)
                    if LAG <= slot < HB + LAG:
                        at, size = BANK_COLS[1]
                        copy(fl, it, probsT[:, (slot - LAG) % (2 * QUAD), at:at + size], ("t", slot - LAG, 1), size)
                    if slot % 2 == 0 and slot // 2 + 1 < PAIRS_B:
                        select_copies(fl, it, slot // 2 + 1)
                    for quad in range(NQUADS):
                        if slot == QUAD * (quad + 1) + LAG:
                            copy(fl, it, oT[:, quad % 2], ("pv", quad))
                    if slot == HB + LAG + 2:
                        for k in range(CT):
                            copy(fl, it, attT[:, k], ("attT", k))

                rounds(act, front, heavy)

            @block.tensor
            def _(pe):
                def begin(fl, it, *name):
                    pe.wait_ge(*fl.free(it, *name))
                    core.met(pe, "pe")
                    return fl.data(*name)

                def stack(fl, it, pair):
                    f, j = pair // PAIRS_T, pair % PAIRS_T
                    for side in range(2):
                        data = begin(fl, it, "sel", side, pair)
                        for part in range(2):
                            last = nc.tensor.matmul(data[:], select[:, side, part, j, :], qk[side][part][:, f], start=part == 0, stop=part == 1)
                        last.then_inc(fl.filled("sel", side, pair), 1)

                def front(fl, it, n, slot):
                    if slot == XT_SLOT:
                        pe.wait_ge(s["xn_done"], n * TT + TT)
                        for k in range(CT):
                            data = begin(fl, it, "xT", k)
                            for t in range(TT):
                                last = nc.tensor.transpose(data[:, t * P:(t + 1) * P], xn[:, t, k * P:(k + 1) * P], core.ident[:])
                            last.then_inc(fl.filled("xT", k), 1)
                    for f, at in ((0, QK0_SLOT), (1, QK1_SLOT)):
                        if slot == at:
                            for k in range(CT):
                                pe.wait_ge(*fl.read(it, "xT", k))
                            for side, weight in enumerate((wq, wk)):
                                data = begin(fl, it, "qk", side, f)
                                for k in range(CT):
                                    last = nc.tensor.matmul(data[:], weight[:, k, f * P:(f + 1) * P], xnT[:, k], start=k == 0, stop=k == CT - 1)
                                last.then_inc(fl.filled("qk", side, f), 1)
                    if slot == V0_SLOT:
                        for b in range(2):
                            data = begin(fl, it, "v", b)
                            for t in (2 * b, 2 * b + 1):
                                for k in range(CT):
                                    last = nc.tensor.matmul(data[:, t % 2 * C:(t % 2 + 1) * C], xnT[:, k, t * P:(t + 1) * P], wv[:, k, :],
                                                            start=k == 0, stop=k == CT - 1)
                            last.then_inc(fl.filled("v", b), 1)
                    if slot == SEL0_SLOT:
                        pe.wait_ge(s["lo_done"], n * 4 + 2)
                        stack(fl, it, 0)
                        for side in range(2):
                            pe.wait_ge(*fl.read(it, "sel", side, 0))
                        core.met(pe, "pe")

                def heavy(fl, it, i, slot):
                    if slot < HB:
                        h, pair = slot, slot // 2
                        rows = slice(h % 2 * 64, h % 2 * 64 + 64)
                        if h % 2 == 0 and pair:
                            for side in range(2):
                                pe.wait_ge(*fl.read(it, "sel", side, pair))
                        for place, (b, t, at) in enumerate(SCORES):
                            data = fl.data("s", h, b) if place == 2 else begin(fl, it, "s", h, b)
                            nc.tensor.matmul(data[:, at:at + (t + 1) * P], stacked[0][rows, pair % 2, t * P:(t + 1) * P],
                                             stacked[1][rows, pair % 2, 0:(t + 1) * P], start=place != 2, stop=False, skip_group_check=True)
                            last = nc.tensor.matmul(data[:, at + t * P:at + (t + 1) * P], ident16[:], causal16[:], start=False, stop=True,
                                                    skip_group_check=True)
                            if place != 1:
                                last.then_inc(fl.filled("s", h, b), 1)
                    if LAG <= slot < HB + LAG:
                        h = slot - LAG
                        for b in range(3):
                            pe.wait_ge(*fl.read(it, "s", h, b))
                        for b in range(3):
                            data = begin(fl, it, "t", h, b)
                            for bank, kt, at in TURNED:
                                if bank == b:
                                    for q in range(kt, TT):
                                        src = SCORE_COLS[q] + kt * P
                                        last = nc.tensor.transpose(data[:, at + (q - kt) * P:at + (q - kt + 1) * P],
                                                                   probs[:, h % (LAG + 1), src:src + P], core.ident[:])
                            last.then_inc(fl.filled("t", h, b), 1)
                    if slot % 2 == 0 and slot // 2 + 1 < PAIRS_B:
                        if slot // 2 + 1 == PAIRS_T:
                            pe.wait_ge(s["lo_done"], i * 4 + 4)
                        stack(fl, it, slot // 2 + 1)
                    for quad in range(NQUADS):
                        if slot == QUAD * (quad + 1) + LAG:
                            heads = range(quad * QUAD, (quad + 1) * QUAD)
                            for b in range(3):
                                pe.wait_ge(*fl.read(it, "t", heads[-1], b))
                            data = begin(fl, it, "pv", quad)
                            for kt in range(TT):
                                at, size = TURNED_COLS[kt], T - kt * P
                                for n, h in enumerate(heads):
                                    last = nc.tensor.matmul(data[n * 32:(n + 1) * 32, kt * P:], v[:, kt, h, :],
                                                            probsT[:, h % (2 * QUAD), at:at + size], start=kt == 0, stop=kt == TT - 1,
                                                            skip_group_check=True)
                            last.then_inc(fl.filled("pv", quad), 1)
                        if slot == QUAD * (quad + 1) + LAG + 1:
                            pe.wait_ge(*fl.read(it, "pv", quad))
                            data = begin(fl, it, "o", quad)
                            for t in range(TT):
                                last = nc.tensor.transpose(data[:, t * P:(t + 1) * P], oT[:, quad % 2, t * P:(t + 1) * P], core.ident[:])
                            last.then_inc(fl.filled("o", quad), 1)
                    if slot == HB + LAG + 2:
                        pe.wait_ge(*fl.read(it, "o", NQUADS - 1))
                        for k in range(CT):
                            data = begin(fl, it, "attT", k)
                            for t in range(TT):
                                last = nc.tensor.transpose(data[:, t * P:(t + 1) * P], att[:, t, k * P:(k + 1) * P], core.ident[:])
                            last.then_inc(fl.filled("attT", k), 1)
                    if slot == HB + LAG + 3:
                        for k in range(CT):
                            pe.wait_ge(*fl.read(it, "attT", k))
                        for b in range(2):
                            data = begin(fl, it, "out", b)
                            for t in (2 * b, 2 * b + 1):
                                for k in range(CT):
                                    last = nc.tensor.matmul(data[:, t % 2 * C:(t % 2 + 1) * C], attT[:, k, t * P:(t + 1) * P], wo[:, k, :],
                                                            start=k == 0, stop=k == CT - 1)
                            last.then_inc(fl.filled("out", b), 1)

                rounds(pe, front, heavy)


def program(nc, dram, out_dram):
    with ExitStack() as ctx:
        core = Core(nc, ctx)
        with ExitStack() as layer:
            la = AttentionA(nc, layer)
            landmarks(core, la, dram)
            layer_a(core, la, dram)
        with ExitStack() as layer:
            ff = FeedForward(nc, layer, 0)
            prepare_ff(core, ff, dram)
            feed_forward(core, ff)
        layer_b(core, dram)
        with ExitStack() as layer:
            ff = FeedForward(nc, layer, 1)
            prepare_ff(core, ff, dram)
            feed_forward(core, ff, out_dram)


def shape_constants():
    ident = np.eye(P, dtype=np.float32)
    shifted = np.zeros((P, BAND + TAPS - 1), np.float32)
    shifted[np.arange(P), np.arange(P) + TAPS - 1] = 1
    feature = np.arange(P) % DB
    frequency = np.float32(1) / np.float32(10000) ** (np.arange(0, DB, 2, dtype=np.float32) / np.float32(DB))
    angle = np.arange(T, dtype=np.float32)[None, :] * frequency[feature // 2][:, None]
    sign = np.where(feature % 2 == 0, np.float32(-1), np.float32(1))[:, None]
    select = np.zeros((P, 2, 2, PAIRS_T, P), np.float32)
    for side, parts in enumerate(((0, 1, 0, 1), (0, 0, 1, 1))):
        for j in range(PAIRS_T):
            for head in range(2):
                for copy, part in enumerate(parts):
                    for d in range(DB):
                        select[(2 * j + head) * DB + d, side, part, j, head * 64 + copy * DB + d] = DB ** -0.5 if side == 0 else 1
    return {
        "ident": ident,
        "i64": np.concatenate([np.eye(M, dtype=np.float32)] * 2),
        "shifted_ident": shifted,
        "cos": np.cos(angle).astype(np.float32),
        "sin": (np.sin(angle) * sign).astype(np.float32),
        "select": select.reshape(P, -1),
        "causal": np.where(np.arange(P)[None, :] > np.arange(P)[:, None], np.float32(-1e30), np.float32(0)),
    }


def kernel(**inputs):
    import concourse.bacc as bacc
    from concourse.bass_utils import run_bass_kernel_spmd

    a = {n[len("L0_attn_a_"):]: np.asarray(v) for n, v in inputs.items() if n.startswith("L0_attn_a_")}
    b = {n[len("L0_attn_b_"):]: np.asarray(v) for n, v in inputs.items() if n.startswith("L0_attn_b_")}
    f = {n[len("L0_ffn_"):]: np.asarray(v) for n, v in inputs.items() if n.startswith("L0_ffn_")}

    by_partition = lambda v: v.reshape(CT, P).T
    router = np.concatenate(
        [f["conf_rwkv"].T, f["conf_trans"][:, None], f["w_diff"][:, None], f["W_aff"], np.zeros((C, 1), np.float32)], axis=1)
    arrays = {
        "x": a["x"].reshape(B * T, C), "w_qkv": a["w_qkv"], "wqT": a["w_qkv"][:, :INNER].T, "wkT": a["w_qkv"][:, INNER:2 * INNER].T,
        "taps": a["w_conv"].reshape(HA * TAPS), "w_fc": a["w_fc"], "b_fc": a["b_fc"],
        "WqT": b["Wq"].T, "WkT": b["Wk"].T, "WvT": b["Wv"].T, "WoT": b["Wo"].T,
        "capital_shares": f["capital_shares"], "router": router, "WsT": f["Ws"].T,
        **{n: by_partition(f[n]) for n in ("ln1_w", "ln1_b", "ln2_w", "ln2_b")},
        **{n: f[n] for n in ("Wr", "Wv", "Wo", "W1", "W2", "W3", "K_rwkv", "V_rwkv")},
        **shape_constants(),
    }
    nc = bacc.Bacc("TRN2", target_bir_lowering=False, num_devices=1)
    staged, dram = {}, {}
    for name, array in arrays.items():
        staged[f"in_{name}_dram"] = np.ascontiguousarray(array)
        dram[name] = nc.dram_tensor(f"in_{name}_dram", array.shape, mybir.dt.from_np(array.dtype), kind="ExternalInput").ap()
    out = nc.dram_tensor("out_0_dram", (B * T, C), F32, kind="ExternalOutput").ap()
    program(nc, dram, out)
    result = run_bass_kernel_spmd(nc, [staged], core_ids=[0])
    return result.results[0]["out_0_dram"].reshape(B, T, C)
```

```python
from contextlib import ExitStack

import concourse.bass as bass
import numpy as np
from concourse import mybir
from concourse.alu_op_type import AluOpType as ALU

F32 = mybir.dt.float32
F32R = mybir.dt.float32r
BF16 = mybir.dt.bfloat16
ACT = mybir.ActivationFunctionType
AX_X = mybir.AxisListType.X
MAX_ALL = bass.bass_isa.ReduceOp.max

P = 128
B, T, C = 8, 512, 256
TT = T // P
CT = C // P
XB = TT * C
EPS = 1e-5

HA, DA, M = 16, 64, 64
LG = T // M
NP = HA // 2
INNER = HA * DA
ITERS = 6
TAPS = 13
PAD = TAPS // 2
BAND = P + TAPS - 1

HB, DB = 16, 16
QUAD = 4

EXPERTS = 3
HID = 4 * C
HT = HID // P
NH = 2 * HT


def cols(tensor, start, n):
    return tensor[:, bass.ds(start, n)]


class Banks:

    def __init__(self, nc, ctx):
        self.data = [ctx.enter_context(nc.psum_tensor(f"bank{b}", [P, T], F32)) for b in range(8)]
        self.bank_full = [ctx.enter_context(nc.semaphore(f"bank_full{b}")) for b in range(8)]
        self.bank_free = [ctx.enter_context(nc.semaphore(f"bank_free{b}")) for b in range(8)]
        self.used = [0] * 8


class Fills:

    def __init__(self, banks, order, rounds=1):
        self.banks = banks
        self.before = list(banks.used)
        self.each = [0] * 8
        self.place = {}
        for name, b in order:
            self.place[name] = (b, self.each[b])
            self.each[b] += 1
        banks.used = [u + n * rounds for u, n in zip(banks.used, self.each)]

    def data(self, *name):
        return self.banks.data[self.place[name][0]]

    def filled(self, *name):
        return self.banks.bank_full[self.place[name][0]]

    def released(self, *name):
        return self.banks.bank_free[self.place[name][0]]

    def full(self, it, *name):
        b, k = self.place[name]
        return self.banks.bank_full[b], self.before[b] + it * self.each[b] + k + 1

    def read(self, it, *name):
        b, k = self.place[name]
        return self.banks.bank_free[b], self.before[b] + it * self.each[b] + k + 2

    def free(self, it, *name):
        b, k = self.place[name]
        return self.banks.bank_free[b], self.before[b] + it * self.each[b] + k + 1


class Core:

    def __init__(self, nc, ctx):
        self.nc = nc
        self.banks = Banks(nc, ctx)
        self.x = ctx.enter_context(nc.sbuf_tensor("x_tokens", [P, B * XB], F32))
        self.ident = ctx.enter_context(nc.sbuf_tensor("ident", [P, P], F32))
        self.neg_half = ctx.enter_context(nc.sbuf_tensor("neg_half", [P, TT], F32))
        self.setup_done = ctx.enter_context(nc.semaphore("setup_done"))
        self.ident_loaded = ctx.enter_context(nc.semaphore("ident_loaded"))
        self.waits_met = {
            e: ctx.enter_context(nc.semaphore(f"waits_met_{e}")) for e in ("pe", "act", "dve", "pool", "sp")
        }

    def met(self, eng, name):
        eng.sem_inc(self.waits_met[name], 1)


def sbuf(nc, ctx, name, shape, dtype=F32):
    return ctx.enter_context(nc.sbuf_tensor(name, shape, dtype))


WAYS = 4
BANDS_DVE, BANDS_EARLY = 2, 3
LAG_T = 3


def landmarks(core, la, dram):
    nc, banks, x = core.nc, core.banks, core.x
    with ExitStack() as ctx:
        sem = lambda name: ctx.enter_context(nc.semaphore(name))
        wqk = sbuf(nc, ctx, "wqk", [P, CT, 2 * INNER])
        stats = sbuf(nc, ctx, "lm_stats", [P, WAYS, TT, 6])
        mv = sbuf(nc, ctx, "lm_mv", [P, WAYS, TT, 2])
        rstd = sbuf(nc, ctx, "lm_rstd", [P, WAYS, TT])
        xn = sbuf(nc, ctx, "lm_xn", [P, WAYS, TT, C])
        xsum = sbuf(nc, ctx, "lm_xsum", [P, CT, B * M])
        neg_max = sbuf(nc, ctx, "lm_neg_max", [P, B, NP])
        row_sum = sbuf(nc, ctx, "lm_row_sum", [P, B, NP])
        row_rcp = sbuf(nc, ctx, "lm_row_rcp", [P, B, NP])
        sums = sbuf(nc, ctx, "lm_sums", [P, 2, B, NP])
        top = sbuf(nc, ctx, "lm_top", [P, 2])
        top_all = sbuf(nc, ctx, "lm_top_all", [P, 2])
        bound = sbuf(nc, ctx, "lm_bound", [P, 1])

        dve_term, pool_term = (sbuf(nc, ctx, f"lm_{n}_band_term", [P, HB_AT, BAND]) for n in ("dve", "pool"))
        dve_signals, pool_signals = ((sem(f"lm_{n}_band_done"), sem(f"lm_{n}_term_done")) for n in ("dve", "pool"))
        x_loaded = [sem(f"x_loaded{w}") for w in range(WAYS)]
        w_loaded = sem("wqk_loaded")
        i64_loaded, stored = sem("i64_loaded"), sem("landmarks_stored")
        ql, kl = (sbuf(nc, ctx, n, [P, NP, B * M]) for n in ("ql", "kl"))
        a, aT = (sbuf(nc, ctx, n, [P, B, NP, M]) for n in ("a", "aT"))
        stats_done, mv_done, var_done, rstd_done, xn_done = map(
            sem, ("lm_stats_done", "lm_mv_done", "lm_var_done", "lm_rstd_done", "lm_xn_done"))
        max_done, exp_done, sum_done, rcp_done, a_done, sums_done = map(
            sem, ("lm_max_done", "lm_exp_done", "lm_sum_done", "lm_rcp_done", "a_done", "sums_done"))
        top_done, top_all_done, bound_done = map(sem, ("top_done", "top_all_done", "bound_done"))

        turn = Fills(banks, [(("xT", par, ct), 2 * par + ct) for par in range(WAYS) for ct in range(CT)], B // WAYS)
        proj = Fills(banks, [(("ql", n), n % 8) for n in range(2 * NP)])
        soft = Fills(banks, [f for b in range(B) for f in ((("sim", b), b % 4), (("aT", b), 4 + b % 4))])

        with nc.Block() as block:

            @block.sync
            def _(sp):
                for free in banks.bank_free:
                    sp.sem_inc(free, 1)

        with nc.Block() as block:

            @block.sync
            def _(sp):
                la.load_taps(sp, dram)
                sp.dma_start(core.ident[:], dram["ident"]).then_inc(core.ident_loaded, 16)
                sp.dma_start(la.i64[:], dram["i64"]).then_inc(i64_loaded, 16)
                def load(it, par):
                    b = it * WAYS + par
                    sp.dma_start(
                        cols(x, b * XB, XB).rearrange("p (t c) -> p t c", c=C),
                        dram["x"][bass.ds(b * T, T), :].rearrange("(t p) c -> p t c", p=P),
                    ).then_inc(x_loaded[par], 16)

                for par in range(WAYS):
                    load(0, par)
                with sp.Fori(1, B // WAYS) as it:
                    for par in range(WAYS):
                        sp.wait_ge(x_loaded[par], it * 16)
                        core.met(sp, "sp")
                        load(it, par)
                la.load(sp, dram)
                for n in range(2 * NP - 8, 2 * NP):
                    sp.wait_ge(*proj.read(0, "ql", n))
                for b in range(B):
                    for src, dst in ((ql, la.ql), (kl, la.kl)):
                        sp.dma_start(dst[b].rearrange("p (j m) -> p j m", m=M), src[:, :, b * M:(b + 1) * M]).then_inc(stored, 16)
                for b in range(B):
                    sp.wait_ge(a_done, b + 1)
                    sp.dma_start(la.a[b], a[:, b].rearrange("p j m -> p (j m)")).then_inc(stored, 16)
                    sp.wait_ge(*soft.read(0, "aT", b))
                    sp.dma_start(la.aT[b], aT[:, b].rearrange("p j m -> p (j m)")).then_inc(stored, 16)
                sp.wait_ge(stored, 4 * B * 16)
                sp.wait_ge(la.loaded, la.loads)

            @block.scalar
            def _(act):
                act.dma_start(wqk[:], dram["w_qkv"][:, 0:2 * INNER].rearrange("(k p) n -> p k n", p=P)).then_inc(w_loaded, 16)
                for n in range(2 * NP):
                    act.wait_ge(*proj.full(0, "ql", n))
                    dst, scale = (ql, DA ** -0.5 / LG) if n < NP else (kl, 1.0 / LG)
                    nc.scalar.activation(dst[:, n % NP, :], proj.data("ql", n)[:], ACT.Copy, scale=scale).then_inc(
                        proj.released("ql", n), 1)
                for b in range(B + LAG_T):
                    if b < B:
                        act.wait_ge(*soft.read(0, "sim", b))
                        nc.scalar.activation(a[:, b], a[:, b], ACT.Exp).then_inc(exp_done, 1)
                    if b >= LAG_T:
                        c = b - LAG_T
                        act.wait_ge(*soft.full(0, "aT", c))
                        nc.scalar.activation(
                            aT[:, c], soft.data("aT", c)[:].rearrange("p (j m) -> p j m", m=M), ACT.Copy
                        ).then_inc(soft.released("aT", c), 1)

            @block.gpsimd
            def _(pool):
                nc.gpsimd.memset(core.neg_half[:], -0.5).then_inc(core.setup_done, 1)
                pool.wait_ge(core.setup_done, 1)
                with pool.Fori(0, B // WAYS) as it:
                    for par in range(WAYS):
                        pool.wait_ge(mv_done, it * WAYS * TT + (par + 1) * TT)
                        core.met(pool, "pool")
                        nc.gpsimd.tensor_scalar(rstd[:, par, :], mv[:, par, :, 1], EPS, None, ALU.add).then_inc(var_done, 1)
                        pool.wait_ge(var_done, it * WAYS + par + 1)
                        nc.gpsimd.tensor_tensor(rstd[:, par, :], rstd[:, par, :], core.neg_half[:], ALU.pow).then_inc(
                            rstd_done, 1)
                for n, q in enumerate(range(BANDS_DVE, BANDS_EARLY)):
                    la.build_bands(nc.gpsimd, pool, n, q, pool_term, pool_signals)
                for b in range(B):
                    pool.wait_ge(rcp_done, b + 1)
                    nc.gpsimd.tensor_tensor(a[:, b], a[:, b], row_rcp[:, b].unsqueeze(2).to_broadcast([P, NP, M]),
                                            ALU.mult).then_inc(a_done, 1)
                pool.wait_ge(top_done, 2)
                nc.gpsimd.partition_all_reduce(top_all[:], top[:], P, MAX_ALL).then_inc(top_all_done, 1)

            @block.vector
            def _(dve):
                with dve.Fori(0, B // WAYS) as it:
                    def statistics(par):
                        dve.wait_ge(x_loaded[par], it * 16 + 16)
                        core.met(dve, "dve")
                        for t in range(TT):
                            nc.vector.bn_stats(stats[:, par, t, :], cols(x, (it * WAYS + par) * XB + t * C, C)).then_inc(stats_done, 1)
                        for t in range(TT):
                            dve.wait_ge(stats_done, it * WAYS * TT + par * TT + t + 1)
                            core.met(dve, "dve")
                            nc.vector.bn_aggr(mv[:, par, t, :], stats[:, par, t, :]).then_inc(mv_done, 1)

                    def normalise(par):
                        dve.wait_ge(rstd_done, it * WAYS + par + 1)
                        core.met(dve, "dve")
                        for t in range(TT):
                            nc.vector.tensor_scalar(
                                xn[:, par, t, :], cols(x, (it * WAYS + par) * XB + t * C, C),
                                mv[:, par, t, 0:1], rstd[:, par, t:t + 1], ALU.subtract, ALU.mult).then_inc(xn_done, 1)

                    def landmark_sums(par):
                        for ct in range(CT):
                            dve.wait_ge(*turn.full(it, "xT", par, ct))
                            core.met(dve, "dve")
                            nc.vector.tensor_reduce(
                                xsum[:, ct, bass.ds((it * WAYS + par) * M, M)],
                                turn.data("xT", par, ct)[:].rearrange("p (m l) -> p m l", l=LG),
                                AX_X, ALU.add).then_inc(turn.released("xT", par, ct), 1)

                    for step in range(WAYS + 2):
                        for work, par in ((statistics, step), (normalise, step - 1), (landmark_sums, step - 2)):
                            if 0 <= par < WAYS:
                                work(par)
                for q in range(BANDS_DVE):
                    la.build_bands(nc.vector, dve, q, q, dve_term, dve_signals)
                grid = lambda ap: ap[:].rearrange("p (j m) -> p j m", m=M)
                spread = lambda ap: ap.unsqueeze(2).to_broadcast([P, NP, M])
                for b in range(B + LAG_T + 1):
                    if b < B:
                        dve.wait_ge(*soft.full(0, "sim", b))
                        nc.vector.tensor_reduce(neg_max[:, b], grid(soft.data("sim", b)), AX_X, ALU.max, negate=True).then_inc(max_done, 1)
                        dve.wait_ge(max_done, b + 1)
                        nc.vector.tensor_tensor(a[:, b], grid(soft.data("sim", b)), spread(neg_max[:, b]), ALU.add).then_inc(soft.released("sim", b), 1)
                    if 1 <= b <= B:
                        c = b - 1
                        dve.wait_ge(exp_done, c + 1)
                        nc.vector.tensor_reduce(row_sum[:, c], a[:, c], AX_X, ALU.add).then_inc(sum_done, 1)
                        dve.wait_ge(sum_done, c + 1)
                        nc.vector.reciprocal(row_rcp[:, c], row_sum[:, c]).then_inc(rcp_done, 1)
                    if 2 <= b <= B + 1:
                        c = b - 2
                        dve.wait_ge(a_done, c + 1)
                        nc.vector.tensor_reduce(sums[:, 0, c], a[:, c], AX_X, ALU.add).then_inc(sums_done, 1)
                    if b >= LAG_T + 1:
                        c = b - LAG_T - 1
                        dve.wait_ge(*soft.read(0, "aT", c))
                        nc.vector.tensor_reduce(sums[:, 1, c], aT[:, c], AX_X, ALU.add).then_inc(sums_done, 1)
                dve.wait_ge(sums_done, 2 * B)
                for side in range(2):
                    nc.vector.tensor_reduce(top[:, side:side + 1], sums[:, side].rearrange("p b j -> p (b j)"), AX_X, ALU.max).then_inc(top_done, 1)
                dve.wait_ge(top_all_done, 1)
                nc.vector.tensor_tensor(bound[:], top_all[:, 0:1], top_all[:, 1:2], ALU.mult).then_inc(bound_done, 1)
                dve.wait_ge(bound_done, 1)
                nc.vector.reciprocal(la.inv_bound[:], bound[:]).then_inc(bound_done, 1)
                dve.wait_ge(bound_done, 2)

            @block.tensor
            def _(pe):
                pe.wait_ge(core.ident_loaded, 16)
                with pe.Fori(0, B // WAYS) as it:
                    for par in range(WAYS):
                        pe.wait_ge(xn_done, it * WAYS * TT + (par + 1) * TT)
                        for ct in range(CT):
                            pe.wait_ge(*turn.free(it, "xT", par, ct))
                            core.met(pe, "pe")
                            for t in range(TT):
                                last = nc.tensor.transpose(
                                    turn.data("xT", par, ct)[:, t * P:(t + 1) * P], xn[:, par, t, ct * P:(ct + 1) * P],
                                    core.ident[:])
                            last.then_inc(turn.filled("xT", par, ct), 1)
                for par in range(WAYS):
                    for ct in range(CT):
                        pe.wait_ge(*turn.read(B // WAYS - 1, "xT", par, ct))
                pe.wait_ge(w_loaded, 16)
                for n in range(2 * NP):
                    pe.wait_ge(*proj.free(0, "ql", n))
                    for ct in range(CT):
                        last = nc.tensor.matmul(proj.data("ql", n)[:], wqk[:, ct, n * P:(n + 1) * P], xsum[:, ct, :],
                                                start=ct == 0, stop=ct == CT - 1)
                    last.then_inc(proj.filled("ql", n), 1)
                for n in range(NP, 2 * NP):
                    pe.wait_ge(*proj.read(0, "ql", n))
                pe.wait_ge(i64_loaded, 16)
                for b in range(B + LAG_T):
                    if b < B:
                        pe.wait_ge(*soft.free(0, "sim", b))
                        for j in range(NP):
                            for h in (slice(0, M), slice(M, 2 * M)):
                                last = nc.tensor.matmul(
                                    soft.data("sim", b)[h, j * M:(j + 1) * M], ql[h, j, b * M:(b + 1) * M],
                                    kl[h, j, b * M:(b + 1) * M], start=True, stop=True)
                        last.then_inc(soft.filled("sim", b), 1)
                    if b >= LAG_T:
                        c = b - LAG_T
                        pe.wait_ge(a_done, c + 1)
                        pe.wait_ge(*soft.free(0, "aT", c))
                        for j in range(NP):
                            for h in (slice(0, M), slice(M, 2 * M)):
                                last = nc.tensor.matmul(soft.data("aT", c)[h, j * M:(j + 1) * M], a[h, c, j, :],
                                                        la.i64[h, :], start=True, stop=True)
                        last.then_inc(soft.filled("aT", c), 1)


HB_AT = 4
BAND_STEPS = TAPS + 1


class AttentionA:

    def __init__(self, nc, ctx):
        self.wqT, self.wkT, self.wfc = (sbuf(nc, ctx, n, [P, NP, C]) for n in ("wqT", "wkT", "wfc"))
        self.bias = sbuf(nc, ctx, "bias_fc", [P, C])
        self.inv_bound = sbuf(nc, ctx, "inv_bound", [P, 1])
        self.i64 = sbuf(nc, ctx, "i64", [P, M])
        self.ql, self.kl, self.a, self.aT = (
            nc.dram_tensor(f"scratch_{n}", (B, P, NP * M), F32, kind="Internal").ap() for n in ("ql", "kl", "a", "aT"))
        self.band = sbuf(nc, ctx, "band", [P, HA, BAND])
        self.taps, self.shifted = sbuf(nc, ctx, "taps", [P, HA, TAPS]), sbuf(nc, ctx, "shifted_ident", [P, BAND + TAPS - 1])
        self.taps_loaded = ctx.enter_context(nc.semaphore("taps_loaded"))
        self.loaded = ctx.enter_context(nc.semaphore("weights_a_loaded"))
        self.loads = 0

    def load(self, eng, dram):
        rows = lambda ap: ap.rearrange("(j p) c -> p j c", p=P)
        for dst, src in (
                (self.wqT, rows(dram["wqT"])), (self.wkT, rows(dram["wkT"])), (self.wfc, rows(dram["w_fc"])),
                (self.bias, dram["b_fc"].partition_broadcast(P))):
            eng.dma_start(dst[:], src).then_inc(self.loaded, 16)
            self.loads += 16

    def load_taps(self, eng, dram):
        eng.dma_start(self.taps[:].rearrange("p h k -> p (h k)"), dram["taps"].partition_broadcast(P)).then_inc(self.taps_loaded, 16)
        eng.dma_start(self.shifted[:], dram["shifted_ident"]).then_inc(self.taps_loaded, 16)

    def build_bands(self, ops, eng, n, q, term, signals):
        band_done, term_done = signals
        some = slice(q * HB_AT, (q + 1) * HB_AT)
        diagonal = lambda k: self.shifted[:, k:k + BAND].unsqueeze(1).to_broadcast([P, HB_AT, BAND])
        tap = lambda k: self.taps[:, some, k:k + 1].to_broadcast([P, HB_AT, BAND])
        band = self.band[:, some]
        eng.wait_ge(self.taps_loaded, 32)
        ops.tensor_tensor(band, tap(0), diagonal(0), ALU.mult).then_inc(band_done, 1)
        for k in range(1, TAPS):
            eng.wait_ge(band_done, n * BAND_STEPS + k)
            ops.tensor_tensor(term[:], tap(k), diagonal(k), ALU.mult).then_inc(term_done, 1)
            eng.wait_ge(term_done, n * (TAPS - 1) + k)
            ops.tensor_tensor(band, band, term[:], ALU.add).then_inc(band_done, 1)
        eng.wait_ge(band_done, n * BAND_STEPS + TAPS)
        ops.tensor_tensor(band, band, diagonal(PAD), ALU.add).then_inc(band_done, 1)
        eng.wait_ge(band_done, (n + 1) * BAND_STEPS)


GP = NP // 2
GROUPS = NP // GP
RESTORE = 2
INVERSE_STEPS = [("w0",)] + [
    n for k in range(ITERS) for n in [("t", k), ("u", k), ("wz", k)] + ([("w", k)] if k == RESTORE else [])]


def layer_a(core, la, dram):
    nc, banks, x = core.nc, core.banks, core.x
    HH = NP // 2
    PASSES = ((0, 0), (0, 1), (1, 0))
    with ExitStack() as ctx:
        sem = lambda name: ctx.enter_context(nc.semaphore(name))
        buf = lambda name, shape: sbuf(nc, ctx, name, shape)
        stats, mv, rstd = buf("a_stats", [P, TT, 6]), buf("a_mv", [P, TT, 2]), buf("a_rstd", [P, TT])
        xn = buf("a_xn", [P, TT, C])
        split = lambda name, shape: [sbuf(nc, ctx, f"{name}_{part}", shape, F32R) for part in ("hi", "lo")]
        xnT, wv = split("a_xnT", [P, CT, T]), split("wv_a", [P, CT, INNER])
        kl_diag, ql_diag = buf("kl_diag", [P, NP, P]), buf("ql_diag", [P, NP, P])
        u, g = split("u", [P, CT, INNER]), split("g", [P, CT, INNER])
        fc = [part[:].rearrange("p k (j c) -> p (k j) c", c=C) for part in g]
        v = buf("v_a", [P, TT, INNER // 2])
        wv_raw = v[:].rearrange("p t n -> p (t n)")
        probs1 = buf("probs1", [P, TT, INNER])
        neg_max1, sum1, rcp1 = (buf(n, [P, 2 * TT, NP]) for n in ("neg_max1", "sum1", "rcp1"))
        e3, e3T = buf("e3", [P, 2, T]), buf("e3T", [P, 2, T])
        neg_max3, sum3, rcp3 = (buf(n, [P, NP]) for n in ("neg_max3", "sum3", "rcp3"))
        av3, inverse = (buf(n, [P, NP, M]) for n in ("av3", "inverse"))
        i7, i15, i13 = (buf(f"i{n}", [P, GP, M]) for n in (7, 15, 13))
        a_in, at = buf("a_in", [P, NP, M]), buf("at", [P, NP, M])
        wz = buf("wz", [P, GROUPS, GP, 2, M])
        t1 = t3 = z = buf("pi_t", [P, GROUPS, GP, M])
        p_diag, avT_diag = buf("pi_p_diag", [P, GROUPS, GP, P]), buf("avT_diag", [P, NP, P])
        conv = split("conv", [P, 2, T])
        band_term = buf("band_term", [P, HB_AT, BAND])
        names = ("stats_done", "mv_done", "var_done", "rstd_done", "xn_done", "landmarks_loaded", "diag_zeroed", "wide_zeroed", "max1_done",
                 "exp1_done", "sum1_done", "rcp1_done", "probs1_done", "max3_done", "rcp3_done", "bias_added", "term_done", "band_done", "wv_loaded", "wv_hi", "wv_lo", "hi_done", "eyes_done", "a_loaded", "t1_done")
        s = {n: sem("a_" + n) for n in names}

        order = [("xT", k) for k in range(CT)] + [("u", k) for k in range(4)] + [("g", k) for k in range(4)]
        for f in range(TT):
            order += [("v", 0, f), ("s1", f)]

        def s3_steps(half):
            lo, hi = half * HH, (half + 1) * HH
            for j in range(lo, hi + 2):
                if j < hi:
                    yield ("s3", j)
                    if half == 0:
                        yield ("s1", TT + j)
                if lo <= j - 1 < hi:
                    yield ("e3T", j - 1)
                if lo <= j - 2 < hi:
                    yield ("av3", j - 2)

        order += [n for n in s3_steps(0) if n[0] != "av3"] + [("v", 1, t) for t in range(TT)]
        order += [n for n in s3_steps(1) if n[0] != "av3"] + [("c", 0), ("avT",), ("c", 1)]
        order += [("fc", k) for k in range(4)] + [("c", j) for j in range(2, NP)]
        fills = Fills(banks, [(n, i % 4) for i, n in enumerate(order)] + [(("av3", 0), 4), (("av3", 1), 5), (("y", 0), 4), (("y", 1), 5)], B)
        inverse_order = [((*n, g), 6 + g) for n in INVERSE_STEPS for g in range(GROUPS)]
        inverse_fills = Fills(banks, inverse_order, B)
        block512 = lambda tensor, k: tensor[:, k // 2, k % 2 * 512:(k % 2 + 1) * 512]
        parts_of = {("xT", k): [w[:, k] for w in xnT] for k in range(CT)}
        for name, tensor in (("u", u), ("g", g)):
            parts_of.update({(name, k): [block512(w, k) for w in tensor] for k in range(4)})
        parts_of.update({("c", j): [w[:, j % 2] for w in conv] for j in range(2)})
        parts_of.update({("fc", k): [w[:, 2 * k:2 * k + 2].rearrange("p j c -> p (j c)") for w in fc] for k in range(4)})
        parts_of.update({("c", j): [w[:, j % 2] for w in conv] for j in range(2, NP)})
        part_at = {name: i for i, name in enumerate(parts_of)}
        heads = lambda ap: ap.rearrange("p (j m) -> p j m", m=M)
        spread = lambda ap, n: ap.unsqueeze(2).to_broadcast([P, n, M])
        halves = (slice(0, M), slice(M, 2 * M))
        group = lambda tensor, g: tensor[:, g * GP:(g + 1) * GP, :]
        single = lambda fl, *n: fl.data(*n)[:, 0:GP * M].rearrange("p (j m) -> p j m", m=M)
        double = lambda fl, *n: fl.data(*n)[:].rearrange("p (j q m) -> p j q m", q=2, m=M)

        def rounds(eng, batch, step):
            with eng.Fori(0, B - 1) as it:
                batch(it, False, lambda i: step(inverse_fills, it, i))
            batch(B - 1, True, lambda i: step(inverse_fills, B - 1, i))

        DIAGS, WIDE = 2, 2

        with nc.Block() as block:

            @block.sync
            def _(sp):
                def load_landmarks(n):
                    for src, dst in ((la.kl, kl_diag), (la.ql, ql_diag)):
                        for h in halves:
                            sp.dma_start(dst[h, :, h], src[bass.ds(n, 1), h, :].rearrange("b p (j m) -> (b p) j m", m=M)).then_inc(
                                s["landmarks_loaded"], 16)

                def load_a(n):
                    for src, dst in ((la.a, a_in), (la.aT, at)):
                        sp.dma_start(dst[:].rearrange("p j m -> p (j m)"), src[bass.ds(n, 1), :, :].rearrange("b p c -> (b p) c")).then_inc(
                            s["a_loaded"], 16)

                load_a(0)
                sp.dma_start(wv_raw.rearrange("p (k n) -> p k n", k=CT), dram["w_qkv"][:, 2 * INNER:].rearrange("(k p) n -> p k n", p=P)).then_inc(
                    s["wv_loaded"], 16)
                sp.wait_ge(s["diag_zeroed"], DIAGS)
                load_landmarks(0)

                def reached(semaphore, value):
                    sp.wait_ge(semaphore, value)
                    core.met(sp, "sp")

                with sp.Fori(0, B - 1) as it:
                    for k in range(4):
                        reached(*fills.full(it, "g", k))
                    load_landmarks(it + 1)
                    for g in range(GROUPS):
                        reached(*inverse_fills.full(it, "w", RESTORE, g))
                    load_a(it + 1)
                sp.wait_ge(s["landmarks_loaded"], B * 64)
                sp.wait_ge(s["a_loaded"], B * 32)

            @block.vector
            def _(dve):
                def statistics(n):
                    dve.wait_ge(s["xn_done"], n * TT)
                    core.met(dve, "dve")
                    for t in range(TT):
                        nc.vector.bn_stats(stats[:, t, :], cols(x, n * XB + t * C, C)).then_inc(s["stats_done"], 1)
                    for t in range(TT):
                        dve.wait_ge(s["stats_done"], n * TT + t + 1)
                        core.met(dve, "dve")
                        nc.vector.bn_aggr(mv[:, t, :], stats[:, t, :]).then_inc(s["mv_done"], 1)

                def normalise(n):
                    dve.wait_ge(s["rstd_done"], n + 1)
                    core.met(dve, "dve")
                    for t in range(TT):
                        nc.vector.tensor_scalar(xn[:, t, :], cols(x, n * XB + t * C, C), mv[:, t, 0:1], rstd[:, t:t + 1],
                                                ALU.subtract, ALU.mult).then_inc(s["xn_done"], 1)

                def second_part(it, *name):
                    hi, lo = parts_of[name]
                    dve.wait_ge(s["hi_done"], it * len(parts_of) + part_at[name] + 1)
                    core.met(dve, "dve")
                    nc.vector.tensor_tensor(lo, fills.data(*name)[:], hi.bitcast(F32), ALU.subtract).then_inc(fills.released(*name), 1)

                def shift1(it, f):
                    dve.wait_ge(*fills.full(it, "s1", f))
                    core.met(dve, "dve")
                    scores = heads(fills.data("s1", f)[:])
                    t, half = f % TT, f // TT
                    nc.vector.tensor_reduce(neg_max1[:, f], scores, AX_X, ALU.max, negate=True).then_inc(s["max1_done"], 1)
                    dve.wait_ge(s["max1_done"], it * 2 * TT + f + 1)
                    nc.vector.tensor_tensor(heads(probs1[:, t, half * 512:(half + 1) * 512]), scores, spread(neg_max1[:, f], NP),
                                            ALU.add).then_inc(fills.released("s1", f), 1)

                def sums1(it, f):
                    t, half = f % TT, f // TT
                    dve.wait_ge(s["exp1_done"], it * 2 * TT + f + 1)
                    core.met(dve, "dve")
                    nc.vector.tensor_reduce(sum1[:, f], heads(probs1[:, t, half * 512:(half + 1) * 512]), AX_X, ALU.add).then_inc(
                        s["sum1_done"], 1)
                    dve.wait_ge(s["sum1_done"], it * 2 * TT + f + 1)
                    core.met(dve, "dve")
                    nc.vector.reciprocal(rcp1[:, f], sum1[:, f]).then_inc(s["rcp1_done"], 1)

                def max3(it, j):
                    dve.wait_ge(*fills.full(it, "s3", j))
                    core.met(dve, "dve")
                    nc.vector.tensor_reduce(neg_max3[:, j:j + 1], fills.data("s3", j)[:], AX_X, ALU.max, negate=True).then_inc(
                        s["max3_done"], 1)

                def scale3(it, half):
                    pairs = slice(half * HH, (half + 1) * HH)
                    for j in range(half * HH, (half + 1) * HH):
                        dve.wait_ge(*fills.read(it, "s3", j))
                    core.met(dve, "dve")
                    nc.vector.reciprocal(rcp3[:, pairs], sum3[:, pairs]).then_inc(s["rcp3_done"], 1)
                    dve.wait_ge(s["rcp3_done"], it * 2 + half + 1)
                    dve.wait_ge(*fills.full(it, "av3", half))
                    nc.vector.tensor_tensor(av3[:, pairs], heads(fills.data("av3", half)[:, 0:HH * M]), spread(rcp3[:, pairs], HH),
                                            ALU.mult).then_inc(fills.released("av3", half), 1)

                def step(fl, it, i):
                    name = INVERSE_STEPS[i]
                    for g in range(GROUPS):
                        if name[0] == "w0":
                            dve.wait_ge(*fl.full(it, *name, g))
                            dve.wait_ge(s["a_loaded"], it * 32 + 32)
                            core.met(dve, "dve")
                            nc.vector.tensor_scalar(wz[:, g, :, 1, :], group(a_in, g), la.inv_bound[:, 0:1], None, ALU.mult)
                    for g in range(GROUPS):
                        if name[0] == "t":
                            dve.wait_ge(*fl.full(it, *name, g))
                            nc.vector.tensor_tensor(t3[:, g], i15[:], single(fl, *name, g), ALU.subtract).then_inc(
                                fl.released(*name, g), 1)
                        elif name[0] == "u":
                            dve.wait_ge(*fl.full(it, *name, g))
                            dve.wait_ge(s["wide_zeroed"], WIDE)
                            core.met(dve, "dve")
                            for h in halves:
                                done = nc.vector.scalar_tensor_tensor(out=p_diag[h, g, :, h], in0=single(fl, *name, g)[h], scalar=-0.25,
                                                                      in1=i13[h], op0=ALU.mult, op1=ALU.add)
                            done.then_inc(fl.released(*name, g), 1)
                        elif name in (("wz", RESTORE), ("wz", ITERS - 1)):
                            pass
                        else:
                            dve.wait_ge(*fl.read(it, *name, g))
                            nc.vector.tensor_tensor(t1[:, g], i7[:], wz[:, g, :, 0, :], ALU.subtract).then_inc(s["t1_done"], 1)

                def batch(it, last, mark):
                    mark(0)
                    if not last:
                        statistics(it + 1)
                    for k in range(CT):
                        second_part(it, "xT", k)
                    for m, name in enumerate(("u", "g")):
                        for k in range(4):
                            second_part(it, name, k)
                            if (name, k) == ("u", 1):
                                mark(1)
                        mark(2 + m)
                    for f in range(TT):
                        shift1(it, f)
                        if f:
                            sums1(it, f - 1)
                        mark(4 + f)
                    if not last:
                        normalise(it + 1)
                    for j in range(HH):
                        max3(it, j)
                        shift1(it, TT + j)
                        sums1(it, TT + j - 1)
                        mark(8 + j)
                    sums1(it, 2 * TT - 1)
                    mark(12)
                    scale3(it, 0)
                    mark(13)
                    mark(14)
                    for j in range(HH, NP):
                        max3(it, j)
                        mark(15 + j - HH)
                    mark(19)
                    scale3(it, 1)
                    for j in range(2):
                        second_part(it, "c", j)
                    for k in range(4):
                        second_part(it, "fc", k)
                    for j in range(2, NP):
                        second_part(it, "c", j)
                    dve.wait_ge(s["bias_added"], it * 2 + 2)
                    for k in range(2):
                        dve.wait_ge(*fills.full(it, "y", k))
                        xs = cols(x, it * XB + k * 512, 512)
                        nc.vector.tensor_tensor(xs, xs, fills.data("y", k)[:], ALU.add).then_inc(fills.released("y", k), 1)

                for diag in (kl_diag, ql_diag):
                    nc.vector.memset(diag[:], 0.0).then_inc(s["diag_zeroed"], 1)
                for tile, n in ((i7, 7.0), (i15, 15.0), (i13, 13.0 / 4)):
                    nc.vector.tensor_scalar(tile[:], la.i64[:].unsqueeze(1).to_broadcast([P, GP, M]), n, None, ALU.mult).then_inc(
                        s["eyes_done"], 1)
                dve.wait_ge(s["eyes_done"], 3)
                statistics(0)
                normalise(0)
                dve.wait_ge(s["wv_hi"], 1)
                flat = [w[:].rearrange("p k n -> p (k n)") for w in wv]
                nc.vector.tensor_tensor(flat[1], wv_raw, flat[0].bitcast(F32), ALU.subtract).then_inc(s["wv_lo"], 1)
                rounds(dve, batch, step)

            @block.gpsimd
            def _(pool):
                def inverse_deviation(n):
                    pool.wait_ge(s["mv_done"], (n + 1) * TT)
                    core.met(pool, "pool")
                    nc.gpsimd.tensor_scalar(rstd[:], mv[:, :, 1], EPS, None, ALU.add).then_inc(s["var_done"], 1)
                    pool.wait_ge(s["var_done"], n + 1)
                    nc.gpsimd.tensor_tensor(rstd[:], rstd[:], core.neg_half[:], ALU.pow).then_inc(s["rstd_done"], 1)

                def batch(it, last, mark):
                    if not last:
                        inverse_deviation(it + 1)
                    pool.wait_ge(s["xn_done"], it * TT + TT)
                    core.met(pool, "pool")
                    for k in range(2):
                        xs = cols(x, it * XB + k * 512, 512).rearrange("p (t c) -> p t c", c=C)
                        nc.gpsimd.tensor_tensor(xs, xs, la.bias[:].unsqueeze(1).to_broadcast([P, 2, C]), ALU.add).then_inc(
                            s["bias_added"], 1)
                    for f in range(2 * TT):
                        t, half = f % TT, f // TT
                        pool.wait_ge(s["rcp1_done"], it * 2 * TT + f + 1)
                        probs = heads(probs1[:, t, half * 512:(half + 1) * 512])
                        nc.gpsimd.tensor_tensor(probs, probs, spread(rcp1[:, f], NP), ALU.mult).then_inc(s["probs1_done"], 1)

                for diag in (p_diag, avT_diag):
                    nc.gpsimd.memset(diag[:], 0.0).then_inc(s["wide_zeroed"], 1)
                inverse_deviation(0)
                for n, q in enumerate(range(BANDS_EARLY, HA // HB_AT)):
                    la.build_bands(nc.gpsimd, pool, n, q, band_term, (s["band_done"], s["term_done"]))
                rounds(pool, batch, lambda fl, it, i: None)

            @block.scalar
            def _(act):
                def copy(it, dst, name):
                    act.wait_ge(*fills.full(it, *name))
                    nc.scalar.activation(dst, fills.data(*name)[:], ACT.Copy).then_inc(fills.released(*name), 1)

                def first_part(it, *name):
                    act.wait_ge(*fills.full(it, *name))
                    nc.scalar.activation(parts_of[name][0], fills.data(*name)[:], ACT.Copy).then_inc(s["hi_done"], 1)

                def exp1(it, f):
                    t, half = f % TT, f // TT
                    act.wait_ge(*fills.read(it, "s1", f))
                    probs = probs1[:, t, half * 512:(half + 1) * 512]
                    nc.scalar.activation(probs, probs, ACT.Exp, scale=DA ** -0.5).then_inc(s["exp1_done"], 1)

                def exp3(it, j):
                    act.wait_ge(s["max3_done"], it * NP + j + 1)
                    nc.scalar.activation(e3[:, j % 2], fills.data("s3", j)[:], ACT.Exp, bias=neg_max3[:, j:j + 1],
                                         accum_out=sum3[:, j:j + 1]).then_inc(fills.released("s3", j), 1)

                def step(fl, it, i):
                    name = INVERSE_STEPS[i]
                    for g in range(GROUPS):
                        if name[0] in ("t", "u"):
                            continue
                        act.wait_ge(*fl.full(it, *name, g))
                        if name[0] == "wz" and name[1] == ITERS - 1:
                            nc.scalar.activation(group(inverse, g), double(fl, *name, g)[:, :, 1, :], ACT.Copy).then_inc(
                                fl.released(*name, g), 1)
                        elif name == ("wz", RESTORE):
                            nc.scalar.activation(z[:, g], double(fl, *name, g)[:, :, 0, :], ACT.Copy)
                            nc.scalar.activation(wz[:, g, :, 1, :], double(fl, *name, g)[:, :, 1, :], ACT.Copy).then_inc(
                                fl.released(*name, g), 1)
                        else:
                            if name[0] == "wz":
                                done = nc.scalar.activation(wz[:, g], double(fl, *name, g), ACT.Copy)
                            else:
                                done = nc.scalar.activation(wz[:, g, :, 0, :], single(fl, *name, g), ACT.Copy,
                                                            scale=la.inv_bound[:, 0:1] if name[0] == "w0" else 1.0)
                            done.then_inc(fl.released(*name, g), 1)

                def batch(it, last, mark):
                    mark(0)
                    for k in range(CT):
                        first_part(it, "xT", k)
                    for m, name in enumerate(("u", "g")):
                        for k in range(4):
                            first_part(it, name, k)
                            if (name, k) == ("u", 1):
                                mark(1)
                        mark(2 + m)
                    for f in range(TT):
                        copy(it, v[:, f], ("v", 0, f))
                        exp1(it, f)
                        mark(4 + f)
                    for j in range(HH + 1):
                        if j < HH:
                            exp3(it, j)
                            exp1(it, TT + j)
                        if j:
                            copy(it, e3T[:, (j - 1) % 2], ("e3T", j - 1))
                        mark(8 + j)
                    for t in range(TT):
                        copy(it, v[:, t], ("v", 1, t))
                        if t % 2 == 0:
                            mark(13 + t // 2)
                    for j in range(HH, NP + 1):
                        if j < NP:
                            exp3(it, j)
                        if j > HH:
                            copy(it, e3T[:, (j - 1) % 2], ("e3T", j - 1))
                        mark(15 + j - HH)
                    first_part(it, "c", 0)
                    act.wait_ge(*fills.full(it, "avT"))
                    for h in halves:
                        done = nc.scalar.activation(avT_diag[h, :, h], heads(fills.data("avT")[:])[h], ACT.Copy)
                    done.then_inc(fills.released("avT"), 1)
                    first_part(it, "c", 1)
                    for k in range(4):
                        first_part(it, "fc", k)
                    for j in range(2, NP):
                        first_part(it, "c", j)

                act.wait_ge(s["wide_zeroed"], WIDE)
                act.wait_ge(s["wv_loaded"], 16)
                nc.scalar.activation(wv[0][:].rearrange("p k n -> p (k n)"), wv_raw, ACT.Copy).then_inc(s["wv_hi"], 1)
                rounds(act, batch, step)

            @block.tensor
            def _(pe):
                def begin_in(fl, it, *name):
                    pe.wait_ge(*fl.free(it, *name))
                    core.met(pe, "pe")
                    return fl.data(*name)

                def begin(it, *name):
                    return begin_in(fills, it, *name)

                steps = [(k, a, b) for k in range(CT) for a, b in PASSES]

                def from_xn(it, name, t, weight):
                    data = begin(it, *name)
                    for n, (k, a, b) in enumerate(steps):
                        last = nc.tensor.matmul(data[:], xnT[a][:, k, t * P:(t + 1) * P], weight(b, k), start=n == 0, stop=n == len(steps) - 1)
                    last.then_inc(fills.filled(*name), 1)

                def scores1(it, f):
                    t, half = f % TT, f // TT
                    from_xn(it, ("s1", f), t, lambda part, k: u[part][:, k, half * 512:(half + 1) * 512])

                def values(it, half, mark):
                    for t in range(TT):
                        from_xn(it, ("v", half, t), t, lambda part, k: wv[part][:, k, half * 512:(half + 1) * 512])
                        if half == 0:
                            if t == 0:
                                for k in range(4):
                                    pe.wait_ge(*fills.read(it, "u", k))
                                core.met(pe, "pe")
                            scores1(it, t)
                            mark(4 + t)
                        elif t % 2 == 0:
                            mark(13 + t // 2)

                def scores3(it, j):
                    data = begin(it, "s3", j)
                    for n, (k, a, b) in enumerate(steps):
                        last = nc.tensor.matmul(data[:], g[a][:, k, j * P:(j + 1) * P], xnT[b][:, k, :], start=n == 0, stop=n == len(steps) - 1)
                    last.then_inc(fills.filled("s3", j), 1)

                def turn3(it, j):
                    pe.wait_ge(*fills.read(it, "s3", j))
                    data = begin(it, "e3T", j)
                    for t in range(TT):
                        last = nc.tensor.transpose(data[:, t * P:(t + 1) * P], e3[:, j % 2, t * P:(t + 1) * P], core.ident[:])
                    last.then_inc(fills.filled("e3T", j), 1)

                def values3(it, j):
                    half, jj = j // HH, j % HH
                    if jj == 0:
                        for t in range(TT):
                            pe.wait_ge(*fills.read(it, "v", half, t))
                        core.met(pe, "pe")
                        begin(it, "av3", half)
                    data = fills.data("av3", half)
                    pe.wait_ge(*fills.read(it, "e3T", j))
                    core.met(pe, "pe")
                    for t in range(TT):
                        for hh in range(2):
                            last = nc.tensor.matmul(
                                data[hh * M:(hh + 1) * M, jj * M:(jj + 1) * M], e3T[:, j % 2, t * P + hh * M:t * P + (hh + 1) * M],
                                v[:, t, (2 * jj + hh) * DA:(2 * jj + hh + 1) * DA], start=t == 0, stop=t == TT - 1,
                                skip_group_check=True)
                    if jj == HH - 1:
                        last.then_inc(fills.filled("av3", half), 1)

                def products(data, lhs, rhs):
                    for j in range(GP):
                        for h in halves:
                            last = nc.tensor.matmul(data[h, j * M:(j + 1) * M], lhs[h, j], rhs[h, j], start=True, stop=True)
                    return last

                def step(fl, it, i):
                    name = INVERSE_STEPS[i]
                    for g in range(GROUPS):
                        k = name[-1]
                        if name[0] == "w0":
                            pe.wait_ge(s["a_loaded"], it * 32 + 32)
                        if name[0] == "t":
                            pe.wait_ge(s["t1_done"], (it * ITERS + k) * GROUPS + g + 1)
                        data = begin_in(fl, it, *name, g)
                        if name[0] == "w0":
                            last = products(data, group(at, g), group(at, g))
                        elif name[0] == "t":
                            last = products(data, wz[:, g, :, 0, :], t1[:, g])
                        elif name[0] == "u":
                            last = products(data, wz[:, g, :, 0, :], t3[:, g])
                        elif name[0] == "w":
                            last = products(data, group(at, g), z[:, g])
                        else:
                            pairs = double(fl, *name, g)
                            for j in range(GP):
                                if k == RESTORE:
                                    for h in halves:
                                        nc.tensor.matmul(pairs[h, j, 0], wz[h, g, j, 1, :], p_diag[h, g, j, h], start=True, stop=True)
                                if k in (RESTORE, ITERS - 1):
                                    last = nc.tensor.matmul(pairs[:, j, 1], p_diag[:, g, j], wz[:, g, j, 1, :], start=True, stop=True)
                                else:
                                    last = nc.tensor.matmul(pairs[:, j], p_diag[:, g, j], wz[:, g, j], start=True, stop=True)
                        last.then_inc(fl.filled(*name, g), 1)

                def convolve(it, j):
                    data = begin(it, "c", j)
                    for t in range(TT):
                        lo, hi = max(0, t * P - PAD), min(T, (t + 1) * P + PAD)
                        off = lo - (t * P - PAD)
                        for hh in range(2):
                            h = 2 * j + hh
                            last = nc.tensor.matmul(
                                data[hh * M:(hh + 1) * M, lo:hi], probs1[:, t, h * M:(h + 1) * M],
                                la.band[:, h, off:off + hi - lo], start=t == 0, stop=t == TT - 1, skip_group_check=True)
                    last.then_inc(fills.filled("c", j), 1)

                def batch(it, last, mark):
                    mark(0)
                    pe.wait_ge(s["xn_done"], it * TT + TT)
                    for k in range(CT):
                        data = begin(it, "xT", k)
                        for t in range(TT):
                            last = nc.tensor.transpose(data[:, t * P:(t + 1) * P], xn[:, t, k * P:(k + 1) * P], core.ident[:])
                        last.then_inc(fills.filled("xT", k), 1)
                    pe.wait_ge(s["landmarks_loaded"], it * 64 + 64)
                    for name, weight, diag in (("u", la.wqT, kl_diag), ("g", la.wkT, ql_diag)):
                        for k in range(4):
                            data = begin(it, name, k)
                            for j in range(HH):
                                pair = k % 2 * HH + j
                                last = nc.tensor.matmul(data[:, j * P:(j + 1) * P], weight[:, pair, k // 2 * P:(k // 2 + 1) * P],
                                                        diag[:, pair, :], start=True, stop=True)
                            last.then_inc(fills.filled(name, k), 1)
                            if (name, k) == ("u", 1):
                                mark(1)
                        mark(2 if name == "u" else 3)
                    for k in range(CT):
                        pe.wait_ge(*fills.read(it, "xT", k))
                    pe.wait_ge(s["wv_lo"], 1)
                    core.met(pe, "pe")
                    values(it, 0, mark)
                    for k in range(4):
                        pe.wait_ge(*fills.read(it, "g", k))
                    core.met(pe, "pe")
                    for n in s3_steps(0):
                        {"s3": scores3, "s1": scores1, "e3T": turn3, "av3": values3}[n[0]](it, n[1])
                        if n[0] == "s1":
                            mark(8 + n[1] - TT)
                        if n == ("av3", HH - 2):
                            mark(12)
                    values(it, 1, mark)
                    for n in s3_steps(1):
                        {"s3": scores3, "e3T": turn3, "av3": values3}[n[0]](it, n[1])
                        if n[0] == "s3":
                            mark(15 + n[1] - HH)
                        if n == ("av3", NP - 2):
                            mark(19)
                    pe.wait_ge(s["probs1_done"], it * 2 * TT + 2 * TT)
                    pe.wait_ge(s["band_done"], (HA // HB_AT - BANDS_EARLY) * BAND_STEPS)
                    core.met(pe, "pe")
                    convolve(it, 0)
                    for half in range(2):
                        pe.wait_ge(*fills.read(it, "av3", half))
                    for g in range(GROUPS):
                        pe.wait_ge(*inverse_fills.read(it, "wz", ITERS - 1, g))
                    core.met(pe, "pe")
                    data = begin(it, "avT")
                    for j in range(NP):
                        for h in (slice(0, M), slice(M, 2 * M)):
                            last = nc.tensor.matmul(data[h, j * M:(j + 1) * M], av3[h, j, :], inverse[h, j, :], start=True, stop=True)
                    last.then_inc(fills.filled("avT"), 1)
                    convolve(it, 1)
                    pe.wait_ge(*fills.read(it, "avT"))
                    for k in range(4):
                        data = begin(it, "fc", k)
                        for jj in range(2):
                            last = nc.tensor.matmul(data[:, jj * C:(jj + 1) * C], avT_diag[:, 2 * k + jj, :], la.wfc[:, 2 * k + jj, :],
                                                    start=True, stop=True)
                        last.then_inc(fills.filled("fc", k), 1)
                    for j in range(1, NP + 1):
                        if 2 <= j < NP:
                            convolve(it, j)
                        if j == 1:
                            for k in range(4):
                                pe.wait_ge(*fills.read(it, "fc", k))
                            core.met(pe, "pe")
                            for k in range(2):
                                begin(it, "y", k)
                        pe.wait_ge(*fills.read(it, "c", j - 1))
                        core.met(pe, "pe")
                        for t in range(TT):
                            for n, (a, b) in enumerate(PASSES):
                                last = nc.tensor.matmul(
                                    fills.data("y", t // 2)[:, t % 2 * C:(t % 2 + 1) * C], conv[a][:, (j - 1) % 2, t * P:(t + 1) * P],
                                    fc[b][:, j - 1, :], start=j == 1 and t % 2 == 0 and n == 0, stop=j == NP and n == 2,
                                    skip_group_check=True)
                            if j == NP and t % 2 == 1:
                                last.then_inc(fills.filled("y", t // 2), 1)

                rounds(pe, batch, step)


class FeedForward:

    def __init__(self, nc, ctx, run):
        self.run = run
        split = lambda name, shape: [sbuf(nc, ctx, f"{name}_{part}_{run}", shape, F32R) for part in ("hi", "lo")]
        self.k = split("k_rwkv", [P, 2, CT, HID])
        self.v = split("v_rwkv", [P, 2, HT, C])
        self.square = {n: split(n.lower() + "_ff", [P, CT, C]) for n in ("Wr", "Wv", "Wo", "W1", "W3", "WsW2")}
        self.router = split("router", [P, CT, 8])
        self.bias = sbuf(nc, ctx, f"bias_ff_{run}", [P, NH + 16])
        self.shares = sbuf(nc, ctx, f"shares_{run}", [P, EXPERTS])

    def bias_of(self, name, k):
        at = self.bias_column(name, k)
        return self.bias[:, at:at + 1]

    def bias_column(self, name, k):
        return NH + 2 * ("Wr", "Wv", "WsW2", "W1").index(name) + k


TURN_SLOT, R_SLOT, V_SLOT, S_SLOT, ATT_SLOT, TURN2_SLOT = 3, 4, 5, 7, 9, 13
W3_SLOT = 3
PIECE_SLOTS = (TURN_SLOT - 1, TURN_SLOT - 1, TURN_SLOT, TURN_SLOT, V_SLOT + 1, ATT_SLOT - 1, ATT_SLOT - 1, ATT_SLOT,
               TURN2_SLOT - 1, TURN2_SLOT, TURN2_SLOT, TURN2_SLOT + 1, TURN2_SLOT + 1)
PRODUCT_SLOT, ROUTER_SLOT = V_SLOT, V_SLOT + 1
BIAS_SLOTS = (TURN_SLOT, TURN_SLOT, R_SLOT, ATT_SLOT, ATT_SLOT, ATT_SLOT, TURN2_SLOT)
AHEAD = 2
SQ_RING = AHEAD + 1


FF_SIGNALS = ("stats_done", "mv_done", "norm_steps", "xn_done", "xq_done", "xT_hi", "gate_done", "gate2_done", "g_done", "g_hi", "g_lo",
    "x1_done", "x1_added", "stats2_done", "mv2_done", "norm2_steps", "hq_done", "hT_hi", "t_done", "t_hi", "t_lo",
    "square_hi", "square_done", "hidden_done", "route_steps", "sig_done", "x_steps")


def feed_forward(core, ff, s, dram, out_dram=None):
    nc, banks, x = core.nc, core.banks, core.x
    with ExitStack() as ctx:
        base = ff.run * B
        x_at = lambda n: (n - base) * XB
        buf = lambda name, shape, dtype=F32: sbuf(nc, ctx, f"{name}_{ff.run}", shape, dtype)
        split = lambda name, shape: [buf(f"{name}_{part}", shape, F32R) for part in ("hi", "lo")]
        stats, mv = buf("f_stats", [P, TT, 6]), buf("f_mv", [P, TT, 2])
        stats2, mv2 = buf("f_stats2", [P, TT, 6]), buf("f_mv2", [P, TT, 2])
        var1, rstd, part, part2, var2, rstd2, both = (
            buf(n, [P, TT]) for n in ("f_var1", "f_rstd", "f_part", "f_part2", "f_var2", "f_rstd2", "f_both"))
        var3, rstd3 = buf("f_var3", [P, TT]), buf("f_rstd3", [P, TT])
        xn, xq, x1 = (buf(n, [P, TT, C]) for n in ("f_xn", "f_xq", "f_x1"))
        hq = xq
        xT, hT, gT = (split(n, [P, CT, T]) for n in ("f_xT", "f_hT", "f_gT"))
        tT = gT
        gate, gate2, g = (buf(n, [P, CT, T]) for n in ("f_gate", "f_gate2", "f_g"))
        r, sq = buf("f_relu", [P, 2, T]), buf("f_square", [P, 2, T])
        h2 = split("f_hidden", [P, SQ_RING, T])
        logits, sig = buf("f_logits", [P, TT, 8]), buf("f_sig", [P, TT, 4])
        bids, win, one, conf = (buf(n, [P, TT, EXPERTS]) for n in ("f_bids", "f_win", "f_one", "f_conf"))
        top, wc, wc_eps, rcp, both_off = (buf(n, [P, TT]) for n in ("f_top", "f_wc", "f_wc_eps", "f_rcp", "f_taken"))
        coef = buf("f_coef", [P, TT, EXPERTS])
        stored = ctx.enter_context(nc.semaphore(f"stored_{ff.run}"))
        raw = [w[:].rearrange("p a n -> p (a n)") for w in (r, sq)] + [buf(f"raw{n}", [P, HID])[:] for n in range(2)]
        RING = len(raw)
        norms = buf("norms", [P, 4, CT])
        wsT, w2, product = (buf(n, [P, CT, C]) for n in ("wsT", "w2", "ws_w2"))
        router, offsets = buf("router_raw", [P, CT, 8]), buf("ln2_offsets", [P, CT, P])
        sem = lambda name: ctx.enter_context(nc.semaphore(f"{name}_{ff.run}"))
        loaded = [sem(f"raw_loaded{n}") for n in range(RING)]
        norms_loaded, small_loaded, hi_done, lo_done, used, offsets_done = map(
            sem, ("norms_loaded", "small_loaded", "w_hi_done", "w_lo_done", "w_biases_done", "offsets_done"))
        NORMS, SMALL = 4 * 16, 4 * 16
        pieces = []
        flat = lambda tile: [w[:].rearrange("p k n -> p (k n)") for w in tile]
        by_rows = lambda ap: ap.rearrange("(k p) n -> p k n", p=P)
        for name, norm in (("Wr", 0), ("Wv", 0), ("Wo", None), ("W1", 2), ("W3", None)):
            sections = [(None, None, 0, CT * C)] if norm is None else [(norm, k, k * C, C) for k in range(CT)]
            biases = [] if norm is None else [(ff.bias_column(name, o), k * C + o * P, k) for o in range(CT) for k in range(CT)]
            pieces.append((by_rows(dram[name]), flat(ff.square[name]), sections, biases))
        for e in range(2):
            for k in range(CT):
                pieces.append((dram["K_rwkv"][e, k * P:(k + 1) * P, :], [w[:, e, k, :] for w in ff.k], [(2, k, 0, HID)],
                               [(e * HT + c, c * P, k) for c in range(HT)]))
        for e in range(2):
            for half in range(2):
                rows, tiles = slice(half * HID // 2, (half + 1) * HID // 2), slice(half * HT // 2, (half + 1) * HT // 2)
                pieces.append((by_rows(dram["V_rwkv"][e, rows, :]), [w[:, e, tiles, :].rearrange("p s c -> p (s c)") for w in ff.v],
                               [(None, None, 0, HID)], []))
        splits = {slot: [(n, q) for n in range(len(pieces)) if PIECE_SLOTS[n] == slot for q in range(len(pieces[n][2]))]
                  + [("product", k) for k in range(CT) if slot == PRODUCT_SLOT] + [("router", k) for k in range(CT) if slot == ROUTER_SLOT]
                  for slot in range(NH)}
        order = [part for slot in range(NH) for part in splits[slot]]
        part_at = {part: n for n, part in enumerate(order)}
        split_count = lambda n: part_at[n, len(pieces[n][2]) - 1] + 1
        with_bias = [n for n, piece in enumerate(pieces) if piece[3]]
        bias_slot = dict(zip(with_bias, BIAS_SLOTS))
        early, late = with_bias[:2], with_bias[2:]
        width = lambda n: sum(section[3] for section in pieces[n][2])
        norm_of = lambda norm, k: norms[:, norm, k:k + 1]

        def section(part):
            n, q = part
            if n == "product":
                return product[:, q, :], [w[:, q, :] for w in ff.square["WsW2"]], norm_of(0, q)
            if n == "router":
                return router[:, q, :], [w[:, q, :] for w in ff.router], norm_of(2, q)
            norm, k, at, size = pieces[n][2][q]
            return raw[n % RING][:, at:at + size], [w[:, at:at + size] for w in pieces[n][1]], 1.0 if norm is None else norm_of(norm, k)

        setup = Fills(banks, [(("product",), 0), (("early",), 1), (("middle",), 2), (("late",), 3)])
        NORM_STEPS, ROUTE_STEPS = 7, 14
        X_STEPS = EXPERTS * TT

        def front_order():
            yield TURN_SLOT, [("xT", k) for k in range(CT)]
            yield R_SLOT, [("r", k) for k in range(CT)]
            for k in range(CT):
                yield V_SLOT + k, [("v", k)]
            for k in range(CT):
                yield S_SLOT + k, [("s", k)]
            yield ATT_SLOT, [("att", k) for k in range(2)]
            yield TURN2_SLOT, [("hT", k) for k in range(CT)]

        in_slot = dict(front_order())

        def place(heavy, front):
            order, side = [], 0
            names = [("u", 0), ("u", 1), ("route",)] if heavy else []
            for slot in range(NH):
                names += in_slot.get(slot, []) if front else []
            for n in names:
                order.append((n, 6 + side % 2))
                side += 1
            if heavy:
                order += [(("h", t), t % 2) for t in range(NH)]
                order += [(("w3", k), 4 + k) for k in range(2)]
                order += [(("e", e, k), 2 + 2 * e + k) for e in range(2) for k in range(2)]
            return order

        first = Fills(banks, place(False, True))
        loop = Fills(banks, place(True, True), B - 1)
        last_fills = Fills(banks, place(True, False))

        def rounds(eng, front, heavy, prepare):
            for slot in range(NH):
                front(first, 0, base, slot)
                prepare(slot)
            with eng.Fori(0, B - 1) as it:
                heavy(loop, it, it + base, -1)
                for slot in range(NH):
                    heavy(loop, it, it + base, slot)
                    front(loop, it, it + 1 + base, slot)
            heavy(last_fills, 0, base + B - 1, -1)
            for slot in range(NH):
                heavy(last_fills, 0, base + B - 1, slot)

        with nc.Block() as block:

            @block.sync
            def _(sp):
                def load(n):
                    piece = pieces[n][0]
                    if n >= RING:
                        sp.wait_ge(lo_done, split_count(n - RING))
                        if n - RING in with_bias:
                            sp.wait_ge(used, with_bias.index(n - RING) + 1)
                    dst = raw[n % RING][:, 0:width(n)]
                    if len(piece.shape) == 3:
                        dst = dst.rearrange("p (k n) -> p k n", k=piece.shape[1])
                    sp.dma_start(dst, piece).then_inc(loaded[n % RING], 16)

                for n, name in enumerate(("ln1_w", "ln1_b", "ln2_w", "ln2_b")):
                    sp.dma_start(norms[:, n, :], dram[name]).then_inc(norms_loaded, 16)
                for n in early:
                    load(n)
                for dst, name in ((wsT, "WsT"), (w2, "W2"), (router, "router")):
                    sp.dma_start(dst[:], by_rows(dram[name])).then_inc(small_loaded, 16)
                sp.dma_start(ff.shares[:], dram["capital_shares"].partition_broadcast(P)).then_inc(small_loaded, 16)
                for n in range(len(early), len(pieces)):
                    load(n)
                if out_dram is not None:
                    with sp.Fori(0, B) as it:
                        sp.wait_ge(s["x_steps"], (it + base) * X_STEPS + X_STEPS)
                        core.met(sp, "sp")
                        sp.dma_start(out_dram[bass.ds(it * T, T), :].rearrange("(t p) c -> p t c", p=P),
                                     cols(x, x_at(it + base), XB).rearrange("p (t c) -> p t c", c=C)).then_inc(stored, 16)
                    sp.wait_ge(stored, 16 * B)

            @block.vector
            def _(dve):
                def two_parts(fl, it, name, hi_sem, count, hi, lo, done=None):
                    dve.wait_ge(hi_sem, count)
                    core.met(dve, "dve")
                    nc.vector.tensor_tensor(lo, fl.data(*name)[:], hi.bitcast(F32), ALU.subtract).then_inc(fl.released(*name), 1)

                def front(fl, it, n, slot):
                    if slot == 0:
                        dve.wait_ge(s["norm_steps"], n * NORM_STEPS)
                        core.met(dve, "dve")
                        for t in range(TT):
                            nc.vector.bn_stats(stats[:, t, :], cols(x, x_at(n) + t * C, C)).then_inc(s["stats_done"], 1)
                        for t in range(TT):
                            dve.wait_ge(s["stats_done"], n * TT + t + 1)
                            core.met(dve, "dve")
                            nc.vector.bn_aggr(mv[:, t, :], stats[:, t, :]).then_inc(s["mv_done"], 1)
                    if slot == 2:
                        dve.wait_ge(s["norm_steps"], n * NORM_STEPS + NORM_STEPS)
                        core.met(dve, "dve")
                        for t in range(TT):
                            xs = cols(x, x_at(n) + t * C, C)
                            nc.vector.tensor_scalar(xq[:, t, :], xs, mv[:, t, 0:1], both[:, t:t + 1], ALU.subtract, ALU.mult).then_inc(
                                s["xq_done"], 1)
                        for t in range(TT):
                            xs = cols(x, x_at(n) + t * C, C)
                            nc.vector.tensor_scalar(xn[:, t, :], xs, mv[:, t, 0:1], rstd[:, t:t + 1], ALU.subtract, ALU.mult).then_inc(
                                s["xn_done"], 1)
                    if slot == TURN_SLOT:
                        for k in range(CT):
                            two_parts(fl, it, ("xT", k), s["xT_hi"], n * CT + k + 1, xT[0][:, k], xT[1][:, k])
                    for k in range(CT):
                        if slot == V_SLOT + k:
                            dve.wait_ge(*fl.full(it, "v", k))
                            dve.wait_ge(s["gate_done"], n * CT + k + 1)
                            core.met(dve, "dve")
                            nc.vector.scalar_tensor_tensor(out=g[:, k], in0=fl.data("v", k)[:], scalar=ff.bias_of("Wv", k), in1=gate[:, k],
                                                           op0=ALU.add, op1=ALU.mult).then_inc(fl.released("v", k), 1)
                        if slot == V_SLOT + k + 1:
                            dve.wait_ge(s["g_hi"], n * CT + k + 1)
                            core.met(dve, "dve")
                            nc.vector.tensor_tensor(gT[1][:, k], g[:, k], gT[0][:, k].bitcast(F32), ALU.subtract).then_inc(s["g_lo"], 1)
                    if slot == ATT_SLOT:
                        dve.wait_ge(s["xn_done"], n * TT + TT)
                        dve.wait_ge(s["x1_added"], n * 2)
                        for k in range(2):
                            dve.wait_ge(*fl.full(it, "att", k))
                            core.met(dve, "dve")
                            nc.vector.tensor_tensor(x1[:, 2 * k:2 * k + 2, :], xn[:, 2 * k:2 * k + 2, :],
                                                    fl.data("att", k)[:].rearrange("p (t c) -> p t c", c=C), ALU.add).then_inc(
                                fl.released("att", k), 1)
                        for t in range(TT):
                            dve.wait_ge(*fl.read(it, "att", t // 2))
                            core.met(dve, "dve")
                            nc.vector.bn_stats(stats2[:, t, :], x1[:, t, :]).then_inc(s["stats2_done"], 1)
                        for t in range(TT):
                            dve.wait_ge(s["stats2_done"], n * TT + t + 1)
                            core.met(dve, "dve")
                            nc.vector.bn_aggr(mv2[:, t, :], stats2[:, t, :]).then_inc(s["mv2_done"], 1)
                    if slot == TURN2_SLOT - 1:
                        dve.wait_ge(s["norm2_steps"], n * 2 + 2)
                        core.met(dve, "dve")
                        for t in range(TT):
                            nc.vector.tensor_scalar(hq[:, t, :], x1[:, t, :], mv2[:, t, 0:1], rstd3[:, t:t + 1], ALU.subtract,
                                                    ALU.mult).then_inc(s["hq_done"], 1)
                    if slot == TURN2_SLOT:
                        for k in range(CT):
                            dve.wait_ge(s["hT_hi"], n * CT + k + 1)
                            core.met(dve, "dve")
                            nc.vector.tensor_tensor(hT[1][:, k], fl.data("hT", k)[:], hT[0][:, k].bitcast(F32), ALU.subtract).then_inc(
                                fl.released("hT", k), 1)

                def add_expert(fl, it, i, e, name, step):
                    dve.wait_ge(s["route_steps"], i * ROUTE_STEPS + ROUTE_STEPS)
                    if step == 0:
                        dve.wait_ge(s["x1_added"], i * 2 + 2)
                    else:
                        dve.wait_ge(s["x_steps"], i * X_STEPS + step * TT)
                    for t in range(TT):
                        bank = (*name, t // 2)
                        dve.wait_ge(*fl.full(it, *bank))
                        core.met(dve, "dve")
                        xs = cols(x, x_at(i) + t * C, C)
                        nc.vector.scalar_tensor_tensor(out=xs, in0=fl.data(*bank)[:, t % 2 * C:(t % 2 + 1) * C],
                                                       scalar=coef[:, t, e:e + 1], in1=xs, op0=ALU.mult, op1=ALU.add).then_inc(
                            s["x_steps"], 1)
                        if t % 2 == 1:
                            dve.wait_ge(s["x_steps"], i * X_STEPS + step * TT + t + 1)
                            dve.sem_inc(fl.released(*bank), 1)

                def route_logits(fl, it, i):
                    dve.wait_ge(*fl.full(it, "route"))
                    core.met(dve, "dve")
                    nc.vector.tensor_tensor(logits[:], fl.data("route")[:, 0:TT * 8].rearrange("p (t e) -> p t e", e=8),
                                            ff.bias[:, NH + 8:NH + 16].unsqueeze(1).to_broadcast([P, TT, 8]), ALU.add).then_inc(
                        fl.released("route"), 1)

                def route(fl, it, i):
                    step = 0

                    def after(instruction):
                        nonlocal step
                        step += 1
                        instruction.then_inc(s["route_steps"], 1)
                        dve.wait_ge(s["route_steps"], i * ROUTE_STEPS + step)
                        core.met(dve, "dve")

                    dve.wait_ge(s["sig_done"], i + 1)
                    core.met(dve, "dve")
                    v = nc.vector
                    spread = lambda ap: ap.unsqueeze(2).to_broadcast([P, TT, EXPERTS])
                    conf_now = sig[:, :, 0:EXPERTS]
                    after(v.tensor_tensor(bids[:], conf_now, ff.shares[:].unsqueeze(1).to_broadcast([P, TT, EXPERTS]), ALU.mult))
                    after(v.tensor_tensor(bids[:], bids[:], spread(sig[:, :, 3]), ALU.mult))
                    after(v.tensor_tensor(bids[:], bids[:], logits[:, :, 4:7], ALU.add))
                    after(v.tensor_reduce(top[:], bids[:], AX_X, ALU.max))
                    after(v.tensor_tensor(win[:], bids[:], spread(top[:]), ALU.is_ge))
                    after(v.tensor_scalar(one[:, :, 0], win[:, :, 0], 1.0, None, ALU.mult))
                    after(v.tensor_tensor(one[:, :, 1], win[:, :, 1], win[:, :, 0], ALU.is_gt))
                    after(v.tensor_tensor(both_off[:], win[:, :, 0], win[:, :, 1], ALU.max))
                    after(v.tensor_tensor(one[:, :, 2], win[:, :, 2], both_off[:], ALU.is_gt))
                    after(v.tensor_tensor(conf[:], one[:], conf_now, ALU.mult))
                    after(v.tensor_reduce(wc[:], conf[:], AX_X, ALU.add))
                    after(v.tensor_scalar(wc_eps[:], wc[:], 1e-6, None, ALU.add))
                    after(v.reciprocal(rcp[:], wc_eps[:]))
                    after(v.tensor_tensor(coef[:], conf[:], spread(rcp[:]), ALU.mult))

                def heavy(fl, it, i, slot):
                    if slot + 1 < NH:
                        t = slot + 1
                        dve.wait_ge(s["square_hi"], i * NH + t + 1)
                        dve.wait_ge(s["square_done"], i * NH + t + 1)
                        core.met(dve, "dve")
                        nc.vector.tensor_tensor(h2[1][:, t % SQ_RING], sq[:, t % 2], h2[0][:, t % SQ_RING].bitcast(F32),
                                                ALU.subtract).then_inc(s["hidden_done"], 1)
                    if slot == 0:
                        for k in range(CT):
                            dve.wait_ge(*fl.full(it, "u", k))
                            dve.wait_ge(s["gate2_done"], i * CT + k + 1)
                            core.met(dve, "dve")
                            nc.vector.scalar_tensor_tensor(out=g[:, k], in0=fl.data("u", k)[:], scalar=ff.bias_of("W1", k), in1=gate2[:, k],
                                                           op0=ALU.add, op1=ALU.mult).then_inc(fl.released("u", k), 1)
                    if slot == 1:
                        route_logits(fl, it, i)
                        for k in range(CT):
                            dve.wait_ge(s["t_hi"], i * CT + k + 1)
                            core.met(dve, "dve")
                            nc.vector.tensor_tensor(tT[1][:, k], g[:, k], tT[0][:, k].bitcast(F32), ALU.subtract).then_inc(s["t_lo"], 1)
                    if slot == 3:
                        route(fl, it, i)
                    if slot == W3_SLOT + 1:
                        add_expert(fl, it, i, 2, ("w3",), 0)
                    if slot == HT:
                        add_expert(fl, it, i, 0, ("e", 0), 1)
                    if slot == NH - 1:
                        add_expert(fl, it, i, 1, ("e", 1), 2)

                def prepare(slot):
                    if slot == TURN_SLOT - 1:
                        dve.wait_ge(norms_loaded, NORMS)
                    if slot == ROUTER_SLOT:
                        dve.wait_ge(small_loaded, SMALL)
                    for part in splits[slot]:
                        src, (hi, lo), scale = section(part)
                        dve.wait_ge(hi_done, part_at[part] + 1)
                        nc.vector.scalar_tensor_tensor(out=lo, in0=src, scalar=scale, in1=hi.bitcast(F32), op0=ALU.mult,
                                                       op1=ALU.subtract).then_inc(lo_done, 1)
                    if slot == TURN_SLOT:
                        for k in range(CT):
                            nc.vector.tensor_scalar(offsets[:, k, :], core.ident[:], 0.0, norm_of(3, k), ALU.mult, ALU.add).then_inc(
                                offsets_done, 1)
                        dve.wait_ge(*setup.read(0, "early"))
                        core.met(dve, "dve")
                    if slot == NH - 1:
                        dve.wait_ge(*setup.read(0, "middle"))
                        dve.wait_ge(*setup.read(0, "late"))
                        core.met(dve, "dve")

                rounds(dve, front, heavy, prepare)

            @block.gpsimd
            def _(pool):
                def front(fl, it, n, slot):
                    g_ = nc.gpsimd
                    if slot == 0:
                        step = 0

                        def after(instruction):
                            nonlocal step
                            step += 1
                            instruction.then_inc(s["norm_steps"], 1)
                            pool.wait_ge(s["norm_steps"], n * NORM_STEPS + step)
                            core.met(pool, "pool")

                        pool.wait_ge(s["mv_done"], n * TT + TT)
                        pool.wait_ge(s["xn_done"], n * TT)
                        core.met(pool, "pool")
                        after(g_.tensor_scalar(var1[:], mv[:, :, 1], EPS, None, ALU.add))
                        after(g_.tensor_tensor(rstd[:], var1[:], core.neg_half[:], ALU.pow))
                        after(g_.tensor_tensor(part[:], mv[:, :, 1], rstd[:], ALU.mult))
                        after(g_.tensor_tensor(part2[:], part[:], rstd[:], ALU.mult))
                        after(g_.tensor_scalar(var2[:], part2[:], EPS, None, ALU.add))
                        after(g_.tensor_tensor(rstd2[:], var2[:], core.neg_half[:], ALU.pow))
                        after(g_.tensor_tensor(both[:], rstd[:], rstd2[:], ALU.mult))
                    if slot == ATT_SLOT + 1:
                        pool.wait_ge(s["mv2_done"], n * TT + TT)
                        pool.wait_ge(s["hq_done"], n * TT)
                        core.met(pool, "pool")
                        g_.tensor_scalar(var3[:], mv2[:, :, 1], EPS, None, ALU.add).then_inc(s["norm2_steps"], 1)
                        pool.wait_ge(s["norm2_steps"], n * 2 + 1)
                        core.met(pool, "pool")
                        g_.tensor_tensor(rstd3[:], var3[:], core.neg_half[:], ALU.pow).then_inc(s["norm2_steps"], 1)
                        pool.wait_ge(s["xn_done"], n * TT + TT)
                        for k in range(2):
                            pool.wait_ge(*fl.read(it, "att", k))
                            core.met(pool, "pool")
                            xs = cols(x, x_at(n) + k * 512, 512)
                            g_.tensor_tensor(xs, xs, x1[:, 2 * k:2 * k + 2, :].rearrange("p t c -> p (t c)"), ALU.add).then_inc(s["x1_added"], 1)

                def square(fl, it, i, t):
                    pool.wait_ge(*fl.read(it, "h", t))
                    if t >= 2:
                        pool.wait_ge(s["hidden_done"], i * NH + t - 1)
                    core.met(pool, "pool")
                    nc.gpsimd.tensor_tensor(sq[:, t % 2], r[:, t % 2], r[:, t % 2], ALU.mult).then_inc(s["square_done"], 1)

                def heavy(fl, it, i, slot):
                    for t in range(AHEAD) if slot == -1 else [slot + AHEAD]:
                        if t < NH:
                            square(fl, it, i, t)

                rounds(pool, front, heavy, lambda slot: None)

            @block.scalar
            def _(act):
                def first_part(fl, it, name, dst, done):
                    act.wait_ge(*fl.full(it, *name))
                    nc.scalar.activation(dst, fl.data(*name)[:], ACT.Copy).then_inc(done, 1)

                def gated(fl, it, name, dst, bias, done):
                    act.wait_ge(*fl.full(it, *name))
                    nc.scalar.activation(dst, fl.data(*name)[:], ACT.Sigmoid, bias=bias).then_inc(fl.released(*name), 1)
                    act.wait_ge(*fl.read(it, *name))
                    act.sem_inc(done, 1)

                def front(fl, it, n, slot):
                    if slot == TURN_SLOT:
                        for k in range(CT):
                            first_part(fl, it, ("xT", k), xT[0][:, k], s["xT_hi"])
                    if slot == R_SLOT:
                        for k in range(CT):
                            gated(fl, it, ("r", k), gate[:, k], ff.bias_of("Wr", k), s["gate_done"])
                    for k in range(CT):
                        if slot == V_SLOT + k:
                            act.wait_ge(*fl.read(it, "v", k))
                            nc.scalar.activation(gT[0][:, k], g[:, k], ACT.Copy).then_inc(s["g_hi"], 1)
                        if slot == S_SLOT + k:
                            gated(fl, it, ("s", k), gate2[:, k], ff.bias_of("WsW2", k), s["gate2_done"])
                    if slot == TURN2_SLOT:
                        for k in range(CT):
                            first_part(fl, it, ("hT", k), hT[0][:, k], s["hT_hi"])

                def hidden(fl, it, i, t):
                    if t >= 2:
                        act.wait_ge(s["square_done"], i * NH + t - 1)
                    act.wait_ge(*fl.full(it, "h", t))
                    nc.scalar.activation(r[:, t % 2], fl.data("h", t)[:], ACT.Relu, bias=ff.bias[:, t:t + 1]).then_inc(fl.released("h", t), 1)
                    act.wait_ge(*fl.read(it, "h", t))
                    nc.scalar.activation(h2[0][:, t % SQ_RING], r[:, t % 2], ACT.Square).then_inc(s["square_hi"], 1)

                def heavy(fl, it, i, slot):
                    if slot == -1:
                        for t in range(AHEAD):
                            hidden(fl, it, i, t)
                    elif slot + AHEAD < NH:
                        hidden(fl, it, i, slot + AHEAD)
                    if slot == 0:
                        for k in range(CT):
                            act.wait_ge(*fl.read(it, "u", k))
                            nc.scalar.activation(tT[0][:, k], g[:, k], ACT.Copy).then_inc(s["t_hi"], 1)
                    if slot == 2:
                        act.wait_ge(*fl.read(it, "route"))
                        nc.scalar.activation(sig[:], logits[:, :, 0:4], ACT.Sigmoid).then_inc(s["sig_done"], 1)

                def bias(name, at, size):
                    act.wait_ge(*setup.full(0, name))
                    return nc.scalar.activation(ff.bias[:, at:at + size], setup.data(name)[:, at:at + size], ACT.Copy)

                def prepare(slot):
                    if slot == TURN_SLOT - 1:
                        act.wait_ge(norms_loaded, NORMS)
                    if slot == TURN_SLOT:
                        bias("early", NH, 4).then_inc(setup.released("early"), 1)
                    if slot == PRODUCT_SLOT:
                        act.wait_ge(*setup.full(0, "product"))
                        nc.scalar.activation(product[:].rearrange("p k n -> p (k n)"), setup.data("product")[:], ACT.Copy).then_inc(
                            setup.released("product"), 1)
                        act.wait_ge(*setup.read(0, "product"))
                    if slot == ROUTER_SLOT:
                        act.wait_ge(small_loaded, SMALL)
                    for part in splits[slot]:
                        if part[0] not in ("product", "router"):
                            act.wait_ge(loaded[part[0] % RING], 16 * (part[0] // RING + 1))
                        src, (hi, _), scale = section(part)
                        nc.scalar.activation(hi, src, ACT.Copy, scale=scale).then_inc(hi_done, 1)
                    if slot == TURN_SLOT:
                        act.wait_ge(*setup.read(0, "early"))
                    if slot == ROUTER_SLOT:
                        bias("middle", NH + 4, 2)
                        bias("middle", NH + 8, 8).then_inc(setup.released("middle"), 1)
                        act.wait_ge(*setup.read(0, "middle"))
                    if slot == NH - 1:
                        bias("late", 0, NH)
                        bias("late", NH + 6, 2).then_inc(setup.released("late"), 1)
                        act.wait_ge(*setup.read(0, "late"))
                        act.wait_ge(lo_done, len(order))

                rounds(act, front, heavy, prepare)

            @block.tensor
            def _(pe):
                def begin(fl, it, *name):
                    pe.wait_ge(*fl.free(it, *name))
                    core.met(pe, "pe")
                    return fl.data(*name)

                PASSES = ((0, 0), (0, 1), (1, 0))

                def to_features(fl, it, name, weight, src, o):
                    data = begin(fl, it, *name)
                    steps = [(k, a, b) for k in range(CT) for a, b in PASSES]
                    for n, (k, a, b) in enumerate(steps):
                        last = nc.tensor.matmul(data[:], weight[a](k, o), src[b][:, k], start=n == 0, stop=n == len(steps) - 1)
                    last.then_inc(fl.filled(*name), 1)

                square = lambda name: [lambda k, o, w=w: w[:, k, o * P:(o + 1) * P] for w in ff.square[name]]

                def to_tokens(fl, it, name, src, weight):
                    steps = [(k, a, b) for k in range(CT) for a, b in PASSES]
                    for bank in range(2):
                        data = begin(fl, it, name, bank)
                        for t in (2 * bank, 2 * bank + 1):
                            for n, (k, a, b) in enumerate(steps):
                                last = nc.tensor.matmul(data[:, t % 2 * C:(t % 2 + 1) * C], src[a][:, k, t * P:(t + 1) * P],
                                                        ff.square[weight][b][:, k, :], start=n == 0, stop=n == len(steps) - 1)
                        last.then_inc(fl.filled(name, bank), 1)

                def turn(fl, it, name, src):
                    for k in range(CT):
                        data = begin(fl, it, name, k)
                        for t in range(TT):
                            last = nc.tensor.transpose(data[:, t * P:(t + 1) * P], src[:, t, k * P:(k + 1) * P], core.ident[:])
                        last.then_inc(fl.filled(name, k), 1)

                def front(fl, it, n, slot):
                    if slot == TURN_SLOT:
                        pe.wait_ge(s["xq_done"], n * TT + TT)
                        turn(fl, it, "xT", xq)
                    if slot == R_SLOT:
                        for k in range(CT):
                            pe.wait_ge(*fl.read(it, "xT", k))
                        for k in range(CT):
                            to_features(fl, it, ("r", k), square("Wr"), xT, k)
                    for k in range(CT):
                        if slot == V_SLOT + k:
                            to_features(fl, it, ("v", k), square("Wv"), xT, k)
                        if slot == S_SLOT + k:
                            to_features(fl, it, ("s", k), square("WsW2"), xT, k)
                    if slot == ATT_SLOT:
                        pe.wait_ge(s["g_lo"], n * CT + CT)
                        to_tokens(fl, it, "att", gT, "Wo")
                    if slot == TURN2_SLOT:
                        pe.wait_ge(s["hq_done"], n * TT + TT)
                        turn(fl, it, "hT", hq)
                    if slot == NH - 1:
                        for k in range(CT):
                            pe.wait_ge(*fl.read(it, "hT", k))
                        core.met(pe, "pe")

                def hidden(fl, it, t):
                    e, c = t // HT, t % HT
                    to_features(fl, it, ("h", t), [lambda k, o, w=w: w[:, e, k, c * P:(c + 1) * P] for w in ff.k], hT, 0)

                def second(fl, it, i, t):
                    e, c = t // HT, t % HT
                    pe.wait_ge(s["hidden_done"], i * NH + t + 1)
                    if c == 0:
                        for bank in range(2):
                            begin(fl, it, "e", e, bank)
                    core.met(pe, "pe")
                    for tok in range(TT):
                        for n, (a, b) in enumerate(PASSES):
                            last = nc.tensor.matmul(
                                fl.data("e", e, tok // 2)[:, tok % 2 * C:(tok % 2 + 1) * C], h2[a][:, t % SQ_RING, tok * P:(tok + 1) * P],
                                ff.v[b][:, e, c, :], start=c == 0 and n == 0 and tok % 2 == 0, stop=c == HT - 1 and n == 2,
                                skip_group_check=True)
                        if c == HT - 1 and tok % 2 == 1:
                            last.then_inc(fl.filled("e", e, tok // 2), 1)

                def heavy(fl, it, i, slot):
                    if slot == -1:
                        for k in range(CT):
                            hidden(fl, it, k)
                            to_features(fl, it, ("u", k), square("W1"), hT, k)
                        return
                    if slot + AHEAD < NH:
                        hidden(fl, it, slot + AHEAD)
                    second(fl, it, i, slot)
                    if slot == 0:
                        data = begin(fl, it, "route")
                        steps = [(k, a, b) for k in range(CT) for a, b in PASSES]
                        for t in range(TT):
                            for n, (k, a, b) in enumerate(steps):
                                last = nc.tensor.matmul(data[:, t * 8:(t + 1) * 8], hT[a][:, k, t * P:(t + 1) * P], ff.router[b][:, k, :],
                                                        start=n == 0, stop=n == len(steps) - 1)
                        last.then_inc(fl.filled("route"), 1)
                    if slot == W3_SLOT:
                        pe.wait_ge(s["t_lo"], i * CT + CT)
                        to_tokens(fl, it, "w3", tT, "W3")

                def biases(name, n, first_of_bank, last_of_bank):
                    pe.wait_ge(loaded[n % RING], 16 * (n // RING + 1))
                    norm = pieces[n][2][0][0] + 1
                    for q, (column, at, k) in enumerate(pieces[n][3]):
                        last = nc.tensor.matmul(setup.data(name)[:, column:column + 1], raw[n % RING][:, at:at + P], norm_of(norm, k),
                                                start=first_of_bank and q == 0, stop=last_of_bank, skip_group_check=True)
                    last.then_inc(used, 1)

                def prepare(slot):
                    if slot == TURN_SLOT:
                        pe.wait_ge(norms_loaded, NORMS)
                        pe.wait_ge(*setup.free(0, "early"))
                        for n in early:
                            biases("early", n, n == early[0], n == early[-1])
                        pe.wait_ge(used, len(early))
                        pe.sem_inc(setup.filled("early"), 1)
                        pe.wait_ge(lo_done, split_count(early[-1]))
                        core.met(pe, "pe")
                    if slot == PRODUCT_SLOT:
                        pe.wait_ge(small_loaded, SMALL)
                        pe.wait_ge(*setup.free(0, "product"))
                        for o in range(CT):
                            for k in range(CT):
                                last = nc.tensor.matmul(setup.data("product")[:, o * C:(o + 1) * C], wsT[:, k, o * P:(o + 1) * P], w2[:, k, :],
                                                        start=k == 0, stop=k == CT - 1)
                        last.then_inc(setup.filled("product"), 1)
                    if slot == ROUTER_SLOT:
                        pe.wait_ge(offsets_done, CT)
                        pe.wait_ge(*setup.free(0, "middle"))
                        for k in range(CT):
                            nc.tensor.matmul(setup.data("middle")[:, NH + 8:NH + 16], offsets[:, k, :], router[:, k, :], start=k == 0,
                                             stop=k == CT - 1, skip_group_check=True)
                        pe.wait_ge(*setup.read(0, "product"))
                        for o in range(CT):
                            for k in range(CT):
                                column = ff.bias_column("WsW2", o)
                                last = nc.tensor.matmul(setup.data("middle")[:, column:column + 1], product[:, k, o * P:(o + 1) * P], norm_of(1, k),
                                                        start=False, stop=k == CT - 1, skip_group_check=True)
                        last.then_inc(setup.filled("middle"), 1)
                        pe.wait_ge(lo_done, part_at["product", CT - 1] + 1)
                        core.met(pe, "pe")
                    for n in late:
                        if bias_slot[n] == slot:
                            if n == late[0]:
                                pe.wait_ge(*setup.free(0, "late"))
                            biases("late", n, n == late[0], n == late[-1])
                    if slot == NH - 1:
                        pe.wait_ge(used, len(with_bias))
                        pe.sem_inc(setup.filled("late"), 1)
                        pe.wait_ge(lo_done, split_count(late[-1]))
                        core.met(pe, "pe")

                rounds(pe, front, heavy, prepare)


NQUADS = HB // QUAD
PAIRS_B = HB // 2
PAIRS_T = PAIRS_B // CT
LAG = 2
SLOTS_B = HB + LAG + 4
STATS_SLOT, XT_SLOT, QK0_SLOTS, QK1_SLOT, V0_SLOT, SEL0_SLOT = 1, 3, (5, 13), 17, 19, 18
SCORES = ((0, 3, 0), (1, 2, 0), (1, 0, 3 * P), (2, 1, 0))
SCORE_COLS = {3: 0, 2: 4 * P, 0: 7 * P, 1: 8 * P}
TURNED = ((0, 0, 0), (1, 1, 0), (1, 3, 3 * P), (2, 2, 0))
TURNED_COLS = {0: 0, 1: 4 * P, 3: 7 * P, 2: 8 * P}
HEAD_COLS = 10 * P
BANK_COLS = ((0, 4 * P), (4 * P, 4 * P), (8 * P, 2 * P))


def layer_b(core, dram):
    nc, banks, x = core.nc, core.banks, core.x
    with ExitStack() as ctx:
        sem = lambda name: ctx.enter_context(nc.semaphore(name))
        buf = lambda name, shape, dtype=F32: sbuf(nc, ctx, name, shape, dtype)
        wq, wk, wv, wo = (buf(n, [P, CT, C]) for n in ("wq_b", "wk_b", "wv_b", "wo_b"))
        cos, sin = buf("cos", [P, T]), buf("sin", [P, T])
        select = buf("select", [P, 2, 2, PAIRS_T, P], F32R)
        ident16, causal16 = buf("ident16", [P, P], BF16), buf("causal16", [P, P], BF16)
        stats, mv, var1, rstd = buf("b_stats", [P, TT, 6]), buf("b_mv", [P, TT, 2]), buf("b_var", [P, TT]), buf("b_rstd", [P, TT])
        xn, xnT = buf("b_xn", [P, TT, C]), buf("b_xnT", [P, CT, T])
        straight, swapped, turned, rotated = (buf(n, [P, 2, T]) for n in ("b_straight", "b_swapped", "b_turned", "b_rotated"))
        qk = [[buf(f"b_{side}_{part}", [P, CT, T], F32R) for part in ("hi", "lo")] for side in ("q", "k")]
        stacked = [buf(f"b_{side}_stacked", [P, 2, T], F32R) for side in ("q", "k")]
        v = buf("b_v", [P, TT, HB, 2 * DB])
        probs = buf("b_probs", [P, LAG + 1, HEAD_COLS])
        probsT = buf("b_probsT", [P, 2 * QUAD, HEAD_COLS])
        neg_max = buf("b_neg_max", [P, 2, TT])
        raw_select, raw_mask = buf("b_raw_select", [P, 16 * P]), buf("b_raw_mask", [P, P])
        oT = buf("b_oT", [P, 2, T])
        rcp, att, attT = buf("b_rcp", [P, TT, QUAD]), buf("b_att", [P, TT, C]), buf("b_attT", [P, CT, T])
        names = ("loaded", "consts_done", "ones_done", "stats_done", "mv_done", "var_done", "rstd_done", "xn_done", "swap_done", "turn_done", "rot_done",
                 "hi_done", "lo_done", "max_done", "rcp_done")
        s = {n: sem("b_" + n) for n in names}
        LOADS, CONSTS, ONES = 8 * 16, 3, 2

        def stack_steps(slot):
            if slot == 0:
                return [(0, 1), (1, 1)]
            pair = (slot + 3) // 2 if slot % 2 else slot // 2 + 1
            return [((slot + 1) % 2, pair)] if pair < PAIRS_B else []

        def pv_steps(quad, slot):
            at = slot - (QUAD * (quad + 1) + LAG)
            if quad == NQUADS - 1:
                return list(range(TT)) if at == 0 else []
            return {0: [0], 1: [1], 2: [2, 3]}.get(at, [])

        def o_slot(quad):
            return QUAD * (quad + 1) + LAG + (1 if quad == NQUADS - 1 else 3)

        def qk_slot(side, f):
            return QK0_SLOTS[side] if f == 0 else QK1_SLOT

        def fill_order(heavy, front):
            order = []
            add = lambda name, b: order.append((name, b))

            for slot in range(SLOTS_B):
                if heavy and slot < HB:
                    for b in range(3):
                        add(("s", slot, b), b)
                if heavy and LAG <= slot < HB + LAG:
                    for b in range(3):
                        add(("t", slot - LAG, b), 3 + b)
                if heavy:
                    for side_, pair in stack_steps(slot):
                        add(("sel", side_, pair), 7 if (side_, pair) == (1, 1) else 6)
                for quad in range(NQUADS):
                    if heavy and pv_steps(quad, slot)[0:1] == [0]:
                        add(("pv", quad), 7)
                    if heavy and slot == o_slot(quad):
                        add(("o", quad), 7)
                if heavy and slot == HB + LAG + 2:
                    for k in range(CT):
                        add(("attT", k), 3 + k)
                if heavy and slot == HB + LAG + 3:
                    for k in range(2):
                        add(("out", k), 3 + k)
                for k in range(CT):
                    if front and slot == XT_SLOT + k:
                        add(("xT", k), 7)
                for f in range(2):
                    for side_ in range(2):
                        if front and slot == qk_slot(side_, f):
                            add(("qk", side_, f), ((7, 6), (2, 0))[f][side_])
                for k in range(2):
                    if front and slot == V0_SLOT + k:
                        add(("v", k), k)
                if front and slot == SEL0_SLOT:
                    for side_ in range(2):
                        add(("sel", side_, 0), (6, 1)[side_])
            return order

        first = Fills(banks, fill_order(False, True))
        loop = Fills(banks, fill_order(True, True), B - 1)
        last_fills = Fills(banks, fill_order(True, False))

        def rounds(eng, front, heavy, prepare):
            for slot in range(SLOTS_B):
                if slot == QK0_SLOTS[0]:
                    prepare()
                front(first, 0, 0, slot)
            with eng.Fori(0, B - 1) as it:
                for slot in range(SLOTS_B):
                    heavy(loop, it, it, slot)
                    front(loop, it, it + 1, slot)
            for slot in range(SLOTS_B):
                heavy(last_fills, 0, B - 1, slot)

        with nc.Block() as block:

            @block.sync
            def _(sp):
                for dst, name in ((wq, "WqT"), (wk, "WkT"), (wv, "WvT"), (wo, "WoT")):
                    sp.dma_start(dst[:], dram[name].rearrange("(k p) n -> p k n", p=P)).then_inc(s["loaded"], 16)
                for dst, name in ((cos, "cos"), (sin, "sin"), (raw_select, "select"), (raw_mask, "causal")):
                    sp.dma_start(dst[:], dram[name]).then_inc(s["loaded"], 16)
                sp.wait_ge(s["loaded"], LOADS)

            @block.vector
            def _(dve):
                def ready(*waits):
                    for wait in waits:
                        dve.wait_ge(*wait)
                    core.met(dve, "dve")

                def front(fl, it, n, slot):
                    if slot == STATS_SLOT:
                        ready((s["xn_done"], n * TT))
                        for t in range(TT):
                            nc.vector.bn_stats(stats[:, t, :], cols(x, n * XB + t * C, C)).then_inc(s["stats_done"], 1)
                        for t in range(TT):
                            ready((s["stats_done"], n * TT + t + 1))
                            nc.vector.bn_aggr(mv[:, t, :], stats[:, t, :]).then_inc(s["mv_done"], 1)
                    if slot == 2:
                        ready((s["rstd_done"], n + 1))
                        for t in range(TT):
                            nc.vector.tensor_scalar(xn[:, t, :], cols(x, n * XB + t * C, C), mv[:, t, 0:1], rstd[:, t:t + 1],
                                                    ALU.subtract, ALU.mult).then_inc(s["xn_done"], 1)
                    for f in range(2):
                        for side in range(2):
                            if slot == qk_slot(side, f):
                                ready(fl.full(it, "qk", side, f), (s["rot_done"], n * 4 + f * 2))
                                nc.vector.tensor_tensor(straight[:, side], fl.data("qk", side, f)[:], cos[:], ALU.mult)
                                nc.vector.stream_shuffle(swapped[:, side], fl.data("qk", side, f)[:], [i ^ 1 for i in range(32)]).then_inc(
                                    fl.released("qk", side, f), 1)

                def heavy(fl, it, i, slot):
                    if slot < HB:
                        for place, (b, t, at) in enumerate(SCORES):
                            ready(fl.full(it, "s", slot, b))
                            nc.vector.tensor_reduce(neg_max[:, slot % 2, place:place + 1], fl.data("s", slot, b)[:, at:at + (t + 1) * P],
                                                    AX_X, ALU.max, negate=True).then_inc(s["max_done"], 1)
                    if LAG <= slot < HB + LAG:
                        for b in (0, 2):
                            ready(fl.full(it, "t", slot - LAG, b))
                            at, size = BANK_COLS[b]
                            nc.vector.tensor_scalar(probsT[:, (slot - LAG) % (2 * QUAD), at:at + size], fl.data("t", slot - LAG, b)[:, 0:size],
                                                    1.0, None, ALU.mult).then_inc(fl.released("t", slot - LAG, b), 1)
                    for quad in range(NQUADS):
                        if slot == o_slot(quad):
                            ready(fl.full(it, "o", quad))
                            o = fl.data("o", quad)[:].rearrange("p (t h d) -> p t h d", t=TT, h=QUAD)
                            nc.vector.reciprocal(rcp[:], o[:, :, :, DB]).then_inc(s["rcp_done"], 1)
                            ready((s["rcp_done"], i * NQUADS + quad + 1))
                            nc.vector.tensor_tensor(
                                att[:, :, quad * QUAD * DB:(quad + 1) * QUAD * DB].rearrange("p t (h d) -> p t h d", h=QUAD),
                                o[:, :, :, 0:DB], rcp[:].unsqueeze(3).to_broadcast([P, TT, QUAD, DB]), ALU.mult).then_inc(
                                fl.released("o", quad), 1)
                    if slot == HB + LAG + 3:
                        for k in range(2):
                            ready(fl.full(it, "out", k))
                            xs = cols(x, i * XB + k * 512, 512)
                            nc.vector.tensor_tensor(xs, xs, fl.data("out", k)[:], ALU.add).then_inc(fl.released("out", k), 1)

                def prepare():
                    nc.vector.memset(v[:, :, :, DB:], 0.0).then_inc(s["ones_done"], 1)
                    ready((s["ones_done"], 1))
                    nc.vector.memset(v[:, :, :, DB:DB + 1], 1.0).then_inc(s["ones_done"], 1)
                    ready((s["loaded"], LOADS))

                rounds(dve, front, heavy, prepare)

            @block.gpsimd
            def _(pool):
                def ready(*waits):
                    for wait in waits:
                        pool.wait_ge(*wait)
                    core.met(pool, "pool")

                def front(fl, it, n, slot):
                    g = nc.gpsimd
                    if slot == 1:
                        ready((s["mv_done"], n * TT + TT), (s["xn_done"], n * TT))
                        g.tensor_scalar(var1[:], mv[:, :, 1], EPS, None, ALU.add).then_inc(s["var_done"], 1)
                        ready((s["var_done"], n + 1))
                        g.tensor_tensor(rstd[:], var1[:], core.neg_half[:], ALU.pow).then_inc(s["rstd_done"], 1)
                    for f in range(2):
                        for side in range(2):
                            if slot == qk_slot(side, f):
                                step = n * 4 + f * 2 + side + 1
                                ready(fl.read(it, "qk", side, f), (s["lo_done"], n * 4 + f * 2))
                                g.tensor_tensor(turned[:, side], swapped[:, side], sin[:], ALU.mult).then_inc(s["turn_done"], 1)
                                ready((s["turn_done"], step))
                                g.tensor_tensor(rotated[:, side], straight[:, side], turned[:, side], ALU.add).then_inc(s["rot_done"], 1)
                                ready((s["hi_done"], step))
                                hi, lo = qk[side]
                                g.tensor_tensor(lo[:, f], rotated[:, side], hi[:, f].bitcast(F32), ALU.subtract).then_inc(s["lo_done"], 1)

                def heavy(fl, it, i, slot):
                    pass

                def prepare():
                    ready((s["loaded"], LOADS))

                rounds(pool, front, heavy, prepare)

            @block.scalar
            def _(act):
                def copy(fl, it, dst, name, size=T):
                    act.wait_ge(*fl.full(it, *name))
                    nc.scalar.activation(dst, fl.data(*name)[:, 0:size], ACT.Copy).then_inc(fl.released(*name), 1)

                def stacked_copy(fl, it, side, pair):
                    copy(fl, it, stacked[side][:, pair % 2], ("sel", side, pair))

                def front(fl, it, n, slot):
                    for k in range(CT):
                        if slot == XT_SLOT + k:
                            copy(fl, it, xnT[:, k], ("xT", k))
                    for f in range(2):
                        for side in range(2):
                            if slot == (SLOTS_B - 1 if f else qk_slot(side, f) + 2):
                                act.wait_ge(s["rot_done"], n * 4 + f * 2 + side + 1)
                                nc.scalar.activation(qk[side][0][:, f], rotated[:, side], ACT.Copy).then_inc(s["hi_done"], 1)
                    for k in range(2):
                        if slot == V0_SLOT + k:
                            act.wait_ge(*fl.full(it, "v", k))
                            for t in range(2):
                                done = nc.scalar.activation(v[:, 2 * k + t, :, 0:DB],
                                                            fl.data("v", k)[:, t * C:(t + 1) * C].rearrange("p (h d) -> p h d", d=DB), ACT.Copy)
                            done.then_inc(fl.released("v", k), 1)
                    if slot == SEL0_SLOT:
                        for side in range(2):
                            stacked_copy(fl, it, side, 0)

                def heavy(fl, it, i, slot):
                    if slot < HB:
                        h = slot
                        for place, (b, t, at) in enumerate(SCORES):
                            size, to = (t + 1) * P, SCORE_COLS[t]
                            act.wait_ge(s["max_done"], i * HB * TT + h * TT + (1, 3, 3, 4)[place])
                            done = nc.scalar.activation(probs[:, h % (LAG + 1), to:to + size], fl.data("s", h, b)[:, at:at + size], ACT.Exp,
                                                        bias=neg_max[:, h % 2, place:place + 1])
                            if place != 1:
                                done.then_inc(fl.released("s", h, b), 1)
                    if LAG <= slot < HB + LAG:
                        at, size = BANK_COLS[1]
                        copy(fl, it, probsT[:, (slot - LAG) % (2 * QUAD), at:at + size], ("t", slot - LAG, 1), size)
                    for side, pair in stack_steps(slot):
                        stacked_copy(fl, it, side, pair)
                    for quad in range(NQUADS):
                        if pv_steps(quad, slot)[-1:] == [TT - 1]:
                            copy(fl, it, oT[:, quad % 2], ("pv", quad))
                    if slot == HB + LAG + 2:
                        for k in range(CT):
                            copy(fl, it, attT[:, k], ("attT", k))

                def prepare():
                    act.wait_ge(s["loaded"], LOADS)
                    for dst, src in ((select[:].rearrange("p a b c d -> p (a b c d)"), raw_select), (ident16[:], core.ident),
                                     (causal16[:], raw_mask)):
                        nc.scalar.activation(dst, src[:], ACT.Copy).then_inc(s["consts_done"], 1)

                rounds(act, front, heavy, prepare)

            @block.tensor
            def _(pe):
                def begin(fl, it, *name):
                    pe.wait_ge(*fl.free(it, *name))
                    core.met(pe, "pe")
                    return fl.data(*name)

                def stack(fl, it, side, pair):
                    f, j = pair // PAIRS_T, pair % PAIRS_T
                    data = begin(fl, it, "sel", side, pair)
                    for part in range(2):
                        last = nc.tensor.matmul(data[:], select[:, side, part, j, :], qk[side][part][:, f], start=part == 0, stop=part == 1)
                    last.then_inc(fl.filled("sel", side, pair), 1)

                def front(fl, it, n, slot):
                    for k in range(CT):
                        if slot == XT_SLOT + k:
                            pe.wait_ge(s["xn_done"], n * TT + TT)
                            data = begin(fl, it, "xT", k)
                            for t in range(TT):
                                last = nc.tensor.transpose(data[:, t * P:(t + 1) * P], xn[:, t, k * P:(k + 1) * P], core.ident[:])
                            last.then_inc(fl.filled("xT", k), 1)
                    for f in range(2):
                        for side, weight in enumerate((wq, wk)):
                            if slot == qk_slot(side, f):
                                pe.wait_ge(*fl.read(it, "xT", CT - 1))
                                core.met(pe, "pe")
                                data = begin(fl, it, "qk", side, f)
                                for k in range(CT):
                                    last = nc.tensor.matmul(data[:], weight[:, k, f * P:(f + 1) * P], xnT[:, k], start=k == 0, stop=k == CT - 1)
                                last.then_inc(fl.filled("qk", side, f), 1)
                    for b in range(2):
                        if slot == V0_SLOT + b:
                            data = begin(fl, it, "v", b)
                            for t in (2 * b, 2 * b + 1):
                                for k in range(CT):
                                    last = nc.tensor.matmul(data[:, t % 2 * C:(t % 2 + 1) * C], xnT[:, k, t * P:(t + 1) * P], wv[:, k, :],
                                                            start=k == 0, stop=k == CT - 1)
                            last.then_inc(fl.filled("v", b), 1)
                    if slot == SEL0_SLOT:
                        if fl is first:
                            pe.wait_ge(s["consts_done"], CONSTS)
                            pe.wait_ge(s["ones_done"], ONES)
                        pe.wait_ge(s["lo_done"], n * 4 + 2)
                        for side in range(2):
                            stack(fl, it, side, 0)
                    if slot == SLOTS_B - 1:
                        for side in range(2):
                            pe.wait_ge(*fl.read(it, "sel", side, 0))
                        core.met(pe, "pe")

                def heavy(fl, it, i, slot):
                    if slot < HB:
                        h, pair = slot, slot // 2
                        rows = slice(h % 2 * 64, h % 2 * 64 + 64)
                        if h % 2 == 0 and pair:
                            for side in range(2):
                                pe.wait_ge(*fl.read(it, "sel", side, pair))
                                core.met(pe, "pe")
                        for place, (b, t, at) in enumerate(SCORES):
                            data = fl.data("s", h, b) if place == 2 else begin(fl, it, "s", h, b)
                            nc.tensor.matmul(data[:, at:at + (t + 1) * P], stacked[0][rows, pair % 2, t * P:(t + 1) * P],
                                             stacked[1][rows, pair % 2, 0:(t + 1) * P], start=place != 2, stop=False, skip_group_check=True)
                            last = nc.tensor.matmul(data[:, at + t * P:at + (t + 1) * P], ident16[:], causal16[:], start=False, stop=True,
                                                    skip_group_check=True)
                            if place != 1:
                                last.then_inc(fl.filled("s", h, b), 1)
                    if LAG <= slot < HB + LAG:
                        h = slot - LAG
                        for b in range(3):
                            pe.wait_ge(*fl.read(it, "s", h, b))
                        for b in range(3):
                            data = begin(fl, it, "t", h, b)
                            for bank, kt, at in TURNED:
                                if bank == b:
                                    for q in range(kt, TT):
                                        src = SCORE_COLS[q] + kt * P
                                        last = nc.tensor.transpose(data[:, at + (q - kt) * P:at + (q - kt + 1) * P],
                                                                   probs[:, h % (LAG + 1), src:src + P], core.ident[:])
                            last.then_inc(fl.filled("t", h, b), 1)
                    for side, pair in stack_steps(slot):
                        if pair == PAIRS_T:
                            pe.wait_ge(s["lo_done"], i * 4 + 4)
                        stack(fl, it, side, pair)
                    for quad in range(NQUADS):
                        steps = pv_steps(quad, slot)
                        if steps:
                            heads = range(quad * QUAD, (quad + 1) * QUAD)
                            if steps[0] == 0:
                                for b in range(3):
                                    pe.wait_ge(*fl.read(it, "t", heads[-1], b))
                                core.met(pe, "pe")
                                begin(fl, it, "pv", quad)
                            data = fl.data("pv", quad)
                            for kt in steps:
                                at, size = TURNED_COLS[kt], T - kt * P
                                for n, h in enumerate(heads):
                                    last = nc.tensor.matmul(data[n * 32:(n + 1) * 32, kt * P:], v[:, kt, h, :],
                                                            probsT[:, h % (2 * QUAD), at:at + size], start=kt == 0, stop=kt == TT - 1,
                                                            skip_group_check=True)
                            if steps[-1] == TT - 1:
                                last.then_inc(fl.filled("pv", quad), 1)
                        if slot == o_slot(quad):
                            pe.wait_ge(*fl.read(it, "pv", quad))
                            data = begin(fl, it, "o", quad)
                            for t in range(TT):
                                last = nc.tensor.transpose(data[:, t * P:(t + 1) * P], oT[:, quad % 2, t * P:(t + 1) * P], core.ident[:])
                            last.then_inc(fl.filled("o", quad), 1)
                    if slot == HB + LAG + 2:
                        pe.wait_ge(*fl.read(it, "o", NQUADS - 1))
                        for k in range(CT):
                            data = begin(fl, it, "attT", k)
                            for t in range(TT):
                                last = nc.tensor.transpose(data[:, t * P:(t + 1) * P], att[:, t, k * P:(k + 1) * P], core.ident[:])
                            last.then_inc(fl.filled("attT", k), 1)
                    if slot == HB + LAG + 3:
                        for k in range(CT):
                            pe.wait_ge(*fl.read(it, "attT", k))
                        for b in range(2):
                            data = begin(fl, it, "out", b)
                            for t in (2 * b, 2 * b + 1):
                                for k in range(CT):
                                    last = nc.tensor.matmul(data[:, t % 2 * C:(t % 2 + 1) * C], attT[:, k, t * P:(t + 1) * P], wo[:, k, :],
                                                            start=k == 0, stop=k == CT - 1)
                            last.then_inc(fl.filled("out", b), 1)

                def prepare():
                    pe.wait_ge(s["loaded"], LOADS)
                    core.met(pe, "pe")

                rounds(pe, front, heavy, prepare)


def program(nc, dram, out_dram):
    with ExitStack() as ctx:
        core = Core(nc, ctx)
        ff_signals = {n: ctx.enter_context(nc.semaphore("f_" + n)) for n in FF_SIGNALS}
        with ExitStack() as layer:
            la = AttentionA(nc, layer)
            landmarks(core, la, dram)
            layer_a(core, la, dram)
        with ExitStack() as layer:
            ff = FeedForward(nc, layer, 0)
            feed_forward(core, ff, ff_signals, dram)
        layer_b(core, dram)
        with ExitStack() as layer:
            ff = FeedForward(nc, layer, 1)
            feed_forward(core, ff, ff_signals, dram, out_dram)


def shape_constants():
    ident = np.eye(P, dtype=np.float32)
    shifted = np.zeros((P, BAND + TAPS - 1), np.float32)
    shifted[np.arange(P), np.arange(P) + TAPS - 1] = 1
    feature = np.arange(P) % DB
    frequency = np.float32(1) / np.float32(10000) ** (np.arange(0, DB, 2, dtype=np.float32) / np.float32(DB))
    angle = np.arange(T, dtype=np.float32)[None, :] * frequency[feature // 2][:, None]
    sign = np.where(feature % 2 == 0, np.float32(-1), np.float32(1))[:, None]
    select = np.zeros((P, 2, 2, PAIRS_T, P), np.float32)
    for side, parts in enumerate(((0, 1, 0, 1), (0, 0, 1, 1))):
        for j in range(PAIRS_T):
            for head in range(2):
                for copy, part in enumerate(parts):
                    for d in range(DB):
                        select[(2 * j + head) * DB + d, side, part, j, head * 64 + copy * DB + d] = DB ** -0.5 if side == 0 else 1
    return {
        "ident": ident,
        "i64": np.concatenate([np.eye(M, dtype=np.float32)] * 2),
        "shifted_ident": shifted,
        "cos": np.cos(angle).astype(np.float32),
        "sin": (np.sin(angle) * sign).astype(np.float32),
        "select": select.reshape(P, -1),
        "causal": np.where(np.arange(P)[None, :] > np.arange(P)[:, None], np.float32(-1e30), np.float32(0)),
    }


def kernel(**inputs):
    import concourse.bacc as bacc
    from concourse.bass_utils import run_bass_kernel_spmd

    a = {n[len("L0_attn_a_"):]: np.asarray(v) for n, v in inputs.items() if n.startswith("L0_attn_a_")}
    b = {n[len("L0_attn_b_"):]: np.asarray(v) for n, v in inputs.items() if n.startswith("L0_attn_b_")}
    f = {n[len("L0_ffn_"):]: np.asarray(v) for n, v in inputs.items() if n.startswith("L0_ffn_")}

    by_partition = lambda v: v.reshape(CT, P).T
    router = np.concatenate(
        [f["conf_rwkv"].T, f["conf_trans"][:, None], f["w_diff"][:, None], f["W_aff"], np.zeros((C, 1), np.float32)], axis=1)
    arrays = {
        "x": a["x"].reshape(B * T, C), "w_qkv": a["w_qkv"], "wqT": a["w_qkv"][:, :INNER].T, "wkT": a["w_qkv"][:, INNER:2 * INNER].T,
        "taps": a["w_conv"].reshape(HA * TAPS), "w_fc": a["w_fc"], "b_fc": a["b_fc"],
        "WqT": b["Wq"].T, "WkT": b["Wk"].T, "WvT": b["Wv"].T, "WoT": b["Wo"].T,
        "capital_shares": f["capital_shares"], "router": router, "WsT": f["Ws"].T,
        **{n: by_partition(f[n]) for n in ("ln1_w", "ln1_b", "ln2_w", "ln2_b")},
        **{n: f[n] for n in ("Wr", "Wv", "Wo", "W1", "W2", "W3", "K_rwkv", "V_rwkv")},
        **shape_constants(),
    }
    nc = bacc.Bacc("TRN2", target_bir_lowering=False, num_devices=1)
    staged, dram = {}, {}
    for name, array in arrays.items():
        staged[f"in_{name}_dram"] = np.ascontiguousarray(array)
        dram[name] = nc.dram_tensor(f"in_{name}_dram", array.shape, mybir.dt.from_np(array.dtype), kind="ExternalInput").ap()
    out = nc.dram_tensor("out_0_dram", (B * T, C), F32, kind="ExternalOutput").ap()
    program(nc, dram, out)
    result = run_bass_kernel_spmd(nc, [staged], core_ids=[0])
    return result.results[0]["out_0_dram"].reshape(B, T, C)
```
